# Optimizing a Trainium2 kernel written in Bass

```python
import numpy as np
import jax
import jax.numpy as jnp

def _softmax(x, axis=-1):
    return jax.nn.softmax(x, axis=axis)

def _gelu(x):
    return jax.nn.gelu(x, approximate=True)

def _silu(x):
    return jax.nn.silu(x)

def _sigmoid(x):
    return jax.nn.sigmoid(x)

def _layernorm(x, axis=-1, eps=1e-05):
    m = jnp.mean(x, axis=axis, keepdims=True)
    v = jnp.var(x, axis=axis, keepdims=True)
    return (x - m) / jnp.sqrt(v + eps)

def _scatter_add(tgt, idx, src, axis=0):
    return tgt.at[idx].add(src)

def _segment_sum(src, seg, n):
    return jax.ops.segment_sum(src, seg, n)
kernel_name = 'mk_cond_seq_d4_seqx_r8_fc4619'

def setup_inputs(seed: int=0):
    np.random.seed(seed)
    _w = jnp.asarray

    def _rec_inputs():
        import jax
        import jax.numpy as jnp
        _rk = jax.random.key(seed)
        x = -0.0002928 + 1 * jax.random.normal(jax.random.fold_in(_rk, 1), (32, 32, 128), jnp.float32)
        _lenS = 32 - jax.random.randint(jax.random.fold_in(_rk, 7), (32,), 0, max(1, 32 // 4) + 1, jnp.int32)
        _lenS2 = 32 - jax.random.randint(jax.random.fold_in(_rk, 8), (32,), 0, max(1, 32 // 4) + 1, jnp.int32)
        itok_B_0_7 = jax.random.randint(jax.random.fold_in(_rk, 11), (32,), 0, 8, jnp.int32)
        itok_B_6_14 = jax.random.randint(jax.random.fold_in(_rk, 12), (32,), 6, 15, jnp.int32)
        itok_B_0_15 = jax.random.randint(jax.random.fold_in(_rk, 13), (32,), 0, 16, jnp.int32)
        itok_B_0_2 = jax.random.randint(jax.random.fold_in(_rk, 14), (32,), 0, 3, jnp.int32)
        return (x, itok_B_0_7, itok_B_6_14, itok_B_0_15, itok_B_0_2)
    x, itok_B_0_7, itok_B_6_14, itok_B_0_15, itok_B_0_2 = _rec_inputs()

    def _L0_cond_setup():
        import jax, jax.numpy as jnp
        import numpy as np
        E, H, I = (8, 128, 512)
        B, S = (4, 128)
        LN_EPS = 1e-12
        key = jax.random.key(seed)
        ks = jax.random.split(key, 8)
        x = jax.random.normal(ks[0], (B, S, H), dtype=jnp.float32)
        expert_idx = jax.random.randint(ks[1], (B,), 0, E, dtype=jnp.int64)
        Wi = jax.random.normal(ks[2], (E, H, I), dtype=jnp.float32) * 0.02
        bi = jnp.zeros((E, I), dtype=jnp.float32)
        Wo = jax.random.normal(ks[3], (E, I, H), dtype=jnp.float32) * 0.02
        bo = jnp.zeros((E, H), dtype=jnp.float32)
        gamma = jnp.ones((E, H), dtype=jnp.float32)
        beta = jnp.zeros((E, H), dtype=jnp.float32)
        return {'input_tensor': x, 'expert_idx': expert_idx, 'Wi': Wi, 'bi': bi, 'Wo': Wo, 'bo': bo, 'gamma': gamma, 'beta': beta}
    _L0_cond_all = _L0_cond_setup()
    _L0_cond_in = {k: v for k, v in _L0_cond_all.items() if k in ('Wi', 'bi', 'Wo', 'bo', 'gamma', 'beta')}
    del _L0_cond_all

    def _L1_cond_setup():
        import jax, jax.numpy as jnp
        import numpy as np
        D = 128
        E = 8
        FF = 512
        TOPK = 2
        S = 32
        SE = 64
        SH = 128
        B, T = (2, 256)

        def _forward(x, subject_ids, ln_g, ln_b, subj_emb, hyp_w1, hyp_b1, hyp_w2, hyp_b2, sty_w1, sty_b1, sty_w2, sty_b2, router_w, exp_w1, exp_b1, exp_w2, exp_b2):
            mu = x.mean(-1, keepdims=True)
            var = x.var(-1, keepdims=True)
            h = (x - mu) * jax.lax.rsqrt(var + 1e-05) * ln_g + ln_b
            m_t = h.mean(1, keepdims=True)
            v_t = h.var(1, keepdims=True)
            h_norm = (h - m_t) * jax.lax.rsqrt(v_t + 1e-08)
            se = subj_emb[subject_ids]
            hyp = jax.nn.relu(se @ hyp_w1 + hyp_b1) @ hyp_w2 + hyp_b2
            sty = jax.nn.relu(hyp @ sty_w1 + sty_b1) @ sty_w2 + sty_b2
            gamma, beta = jnp.split(sty, 2, axis=-1)
            gamma = jax.nn.softplus(gamma) + 1e-08
            h = h_norm * gamma[:, None, :] + beta[:, None, :]
            h_flat = h.reshape(-1, D)
            probs = jax.nn.softmax(h_flat @ router_w, axis=-1)
            gates, idx = jax.lax.top_k(probs, TOPK)
            gates = gates / gates.sum(-1, keepdims=True)
            N = h_flat.shape[0]
            combine = jnp.zeros((N, E), h_flat.dtype).at[jnp.arange(N)[:, None], idx].add(gates)
            hid = jax.nn.relu(jnp.einsum('nd,edf->nef', h_flat, exp_w1) + exp_b1)
            eout = jnp.einsum('nef,efd->ned', hid, exp_w2) + exp_b2
            y = jnp.einsum('ned,ne->nd', eout, combine)
            return x + y.reshape(x.shape)
        key = jax.random.key(seed)
        ks = jax.random.split(key, 16)
        n = lambda k, sh, s=0.02: jax.random.normal(k, sh, dtype=jnp.float32) * s
        return {'x': jax.random.normal(ks[0], (B, T, D), dtype=jnp.float32), 'subject_ids': jax.random.randint(ks[1], (B,), 0, S), 'ln_g': jnp.ones((D,), jnp.float32), 'ln_b': jnp.zeros((D,), jnp.float32), 'subj_emb': n(ks[2], (S, SE)), 'hyp_w1': n(ks[3], (SE, SH), 1.0 / np.sqrt(SE)), 'hyp_b1': jnp.zeros((SH,), jnp.float32), 'hyp_w2': n(ks[4], (SH, SH), 1.0 / np.sqrt(SH)), 'hyp_b2': jnp.zeros((SH,), jnp.float32), 'sty_w1': n(ks[5], (SH, SH // 2), 1.0 / np.sqrt(SH)), 'sty_b1': jnp.zeros((SH // 2,), jnp.float32), 'sty_w2': n(ks[6], (SH // 2, 2 * D), 1.0 / np.sqrt(SH // 2)), 'sty_b2': jnp.zeros((2 * D,), jnp.float32), 'router_w': n(ks[7], (D, E), 1.0 / np.sqrt(D)), 'exp_w1': n(ks[8], (E, D, FF), 1.0 / np.sqrt(D)), 'exp_b1': jnp.zeros((E, FF), jnp.float32), 'exp_w2': n(ks[9], (E, FF, D), 1.0 / np.sqrt(FF)), 'exp_b2': jnp.zeros((E, D), jnp.float32)}
    _L1_cond_all = _L1_cond_setup()
    _L1_cond_in = {k: v for k, v in _L1_cond_all.items() if k in ('ln_g', 'ln_b', 'subj_emb', 'hyp_w1', 'hyp_b1', 'hyp_w2', 'hyp_b2', 'sty_w1', 'sty_b1', 'sty_w2', 'sty_b2', 'router_w', 'exp_w1', 'exp_b1', 'exp_w2', 'exp_b2')}
    del _L1_cond_all

    def _L2_cond_setup():
        import jax, jax.numpy as jnp
        import numpy as np
        B, S, D = (32, 128, 128)
        A = 32
        E = 16
        LN_EPS = 1e-05
        key = jax.random.key(seed)
        ks = jax.random.split(key, 10)
        s = lambda fan_in: 1.0 / np.sqrt(fan_in)
        return {'hidden_states': jax.random.normal(ks[0], (B, S, D), dtype=jnp.float32), 'domain_id': jax.random.randint(ks[1], (B,), 0, E, dtype=jnp.int64), 'down_W': jax.random.uniform(ks[2], (A, D), jnp.float32, -s(D), s(D)), 'down_b': jax.random.uniform(ks[3], (A,), jnp.float32, -s(D), s(D)), 'up_W': jax.random.uniform(ks[4], (D, A), jnp.float32, -s(A), s(A)), 'up_b': jax.random.uniform(ks[5], (D,), jnp.float32, -s(A), s(A)), 'expert_W': jax.random.uniform(ks[6], (E, A, A), jnp.float32, -s(A), s(A)), 'expert_b': jax.random.uniform(ks[7], (E, A), jnp.float32, -s(A), s(A)), 'domain_emb': jax.random.normal(ks[8], (E, A), dtype=jnp.float32), 'ln_gamma': jnp.ones((D,), jnp.float32), 'ln_beta': jnp.zeros((D,), jnp.float32)}
    _L2_cond_all = _L2_cond_setup()
    _L2_cond_in = {k: v for k, v in _L2_cond_all.items() if k in ('down_W', 'down_b', 'up_W', 'up_b', 'expert_W', 'expert_b', 'domain_emb', 'ln_gamma', 'ln_beta')}
    del _L2_cond_all

    def _L3_cond_setup():
        import jax, jax.numpy as jnp
        import numpy as np
        H = 128
        EPS = 1e-05

        def _gelu(x):
            return jax.nn.gelu(x, approximate=False)
        key = jax.random.key(seed)
        ks = jax.random.split(key, 16)
        s = 1.0 / np.sqrt(H)
        inp = {'x': jax.random.normal(ks[0], (64, 128, H), dtype=jnp.float32), 'condition': jax.random.randint(ks[1], (64,), 0, 3), 'w1_nr': jax.random.normal(ks[2], (H, H), dtype=jnp.float32) * s, 'b1_nr': jnp.zeros((H,), dtype=jnp.float32), 'w2_nr': jax.random.normal(ks[3], (H, H), dtype=jnp.float32) * s, 'b2_nr': jnp.zeros((H,), dtype=jnp.float32), 'w1_tsr': jax.random.normal(ks[4], (H, H), dtype=jnp.float32) * s, 'b1_tsr': jnp.zeros((H,), dtype=jnp.float32), 'w2_tsr': jax.random.normal(ks[5], (H, H), dtype=jnp.float32) * s, 'b2_tsr': jnp.zeros((H,), dtype=jnp.float32), 'w1_sr': jax.random.normal(ks[6], (H, 2 * H), dtype=jnp.float32) * s, 'b1_sr': jnp.zeros((2 * H,), dtype=jnp.float32), 'w2_sr': jax.random.normal(ks[7], (2 * H, H), dtype=jnp.float32) * (1.0 / np.sqrt(2 * H)), 'b2_sr': jnp.zeros((H,), dtype=jnp.float32), 'w3_sr': jax.random.normal(ks[8], (H, H), dtype=jnp.float32) * s, 'b3_sr': jnp.zeros((H,), dtype=jnp.float32), 'gamma': jnp.ones((H,), dtype=jnp.float32), 'beta': jnp.zeros((H,), dtype=jnp.float32)}
        return inp
    _L3_cond_all = _L3_cond_setup()
    _L3_cond_in = {k: v for k, v in _L3_cond_all.items() if k in ('w1_nr', 'b1_nr', 'w2_nr', 'b2_nr', 'w1_tsr', 'b1_tsr', 'w2_tsr', 'b2_tsr', 'w1_sr', 'b1_sr', 'w2_sr', 'b2_sr', 'w3_sr', 'b3_sr', 'gamma', 'beta')}
    del _L3_cond_all
    return {'x': x, 'itok_B_0_7': itok_B_0_7, 'itok_B_6_14': itok_B_6_14, 'itok_B_0_15': itok_B_0_15, 'itok_B_0_2': itok_B_0_2, 'L0_cond_Wi': _L0_cond_in['Wi'], 'L0_cond_bi': _L0_cond_in['bi'], 'L0_cond_Wo': _L0_cond_in['Wo'], 'L0_cond_bo': _L0_cond_in['bo'], 'L0_cond_gamma': _L0_cond_in['gamma'], 'L0_cond_beta': _L0_cond_in['beta'], 'L1_cond_ln_g': _L1_cond_in['ln_g'], 'L1_cond_ln_b': _L1_cond_in['ln_b'], 'L1_cond_subj_emb': _L1_cond_in['subj_emb'], 'L1_cond_hyp_w1': _L1_cond_in['hyp_w1'], 'L1_cond_hyp_b1': _L1_cond_in['hyp_b1'], 'L1_cond_hyp_w2': _L1_cond_in['hyp_w2'], 'L1_cond_hyp_b2': _L1_cond_in['hyp_b2'], 'L1_cond_sty_w1': _L1_cond_in['sty_w1'], 'L1_cond_sty_b1': _L1_cond_in['sty_b1'], 'L1_cond_sty_w2': _L1_cond_in['sty_w2'], 'L1_cond_sty_b2': _L1_cond_in['sty_b2'], 'L1_cond_router_w': _L1_cond_in['router_w'], 'L1_cond_exp_w1': _L1_cond_in['exp_w1'], 'L1_cond_exp_b1': _L1_cond_in['exp_b1'], 'L1_cond_exp_w2': _L1_cond_in['exp_w2'], 'L1_cond_exp_b2': _L1_cond_in['exp_b2'], 'L2_cond_down_W': _L2_cond_in['down_W'], 'L2_cond_down_b': _L2_cond_in['down_b'], 'L2_cond_up_W': _L2_cond_in['up_W'], 'L2_cond_up_b': _L2_cond_in['up_b'], 'L2_cond_expert_W': _L2_cond_in['expert_W'], 'L2_cond_expert_b': _L2_cond_in['expert_b'], 'L2_cond_domain_emb': _L2_cond_in['domain_emb'], 'L2_cond_ln_gamma': _L2_cond_in['ln_gamma'], 'L2_cond_ln_beta': _L2_cond_in['ln_beta'], 'L3_cond_w1_nr': _L3_cond_in['w1_nr'], 'L3_cond_b1_nr': _L3_cond_in['b1_nr'], 'L3_cond_w2_nr': _L3_cond_in['w2_nr'], 'L3_cond_b2_nr': _L3_cond_in['b2_nr'], 'L3_cond_w1_tsr': _L3_cond_in['w1_tsr'], 'L3_cond_b1_tsr': _L3_cond_in['b1_tsr'], 'L3_cond_w2_tsr': _L3_cond_in['w2_tsr'], 'L3_cond_b2_tsr': _L3_cond_in['b2_tsr'], 'L3_cond_w1_sr': _L3_cond_in['w1_sr'], 'L3_cond_b1_sr': _L3_cond_in['b1_sr'], 'L3_cond_w2_sr': _L3_cond_in['w2_sr'], 'L3_cond_b2_sr': _L3_cond_in['b2_sr'], 'L3_cond_w3_sr': _L3_cond_in['w3_sr'], 'L3_cond_b3_sr': _L3_cond_in['b3_sr'], 'L3_cond_gamma': _L3_cond_in['gamma'], 'L3_cond_beta': _L3_cond_in['beta']}

def reference(x, itok_B_0_7, itok_B_6_14, itok_B_0_15, itok_B_0_2, L0_cond_Wi, L0_cond_bi, L0_cond_Wo, L0_cond_bo, L0_cond_gamma, L0_cond_beta, L1_cond_ln_g, L1_cond_ln_b, L1_cond_subj_emb, L1_cond_hyp_w1, L1_cond_hyp_b1, L1_cond_hyp_w2, L1_cond_hyp_b2, L1_cond_sty_w1, L1_cond_sty_b1, L1_cond_sty_w2, L1_cond_sty_b2, L1_cond_router_w, L1_cond_exp_w1, L1_cond_exp_b1, L1_cond_exp_w2, L1_cond_exp_b2, L2_cond_down_W, L2_cond_down_b, L2_cond_up_W, L2_cond_up_b, L2_cond_expert_W, L2_cond_expert_b, L2_cond_domain_emb, L2_cond_ln_gamma, L2_cond_ln_beta, L3_cond_w1_nr, L3_cond_b1_nr, L3_cond_w2_nr, L3_cond_b2_nr, L3_cond_w1_tsr, L3_cond_b1_tsr, L3_cond_w2_tsr, L3_cond_b2_tsr, L3_cond_w1_sr, L3_cond_b1_sr, L3_cond_w2_sr, L3_cond_b2_sr, L3_cond_w3_sr, L3_cond_b3_sr, L3_cond_gamma, L3_cond_beta):
    import jax
    import jax.numpy as jnp

    def _L0_cond_ref(input_tensor, expert_idx, Wi, bi, Wo, bo, gamma, beta):
        import jax, jax.numpy as jnp
        import numpy as np
        E, H, I = (8, 128, 512)
        B, S = (4, 128)
        LN_EPS = 1e-12
        Wi_b = Wi[expert_idx]
        bi_b = bi[expert_idx]
        Wo_b = Wo[expert_idx]
        bo_b = bo[expert_idx]
        g_b = gamma[expert_idx]
        be_b = beta[expert_idx]
        h = jax.nn.gelu(jnp.einsum('bsh,bhi->bsi', input_tensor, Wi_b) + bi_b[:, None, :], approximate=False)
        o = jnp.einsum('bsi,bih->bsh', h, Wo_b) + bo_b[:, None, :]
        r = o + input_tensor
        mu = jnp.mean(r, axis=-1, keepdims=True)
        var = jnp.mean(jnp.square(r - mu), axis=-1, keepdims=True)
        y = (r - mu) * jax.lax.rsqrt(var + LN_EPS)
        return y * g_b[:, None, :] + be_b[:, None, :]

    def _L1_cond_ref(x, subject_ids, ln_g, ln_b, subj_emb, hyp_w1, hyp_b1, hyp_w2, hyp_b2, sty_w1, sty_b1, sty_w2, sty_b2, router_w, exp_w1, exp_b1, exp_w2, exp_b2):
        import jax, jax.numpy as jnp
        import numpy as np
        D = 128
        E = 8
        FF = 512
        TOPK = 2
        S = 32
        SE = 64
        SH = 128
        B, T = (2, 256)

        def _forward(x, subject_ids, ln_g, ln_b, subj_emb, hyp_w1, hyp_b1, hyp_w2, hyp_b2, sty_w1, sty_b1, sty_w2, sty_b2, router_w, exp_w1, exp_b1, exp_w2, exp_b2):
            mu = x.mean(-1, keepdims=True)
            var = x.var(-1, keepdims=True)
            h = (x - mu) * jax.lax.rsqrt(var + 1e-05) * ln_g + ln_b
            m_t = h.mean(1, keepdims=True)
            v_t = h.var(1, keepdims=True)
            h_norm = (h - m_t) * jax.lax.rsqrt(v_t + 1e-08)
            se = subj_emb[subject_ids]
            hyp = jax.nn.relu(se @ hyp_w1 + hyp_b1) @ hyp_w2 + hyp_b2
            sty = jax.nn.relu(hyp @ sty_w1 + sty_b1) @ sty_w2 + sty_b2
            gamma, beta = jnp.split(sty, 2, axis=-1)
            gamma = jax.nn.softplus(gamma) + 1e-08
            h = h_norm * gamma[:, None, :] + beta[:, None, :]
            h_flat = h.reshape(-1, D)
            probs = jax.nn.softmax(h_flat @ router_w, axis=-1)
            gates, idx = jax.lax.top_k(probs, TOPK)
            gates = gates / gates.sum(-1, keepdims=True)
            N = h_flat.shape[0]
            combine = jnp.zeros((N, E), h_flat.dtype).at[jnp.arange(N)[:, None], idx].add(gates)
            hid = jax.nn.relu(jnp.einsum('nd,edf->nef', h_flat, exp_w1) + exp_b1)
            eout = jnp.einsum('nef,efd->ned', hid, exp_w2) + exp_b2
            y = jnp.einsum('ned,ne->nd', eout, combine)
            return x + y.reshape(x.shape)
        return _forward(x, subject_ids, ln_g, ln_b, subj_emb, hyp_w1, hyp_b1, hyp_w2, hyp_b2, sty_w1, sty_b1, sty_w2, sty_b2, router_w, exp_w1, exp_b1, exp_w2, exp_b2)

    def _L2_cond_ref(hidden_states, domain_id, down_W, down_b, up_W, up_b, expert_W, expert_b, domain_emb, ln_gamma, ln_beta):
        import jax, jax.numpy as jnp
        import numpy as np
        B, S, D = (32, 128, 128)
        A = 32
        E = 16
        LN_EPS = 1e-05
        residual = hidden_states
        hidden = jnp.einsum('bsd,ad->bsa', hidden_states, down_W) + down_b
        hidden = jax.nn.gelu(hidden, approximate=False)
        valid = (domain_id >= 0) & (domain_id < E)
        idx = jnp.clip(domain_id, 0, E - 1)
        Wsel = expert_W[idx]
        bsel = expert_b[idx]
        expert_out = jnp.einsum('bsa,boa->bso', hidden, Wsel) + bsel[:, None, :]
        domain_output = jnp.where(valid[:, None, None], expert_out, hidden)
        hidden = domain_output + domain_emb[idx][:, None, :]
        hidden = jnp.einsum('bsa,da->bsd', hidden, up_W) + up_b
        x = hidden + residual
        mu = jnp.mean(x, axis=-1, keepdims=True)
        var = jnp.mean(jnp.square(x - mu), axis=-1, keepdims=True)
        return (x - mu) * jax.lax.rsqrt(var + LN_EPS) * ln_gamma + ln_beta

    def _L3_cond_ref(x, condition, w1_nr, b1_nr, w2_nr, b2_nr, w1_tsr, b1_tsr, w2_tsr, b2_tsr, w1_sr, b1_sr, w2_sr, b2_sr, w3_sr, b3_sr, gamma, beta):
        import jax, jax.numpy as jnp
        import numpy as np
        H = 128
        EPS = 1e-05

        def _gelu(x):
            return jax.nn.gelu(x, approximate=False)
        out_nr = _gelu(jnp.einsum('bth,hk->btk', x, w1_nr) + b1_nr)
        out_nr = jnp.einsum('bth,hk->btk', out_nr, w2_nr) + b2_nr
        out_tsr = _gelu(jnp.einsum('bth,hk->btk', x, w1_tsr) + b1_tsr)
        out_tsr = jnp.einsum('bth,hk->btk', out_tsr, w2_tsr) + b2_tsr
        h = _gelu(jnp.einsum('bth,hk->btk', x, w1_sr) + b1_sr)
        h = _gelu(jnp.einsum('bth,hk->btk', h, w2_sr) + b2_sr)
        out_sr = jnp.einsum('bth,hk->btk', h, w3_sr) + b3_sr
        c = condition[:, None, None]
        out = jnp.where(c == 0, out_nr, jnp.where(c == 1, out_tsr, jnp.where(c == 2, out_sr, jnp.zeros_like(x))))
        y = x + out
        mu = jnp.mean(y, axis=-1, keepdims=True)
        var = jnp.mean((y - mu) ** 2, axis=-1, keepdims=True)
        return (y - mu) * jax.lax.rsqrt(var + EPS) * gamma + beta
    x = _L0_cond_ref(x, itok_B_0_7, L0_cond_Wi, L0_cond_bi, L0_cond_Wo, L0_cond_bo, L0_cond_gamma, L0_cond_beta)
    x = _L1_cond_ref(x, itok_B_6_14, L1_cond_ln_g, L1_cond_ln_b, L1_cond_subj_emb, L1_cond_hyp_w1, L1_cond_hyp_b1, L1_cond_hyp_w2, L1_cond_hyp_b2, L1_cond_sty_w1, L1_cond_sty_b1, L1_cond_sty_w2, L1_cond_sty_b2, L1_cond_router_w, L1_cond_exp_w1, L1_cond_exp_b1, L1_cond_exp_w2, L1_cond_exp_b2)
    x = _L2_cond_ref(x, itok_B_0_15, L2_cond_down_W, L2_cond_down_b, L2_cond_up_W, L2_cond_up_b, L2_cond_expert_W, L2_cond_expert_b, L2_cond_domain_emb, L2_cond_ln_gamma, L2_cond_ln_beta)
    x = _L3_cond_ref(x, itok_B_0_2, L3_cond_w1_nr, L3_cond_b1_nr, L3_cond_w2_nr, L3_cond_b2_nr, L3_cond_w1_tsr, L3_cond_b1_tsr, L3_cond_w2_tsr, L3_cond_b2_tsr, L3_cond_w1_sr, L3_cond_b1_sr, L3_cond_w2_sr, L3_cond_b2_sr, L3_cond_w3_sr, L3_cond_b3_sr, L3_cond_gamma, L3_cond_beta)
    return x

_drawn_inputs = setup_inputs


def setup_inputs(seed=0):
    import zlib

    import numpy as np

    out = dict(_drawn_inputs(seed))
    spreads = {'L0_cond_bi': (0.0, 0.1),
     'L0_cond_bo': (0.0, 0.1),
     'L0_cond_gamma': (1.0, 0.2),
     'L0_cond_beta': (0.0, 0.1),
     'L1_cond_ln_g': (1.0, 0.6),
     'L1_cond_ln_b': (0.0, 0.8),
     'L1_cond_hyp_b1': (0.0, 0.1),
     'L1_cond_hyp_b2': (0.0, 0.1),
     'L1_cond_sty_b1': (0.0, 0.1),
     'L1_cond_sty_b2': (0.0, 0.1),
     'L1_cond_exp_b1': (0.0, 0.1),
     'L1_cond_exp_b2': (0.0, 0.1),
     'L2_cond_ln_gamma': (1.0, 0.2),
     'L2_cond_ln_beta': (0.0, 0.1),
     'L3_cond_b1_nr': (0.0, 0.273),
     'L3_cond_b2_nr': (0.0, 0.1),
     'L3_cond_b1_tsr': (0.0, 0.1),
     'L3_cond_b2_tsr': (0.0, 0.1),
     'L3_cond_b1_sr': (0.0, 0.385),
     'L3_cond_b2_sr': (0.0, 0.1),
     'L3_cond_b3_sr': (0.0, 0.1),
     'L3_cond_gamma': (1.0, 0.2),
     'L3_cond_beta': (0.0, 0.1)}
    factors = {'L2_cond_down_b': 6.278}
    for name, (base, spread) in spreads.items():
        noise = np.random.default_rng([zlib.crc32(name.encode()), seed]).standard_normal(out[name].shape)
        drawn = base * np.exp(spread * noise) if base else spread * noise
        out[name] = jnp.asarray(drawn.astype(out[name].dtype))
    for name, factor in factors.items():
        out[name] = (out[name] * factor).astype(out[name].dtype)
    return out
```

```python
import concourse.bass as bass
from concourse import mybir
from contextlib import ExitStack

F32 = mybir.dt.float32
F32R = mybir.dt.float32r
BF16 = mybir.dt.bfloat16
I32 = mybir.dt.int32
U32 = mybir.dt.uint32
ALU = mybir.AluOpType
ACT = mybir.ActivationFunctionType
AX = mybir.AxisListType

P = 128
D = 128
B, S = 32, 32
NTOK = B * S
GRP = P // S
NG = NTOK // P
NH = 2
GH = NG // NH
BH = B // NH
T = NTOK // NH
FF = 512
NF = FF // P
E0, E1, NSUBJ = 8, 8, 32
A2 = 32
NCOND = 3
NBLK = 18
NE = NH * E1
NU = 3
NR = 3
RAW = 2
HALF_EXP = -0.5
EULER = 2.718281828459045

C_LNG, C_LNB, C_HB1, C_HB2, C_SB1, C_SB2G, C_SB2B = range(7)
C_B1NR, C_B1TSR, C_B1SR0, C_B1SR1, C_B2SR, C_DB, C_P32 = range(7, 14)
C_EB1 = 14
NCOL = C_EB1 + E1 * NF

MATS = {}
NMAT = 0
for _name, _w in (("hyp_w1", 128), ("hyp_w2", 128), ("sty_w1", 64), ("sty_w2", 256), ("subj", 64),
                  ("router", 8), ("ident", 128), ("downT", 128), ("upT", 128), ("exp_b2", 128),
                  ("w1_nr", 128), ("w1_tsr", 128), ("w1_sr", 256), ("w2_sr0", 128), ("w2_sr1", 128),
                  ("w2_nr", 128), ("w2_tsr", 128), ("w3_sr", 128)):
    MATS[_name] = (NMAT, NMAT + _w)
    NMAT += _w
MAT_EARLY = MATS["w1_nr"][0]

R_BI, R_BO, R_GAM, R_BET, R_B3 = 0, 512, 640, 768, 896
NROW = 1024


def build_program(nc, in_x_nat, in_x_t, in_ids_row, in_ids_all, in_ids_j, in_cols, in_mats, in_rows,
                  in_bcast, in_l2tab, in_wi, in_wo, in_w1, in_w2, out):
    ctx = ExitStack()
    with ctx:
        def sb(name, shape, dt=F32):
            return ctx.enter_context(nc.sbuf_tensor(name, shape, dt))

        def sem(name):
            return ctx.enter_context(nc.semaphore(name))

        x_nat = sb("x_nat", [P, NG, D])
        x_t = sb("x_t", [P, NTOK])
        ids_row = sb("ids_row", [1, B], I32)
        ids_all = sb("ids_all", [P, 4, B], I32)
        ids_f = sb("ids_f", [P, 4, B])
        ids_j = sb("ids_j", [P, NG], I32)
        cols = sb("cols", [P, NCOL])
        mats = sb("mats", [P, MAT_EARLY])
        rows3 = sb("rows3", [96, NROW], BF16)
        wi_all = sb("wi_all", [P, E0, FF])
        wo_all = sb("wo_all", [P, E0, FF])
        w1_raw = sb("w1_raw", [P, RAW, FF])
        w2_raw = sb("w2_raw", [P, RAW, FF])
        w1_hi = sb("w1_hi", [P, E1, FF], F32R)
        w1_lo = sb("w1_lo", [P, E1, FF], F32R)
        w2_hi = sb("w2_hi", [P, E1, FF], F32R)
        w2_lo = sb("w2_lo", [P, E1, FF], F32R)
        oh0 = sb("oh0", [96, NTOK], BF16)
        ohc = sb("ohc", [96, NTOK], BF16)
        ohs = sb("ohs", [NSUBJ, B])
        cmask = sb("cmask", [P, NCOND, B])
        half_exp = sb("half_exp", [P, 16])
        euler = sb("euler", [P, GH])
        iota8 = sb("iota8", [P, E1], I32)
        se_t = sb("se_t", [64, B])
        hy1 = sb("hy1", [P, B])
        hy2 = sb("hy2", [P, B])
        st1 = sb("st1", [64, B])
        gam_raw = sb("gam_raw", [P, B])
        gam_abs = sb("gam_abs", [P, B])
        gam_exp = sb("gam_exp", [P, B])
        gam_log = sb("gam_log", [P, B])
        gam_s = sb("gam_s", [P, B])
        bet_s = sb("bet_s", [P, B])
        wi_sel0 = sb("wi_sel0", [P, GRP, FF])
        wo_sel0 = sb("wo_sel0", [P, GRP, FF])
        with nc.sbuf_tensor("wi_sel1", [P, GRP, FF], F32) as wi_sel1, \
                nc.sbuf_tensor("wo_sel1", [P, GRP, FF], F32) as wo_sel1:
            pass
        hid_hi1 = sb("hid_hi1", [P, NF, T], F32R)
        hid_lo1 = sb("hid_lo1", [P, NF, T], F32R)
        hid_hi = [sb("hid_hi0", [P, NF, T], F32R), hid_hi1]
        hid_lo = [sb("hid_lo0", [P, NF, T], F32R), hid_lo1]

        def wi_sel(g):
            return wi_sel1 if g < GH and g % 2 else wi_sel0

        def wo_sel(g):
            return wo_sel1 if g < GH and g % 2 else wo_sel0

        h0 = sb("h0", [P, 2, FF])
        h0t = sb("h0t", [P, 2, FF])
        rows_f = h0[:, :, :].rearrange("p a n -> p (a n)")
        res0 = sb("res0", [P, 2, D])
        y0 = sb("y0", [P, 2, D])
        stat0 = sb("stat0", [P, 2, 6])
        mv0 = sb("mv0", [P, 2, 2])
        rs0 = sb("rs0", [P, 2, 2])
        x1 = acc = x_nat
        stat1 = sb("stat1", [P, 2, 6])
        mv1 = sb("mv1", [P, 2, 2])
        rs1 = sb("rs1", [P, 2, 2])
        z1 = sb("z1", [P, GH, D])
        hn = sb("hn", [P, T])
        cen = h2 = hn
        tsum = sb("tsum", [P, BH])
        tmean = sb("tmean", [P, BH])
        sq = z1[:, :, :].rearrange("p g d -> p (g d)")
        tvar = sb("tvar", [P, BH])
        trs = sb("trs", [P, 2, BH])
        tscale = sb("tscale", [P, BH])
        h2_hi = sb("h2_hi", [P, NH, T], F32R)
        h2_lo = sb("h2_lo", [P, NH, T], F32R)
        logit = sb("logit", [P, GH, E1])
        top = sb("top", [P, GH, 8])
        topi = sb("topi", [P, GH, 8], U32)
        topf = sb("topf", [P, GH, 8])
        dif = sb("dif", [P, GH])
        ratio = sb("ratio", [P, GH])
        wtop = sb("wtop", [P, 3, GH])
        eq1 = sb("eq1", [P, GH, E1])
        eq2 = sb("eq2", [P, GH, E1])
        comb = sb("comb", [P, NH, GH, E1])
        comb_t = sb("comb_t", [E1, T])
        r1 = sb("r1", [P, NR, T])
        l2g = sb("l2g", [P, NG, A2 + 2])
        l2i_f = sb("l2i_f", [P, NG])
        l2i = sb("l2i", [P, NG], I32)
        l2b = sb("l2b", [P, NG])
        old = wi_all[:, :, :].rearrange("p e n -> p (e n)")
        old2 = wo_all[:, :, :].rearrange("p e n -> p (e n)")

        def groups(ap):
            return ap.rearrange("p (g d) -> p g d", d=D)

        bd_h = groups(old[:, 0:2 * T])
        tt = old[:, 2 * T:3 * T]
        hb = sb("hb", [P, P])
        accb = groups(old[:, 3 * T:4 * T])
        pre = groups(old[:, 4 * T:5 * T])
        stat2 = sb("stat2", [P, GH, 6])
        mv2 = sb("mv2", [P, GH, 2])
        rs2 = sb("rs2", [P, 2, GH])
        zz = groups(old[:, 5 * T:6 * T])
        x3 = groups(old[:, 6 * T:8 * T])
        bd_w = groups(wi_sel0[:, 0:2, :].rearrange("p j n -> p (j n)"))
        mats_l3 = wo_sel0[:, 0:3, :].rearrange("p j n -> p (j n)")[:, 0:NMAT - MAT_EARLY]
        bcast = wi_sel0[:, 2:4, :].rearrange("p j n -> p (j n)")[:, 0:5 * D].rearrange("p (k d) -> p k d", k=5)
        a_l3 = old2[:, 0:4 * T].rearrange("p (k t) -> p k t", k=4)
        a_sr2 = old2[:, 4 * T:5 * T]
        yout = groups(old2[:, 5 * T:7 * T])

        ps = ctx.enter_context(nc.psum_tensor("ps", [P, 8, 512], F32))

        def bank_up(g):
            return ps[:, 3 * (g % 2) if g < GH else 0, :]

        def bank_tr(g):
            return ps[:, 1 + 3 * (g % 2) if g < GH else 1, :]

        def bank_sm(g):
            return ps[:, 2 + 3 * (g % 2) if g < GH else 2, :]

        B0, B1, B2 = ps[:, 0, :], ps[:, 1, :], ps[:, 2, :]

        def bank_u(n):
            return ps[:, 3 + n % NU, :]

        def bank_d(n):
            return ps[:, 6 + n % 2, :]

        def mat(name, rows=P):
            a, b = MATS[name]
            if a >= MAT_EARLY:
                return mats_l3[0:rows, a - MAT_EARLY:b - MAT_EARLY]
            return mats[0:rows, a:b]

        def col(c, rows=P):
            return cols[0:rows, c:c + 1]

        ld_idrow = sem("ld_idrow")
        ld_ids = sem("ld_ids")
        ld_small = sem("ld_small")
        ld_rows = sem("ld_rows")
        ld_xt = sem("ld_xt")
        ld_xn = sem("ld_xn")
        ld_wi = sem("ld_wi")
        ld_wo = sem("ld_wo")
        ld_late = sem("ld_late")
        ld_w = [sem(f"ld_w{i}") for i in range(RAW)]
        ld_l2 = sem("ld_l2")
        st_out = sem("st_out")
        k_rows0 = sem("k_rows0")
        k_oh = sem("k_oh")
        k_const = sem("k_const")
        k_bd0 = sem("k_bd0")
        k_bd = sem("k_bd")
        sty_mm = sem("sty_mm")
        sty_ev = sem("sty_ev")
        sty_done = sem("sty_done")
        wi_picked = sem("wi_picked")
        wo_picked = sem("wo_picked")
        up0_done = sem("up0_done")
        gelu0_done = sem("gelu0_done")
        tr0_done = sem("tr0_done")
        h0t_done = sem("h0t_done")
        dn0_done = sem("dn0_done")
        var0_ready = sem("var0_ready")
        rs0_ready = sem("rs0_ready")
        x1_ready = sem("x1_ready")
        var1_ready = sem("var1_ready")
        rs1_ready = sem("rs1_ready")
        z1_ready = sem("z1_ready")
        zt_done = sem("zt_done")
        hn_ready = sem("hn_ready")
        cen_ready = sem("cen_ready")
        sq_ready = sem("sq_ready")
        tvar_ready = sem("tvar_ready")
        trs_ready = sem("trs_ready")
        h2_ready = sem("h2_ready")
        h2s_ready = sem("h2s_ready")
        route_mm = sem("route_mm")
        dif_ready = sem("dif_ready")
        ratio_ready = sem("ratio_ready")
        comb_ready = sem("comb_ready")
        combt_mm = sem("combt_mm")
        combt_ready = sem("combt_ready")
        b2_mm = sem("b2_mm")
        acc_ready = sem("acc_ready")
        w_hi = sem("w_hi")
        w_lo = sem("w_lo")
        up1_done = sem("up1_done")
        relu_done = sem("relu_done")
        hi_done = sem("hi_done")
        lo_dve = sem("lo_dve")
        lo_pool = sem("lo_pool")
        dn1_done = sem("dn1_done")
        gate_done = sem("gate_done")
        x2t_mm = sem("x2t_mm")
        x2t_ready = sem("x2t_ready")
        accb_ready = sem("accb_ready")
        dproj_mm = sem("dproj_mm")
        hb_ready = sem("hb_ready")
        exp_mm = sem("exp_mm")
        bdh_ready = sem("bdh_ready")
        up2_mm = sem("up2_mm")
        var2_ready = sem("var2_ready")
        rs2_ready = sem("rs2_ready")
        x3_ready = sem("x3_ready")
        x3t_mm = sem("x3t_mm")
        x3t_ready = sem("x3t_ready")
        l3a_mm = sem("l3a_mm")
        l3a_act = sem("l3a_act")
        l3a_mask = sem("l3a_mask")
        l3b_mm = sem("l3b_mm")
        l3b_act = sem("l3b_act")
        l3b_mask = sem("l3b_mask")
        l3o_mm = sem("l3o_mm")
        var3_ready = sem("var3_ready")
        rs3_ready = sem("rs3_ready")
        y_ready = sem("y_ready")
        dve_seq = sem("dve_seq")
        pool_seq = sem("pool_seq")
        act_seq = sem("act_seq")

        def free_r1(eng, u):
            n, f = u // NF, u % NF
            eng.wait_ge((lo_dve, lo_pool)[f % 2], 2 * n + f // 2 + 1)

        block = ctx.enter_context(nc.Block())

        @block.sync
        def _(sp):
            sp.dma_start(ids_row[:], in_ids_row).then_inc(ld_idrow, 16)
            sp.dma_start(ids_all[:], in_ids_all).then_inc(ld_ids, 16)
            sp.dma_start(ids_j[:], in_ids_j).then_inc(ld_ids, 16)
            sp.dma_start(cols[:], in_cols).then_inc(ld_ids, 16)
            sp.wait_ge(k_rows0, 1)
            for q in range(3):
                sp.dma_start(rows_f[32 * q:32 * q + 8, :], in_rows).then_inc(ld_rows, 16)
            sp.dma_start(wi_all[:], in_wi).then_inc(ld_wi, 16)
            sp.dma_start(x_t[:], in_x_t).then_inc(ld_xt, 16)
            sp.dma_start(mats[:, 0:MAT_EARLY], in_mats[:, 0:MAT_EARLY]).then_inc(ld_small, 16)
            sp.dma_start(x_nat[:], in_x_nat).then_inc(ld_xn, 16)
            sp.dma_start(wo_all[:], in_wo).then_inc(ld_wo, 16)
            for e in range(E1):
                if e >= RAW:
                    sp.wait_ge(w_lo, 2 * (e - RAW + 1))
                sp.dma_start(w1_raw[:, e % RAW, :], in_w1[:, e, :]).then_inc(ld_w[e % RAW], 16)
                sp.dma_start(w2_raw[:, e % RAW, :], in_w2[:, e, :]).then_inc(ld_w[e % RAW], 16)
            sp.wait_ge(dn0_done, NG)
            sp.dma_start(mats_l3, in_mats[:, MAT_EARLY:NMAT]).then_inc(ld_late, 16)
            sp.dma_start(bcast, in_bcast).then_inc(ld_late, 16)
            for c in range(NH):
                sp.wait_ge(y_ready, c + 1)
                sp.dma_start(out[:, c * GH:(c + 1) * GH, :], yout[:, c * GH:(c + 1) * GH, :]).then_inc(st_out, 16)
            sp.wait_ge(st_out, 16 * NH)

        @block.tensor
        def _(pe):
            ident = mat("ident")

            def style():
                pe.wait_ge(ld_small, 16)
                pe.wait_ge(k_oh, 1)
                pe.matmul(B0[0:64, 0:B], mat("subj", NSUBJ), ohs[:], start=True, stop=True).then_inc(sty_mm, 1)
                pe.wait_ge(sty_ev, 1)
                pe.matmul(B1[:, 0:B], mat("hyp_w1", 64), se_t[:], start=True, stop=True).then_inc(sty_mm, 1)
                pe.wait_ge(sty_ev, 2)
                pe.matmul(B0[:, 0:B], mat("hyp_w2"), hy1[:], start=True, stop=True).then_inc(sty_mm, 1)
                pe.wait_ge(sty_ev, 3)
                pe.matmul(B1[0:64, 0:B], mat("sty_w1"), hy2[:], start=True, stop=True).then_inc(sty_mm, 1)
                pe.wait_ge(sty_ev, 4)
                w = mat("sty_w2", 64)
                pe.matmul(B0[:, 0:B], w[:, 0:D], st1[:], start=True, stop=True).then_inc(sty_mm, 1)
                pe.matmul(B1[:, 0:B], w[:, D:2 * D], st1[:], start=True, stop=True).then_inc(sty_mm, 1)

            def l0_up(g):
                if g == 0:
                    pe.wait_ge(k_rows0, 2)
                    pe.wait_ge(k_oh, 3)
                    pe.wait_ge(ld_xt, 16)
                    pe.wait_ge(sty_done, 2)
                pe.wait_ge(wi_picked, g + 1)
                if g >= GH:
                    pe.wait_ge(gelu0_done, g)
                elif g >= 2:
                    pe.wait_ge(gelu0_done, g - 1)
                bank = bank_up(g)
                pe.matmul(bank, oh0[:, P * g:P * g + P], rows3[:, R_BI:R_BI + FF], start=True, stop=False,
                          skip_group_check=True)
                for j in range(GRP):
                    mm = pe.matmul(bank[S * j:S * j + S, :], x_t[:, P * g + S * j:P * g + S * j + S],
                                   wi_sel(g)[:, j, :], start=False, stop=True, skip_group_check=True)
                mm.then_inc(up0_done, 1)

            def l0_turn(g):
                pe.wait_ge(gelu0_done, g + 1)
                if g >= GH:
                    pe.wait_ge(h0t_done, g)
                    pe.wait_ge(combt_ready, 1)
                elif g >= 2:
                    pe.wait_ge(h0t_done, g - 1)
                if g == 0:
                    pe.wait_ge(ld_small, 16)
                for f in range(NF):
                    mm = pe.transpose(bank_tr(g)[:, P * f:P * f + P], h0[:, g % 2, P * f:P * f + P], ident)
                mm.then_inc(tr0_done, 1)

            def l0_down(g):
                pe.wait_ge(h0t_done, g + 1)
                pe.wait_ge(wo_picked, g + 1)
                if g >= GH:
                    pe.wait_ge(x1_ready, g)
                    pe.wait_ge(acc_ready, 1)
                elif g >= 2:
                    pe.wait_ge(x1_ready, g - 1)
                bank = bank_sm(g)
                pe.matmul(bank[:, 0:3 * D], oh0[:, P * g:P * g + P], rows3[:, R_BO:R_BO + 3 * D], start=True,
                          stop=False, skip_group_check=True)
                for f in range(NF):
                    for j in range(GRP):
                        mm = pe.matmul(bank[S * j:S * j + S, 0:D],
                                       h0t[:, g % 2, P * f + S * j:P * f + S * j + S],
                                       wo_sel(g)[:, j, P * f:P * f + P], start=False, stop=f == NF - 1,
                                       skip_group_check=True)
                mm.then_inc(dn0_done, 1)

            def z_turn(c):
                pe.wait_ge(z1_ready, GH * (c + 1))
                for i in range(GH):
                    mm = pe.transpose(B1[:, P * i:P * i + P], z1[:, i, :], ident)
                mm.then_inc(zt_done, 1)

            def route(c):
                pe.wait_ge(h2_ready, c + 1)
                for i in range(GH):
                    mm = pe.matmul(B2[:, E1 * i:E1 * i + E1], h2[:, P * i:P * i + P], mat("router"),
                                   start=True, stop=True)
                mm.then_inc(route_mm, 1)

            def comb_turn(c):
                pe.wait_ge(comb_ready, c + 1)
                for i in range(GH):
                    mm = pe.transpose(B1[0:E1, P * i:P * i + P], comb[:, c, i, :], ident)
                mm.then_inc(combt_mm, 1)

            def b2_sum(c):
                pe.wait_ge(combt_ready, c + 1)
                for i in range(GH):
                    mm = pe.matmul(B2[:, P * i:P * i + P], comb_t[:, P * i:P * i + P], mat("exp_b2", E1),
                                   start=True, stop=True)
                mm.then_inc(b2_mm, 1)

            def l1_up(n):
                c, e = n // E1, n % E1
                if c == 0:
                    pe.wait_ge(w_lo, 2 * (e + 1))
                    pe.wait_ge(w_hi, 2 * (e + 1))
                if e == 0:
                    pe.wait_ge(h2s_ready, c + 1)
                hi, lo = h2_hi[:, c, :], h2_lo[:, c, :]
                for f in range(NF):
                    u = NF * n + f
                    if u >= NU:
                        pe.wait_ge(relu_done, u - NU + 1)
                    whi, wlo = w1_hi[:, e, P * f:P * f + P], w1_lo[:, e, P * f:P * f + P]
                    pe.matmul(bank_u(u), whi, hi, start=True, stop=False)
                    pe.matmul(bank_u(u), whi, lo, start=False, stop=False)
                    pe.matmul(bank_u(u), wlo, hi, start=False, stop=True).then_inc(up1_done, 1)

            def l1_down(n):
                e = n % E1
                pe.wait_ge(hi_done, NF * (n + 1))
                pe.wait_ge(lo_dve, 2 * (n + 1))
                pe.wait_ge(lo_pool, 2 * (n + 1))
                if n >= 2:
                    pe.wait_ge(gate_done, n - 1)
                for i in range(GH):
                    o = bank_d(n)[:, P * i:P * i + P]
                    for f in range(NF):
                        hi = hid_hi[n % 2][:, f, P * i:P * i + P]
                        lo = hid_lo[n % 2][:, f, P * i:P * i + P]
                        whi, wlo = w2_hi[:, e, P * f:P * f + P], w2_lo[:, e, P * f:P * f + P]
                        pe.matmul(o, hi, whi, start=f == 0, stop=False)
                        pe.matmul(o, hi, wlo, start=False, stop=False)
                        mm = pe.matmul(o, lo, whi, start=False, stop=f == NF - 1)
                mm.then_inc(dn1_done, 1)

            def x2_turn(c):
                pe.wait_ge(gate_done, E1 * (c + 1))
                for i in range(GH):
                    mm = pe.transpose(B1[:, P * i:P * i + P], acc[:, GH * c + i, :], ident)
                mm.then_inc(x2t_mm, 1)

            def l2_down(c):
                pe.wait_ge(x2t_ready, c + 1)
                xv = tt.rearrange("p (g j s) -> p g j s", g=GH, j=GRP)
                for j in range(GRP):
                    mm = pe.matmul(B2[A2 * j:A2 * j + A2, 0:P], mat("downT")[:, 0:A2], xv[:, :, j, :],
                                   start=True, stop=True, skip_group_check=True)
                mm.then_inc(dproj_mm, 1)

            def l2_expert(c):
                pe.wait_ge(hb_ready, c + 1)
                if c == 0:
                    pe.wait_ge(k_bd, 1)
                for i in range(GH):
                    mm = pe.matmul(B1[:, S * i:S * i + S], bd_w[:, GH * c + i, :], hb[:, S * i:S * i + S],
                                   start=True, stop=True)
                mm.then_inc(exp_mm, 1)

            def l2_up(c):
                pe.wait_ge(bdh_ready, c + 1)
                for i in range(GH):
                    mm = pe.matmul(B2[:, P * i:P * i + P], bd_h[:, GH * c + i, :], mat("upT"), start=True,
                                   stop=True)
                mm.then_inc(up2_mm, 1)

            def x3_turn(c):
                pe.wait_ge(x3_ready, c + 1)
                for i in range(GH):
                    mm = pe.transpose(B1[:, P * i:P * i + P], x3[:, GH * c + i, :], ident)
                mm.then_inc(x3t_mm, 1)

            def l3_a(c, k):
                w = (mat("w1_nr"), mat("w1_tsr"), mat("w1_sr")[:, 0:P], mat("w1_sr")[:, P:2 * P])[k]
                if k == 0:
                    pe.wait_ge(x3t_ready, c + 1)
                    pe.wait_ge(ld_late, 32)
                if k == 3:
                    pe.wait_ge(l3a_act, 4 * c + 1)
                pe.matmul((B0, B2, B1, B0)[k], w, tt, start=True, stop=True).then_inc(l3a_mm, 1)

            def l3_b(c):
                pe.wait_ge(l3a_act, 4 * c + 4)
                pe.matmul(B2, mat("w2_sr0"), a_l3[:, 2, :], start=True, stop=False)
                pe.matmul(B2, mat("w2_sr1"), a_l3[:, 3, :], start=False, stop=True).then_inc(l3b_mm, 1)

            def l3_out(c):
                pe.wait_ge(l3a_mask, 2 * (c + 1))
                pe.wait_ge(l3b_mask, c + 1)
                for i in range(GH):
                    o = B0[:, P * i:P * i + P]
                    t = slice(P * i, P * i + P)
                    g = GH * c + i
                    pe.matmul(o, ohc[:, P * g:P * g + P], rows3[:, R_B3:R_B3 + D], start=True, stop=False)
                    pe.matmul(o, a_l3[:, 0, t], mat("w2_nr"), start=False, stop=False)
                    pe.matmul(o, a_l3[:, 1, t], mat("w2_tsr"), start=False, stop=False)
                    mm = pe.matmul(o, a_sr2[:, t], mat("w3_sr"), start=False, stop=True)
                mm.then_inc(l3o_mm, 1)

            def side(k):
                if k in (0, 2, 4, 6):
                    l0_up(GH + k // 2)
                if k in (2, 4, 6, 8):
                    l0_down(GH + k // 2 - 1)
                if k in (1, 3, 5, 7):
                    l0_turn(GH + k // 2)
                if k == 10:
                    z_turn(1)
                if k == 12:
                    route(1)
                if k == 14:
                    comb_turn(1)
                if k == 15:
                    b2_sum(1)
                if k == 18:
                    x2_turn(0)
                if k == 19:
                    l2_down(0)
                if k == 20:
                    l2_expert(0)
                if k == 21:
                    l2_up(0)
                if k == 24:
                    x3_turn(0)
                if k == 25:
                    l3_a(0, 0)
                    l3_a(0, 1)
                if k == 26:
                    l3_a(0, 2)
                    l3_a(0, 3)
                if k == 27:
                    l3_b(0)
                if k == 29:
                    l3_out(0)

            style()
            l0_up(0)
            l0_up(1)
            for g in range(GH):
                l0_turn(g)
                l0_down(g)
                if g + 2 < GH:
                    l0_up(g + 2)
            z_turn(0)
            route(0)
            l1_up(0)
            comb_turn(0)
            b2_sum(0)
            side(0)
            side(1)
            for n in range(1, NE):
                l1_up(n)
                side(2 * n)
                l1_down(n - 1)
                side(2 * n + 1)
            l1_down(NE - 1)
            x2_turn(1)
            l2_down(1)
            l2_expert(1)
            l2_up(1)
            x3_turn(1)
            for k in range(4):
                l3_a(1, k)
            l3_b(1)
            l3_out(1)

        @block.scalar
        def _(act):
            seq = [0]

            def link(ins):
                seq[0] += 1
                ins.then_inc(act_seq, 1)
                act.wait_ge(act_seq, seq[0])

            def style():
                act.wait_ge(ld_ids, 48)
                act.wait_ge(sty_mm, 1)
                nc.scalar.copy(se_t[:], B0[0:64, 0:B]).then_inc(sty_ev, 1)
                act.wait_ge(sty_mm, 2)
                nc.scalar.activation(hy1[:], B1[:, 0:B], ACT.Relu, bias=col(C_HB1)).then_inc(sty_ev, 1)
                act.wait_ge(sty_mm, 3)
                nc.scalar.activation(hy2[:], B0[:, 0:B], ACT.Identity, bias=col(C_HB2)).then_inc(sty_ev, 1)
                act.wait_ge(sty_mm, 4)
                nc.scalar.activation(st1[:], B1[0:64, 0:B], ACT.Relu, bias=col(C_SB1, 64)).then_inc(sty_ev, 1)
                act.wait_ge(sty_mm, 6)
                link(nc.scalar.activation(gam_raw[:], B0[:, 0:B], ACT.Identity, bias=col(C_SB2G)))
                link(nc.scalar.activation(bet_s[:], B1[:, 0:B], ACT.Identity, bias=col(C_SB2B)))
                link(nc.scalar.activation(gam_abs[:], gam_raw[:], ACT.Abs))
                link(nc.scalar.activation(gam_exp[:], gam_abs[:], ACT.Exp, scale=-1.0))
                nc.scalar.activation(gam_log[:], gam_exp[:], ACT.Ln, bias=1.0).then_inc(sty_done, 1)

            def pick_wo(g):
                if g == 0:
                    act.wait_ge(ld_idrow, 16)
                    act.wait_ge(ld_wo, 16)
                if g >= GH:
                    act.wait_ge(dn0_done, g)
                elif g >= 2:
                    act.wait_ge(dn0_done, g - 1)
                for j in range(GRP):
                    b = GRP * g + j
                    act.reg_load(reg, ids_row[0:1, b:b + 1])
                    e = act.snap(reg, min_val=0, max_val=E0 - 1)
                    ins = nc.scalar.copy(wo_sel(g)[:, j:j + 1, :], wo_all[:, bass.ds(e, 1), :])
                ins.then_inc(wo_picked, 1)

            def gelu0(g):
                act.wait_ge(up0_done, g + 1)
                if g >= 2:
                    act.wait_ge(tr0_done, g - 1)
                nc.scalar.activation(h0[:, g % 2, :], bank_up(g), ACT.Gelu).then_inc(gelu0_done, 1)

            def split_hi(e):
                act.wait_ge(ld_w[e % RAW], 32 * (e // RAW + 1))
                nc.scalar.copy(w1_hi[:, e, :], w1_raw[:, e % RAW, :]).then_inc(w_hi, 1)
                nc.scalar.copy(w2_hi[:, e, :], w2_raw[:, e % RAW, :]).then_inc(w_hi, 1)

            def ln_affine(c):
                act.wait_ge(zt_done, c + 1)
                if c:
                    act.wait_ge(route_mm, c)
                    act.wait_ge(h2s_ready, c)
                nc.scalar.activation(hn[:], B1, ACT.Identity, bias=col(C_LNB), scale=col(C_LNG)).then_inc(hn_ready, 1)

            def square(c):
                act.wait_ge(cen_ready, c + 1)
                if c:
                    act.wait_ge(tvar_ready, c)
                nc.scalar.activation(sq, cen[:], ACT.Square).then_inc(sq_ready, 1)

            def relu(n):
                e = n % E1
                for f in range(NF):
                    u = NF * n + f
                    act.wait_ge(up1_done, u + 1)
                    if u >= NR:
                        free_r1(act, u - NR)
                    c = C_EB1 + NF * e + f
                    nc.scalar.activation(r1[:, u % NR, :], bank_u(u), ACT.Relu, bias=col(c)).then_inc(relu_done, 1)

            def turn_copy(c, mm, ready, free, nfree):
                act.wait_ge(mm, c + 1)
                if nfree:
                    act.wait_ge(free, nfree)
                nc.scalar.copy(tt, B1).then_inc(ready, 1)

            def l2_gelu(c):
                act.wait_ge(dproj_mm, c + 1)
                if c:
                    act.wait_ge(exp_mm, c)
                nc.scalar.activation(hb[:], B2[:, 0:P], ACT.Gelu, bias=col(C_DB)).then_inc(hb_ready, 1)

            def l3_gelu(c, k):
                act.wait_ge(l3a_mm, 4 * c + k + 1)
                if c and k == 0:
                    act.wait_ge(l3o_mm, c)
                    act.wait_ge(l3b_mm, c)
                nc.scalar.activation(a_l3[:, k, :], (B0, B2, B1, B0)[k], ACT.Gelu,
                                     bias=col((C_B1NR, C_B1TSR, C_B1SR0, C_B1SR1)[k])).then_inc(l3a_act, 1)

            def l3_gelu2(c):
                act.wait_ge(l3b_mm, c + 1)
                nc.scalar.activation(a_sr2, B2, ACT.Gelu, bias=col(C_B2SR)).then_inc(l3b_act, 1)

            def side(k):
                if k in (0, 2, 4, 6):
                    gelu0(GH + k // 2)
                    pick_wo(GH + k // 2)
                if k == 10:
                    ln_affine(1)
                if k == 11:
                    square(1)
                if k == 18:
                    turn_copy(0, x2t_mm, x2t_ready, x2t_ready, 0)
                if k == 19:
                    l2_gelu(0)
                if k == 24:
                    turn_copy(0, x3t_mm, x3t_ready, dproj_mm, 1)
                if k == 25:
                    l3_gelu(0, 0)
                    l3_gelu(0, 1)
                if k == 26:
                    l3_gelu(0, 2)
                    l3_gelu(0, 3)
                if k == 27:
                    l3_gelu2(0)

            with act.register("act_expert") as reg:
                style()
                gelu0(0)
                pick_wo(0)
                gelu0(1)
                pick_wo(1)
                split_hi(0)
                for g in range(2, GH):
                    gelu0(g)
                    pick_wo(g)
                    split_hi(g - 1)
                split_hi(3)
                ln_affine(0)
                square(0)
                for e in range(4, E1):
                    split_hi(e)
                for n in range(NE):
                    relu(n)
                    side(2 * n)
                    side(2 * n + 1)
                turn_copy(1, x2t_mm, x2t_ready, l3a_mm, 4)
                l2_gelu(1)
                turn_copy(1, x3t_mm, x3t_ready, dproj_mm, 2)
                for k in range(4):
                    l3_gelu(1, k)
                l3_gelu2(1)

        @block.vector
        def _(dve):
            V = nc.vector
            seq = [0]

            def link(ins):
                seq[0] += 1
                ins.then_inc(dve_seq, 1)
                dve.wait_ge(dve_seq, seq[0])

            def by_seq(ap, n):
                return ap.unsqueeze(2).broadcast_to([ap.shape[0], n, S])

            def tables():
                link(V.memset(rows3[:], 0.0))
                V.memset(euler[:], EULER)
                V.memset(half_exp[:], HALF_EXP).then_inc(k_rows0, 1)
                dve.wait_ge(ld_ids, 48)
                link(V.tensor_copy(ids_f[:], ids_all[:]))
                V.tensor_scalar(ohs[:], ids_f[0:NSUBJ, 1, :], col(C_P32, NSUBJ), None, ALU.is_equal).then_inc(k_oh, 1)
                for src, dst in ((0, oh0), (3, ohc)):
                    V.tensor_scalar(dst[:].rearrange("p (b s) -> p b s", s=S), by_seq(ids_f[0:96, src, :], B),
                                    col(C_P32, 96), None, ALU.is_equal).then_inc(k_oh, 1)
                dve.wait_ge(ld_rows, 48)
                for q in range(3):
                    rows = slice(32 * q, 32 * q + 8)
                    link(V.tensor_copy(rows3[rows, :], rows_f[rows, :]))
                    for _ in range(q):
                        link(V.tensor_tensor(rows_f[rows, :], rows_f[rows, :], rows3[rows, :], ALU.subtract))
                        link(V.tensor_copy(rows3[rows, :], rows_f[rows, :]))
                V.memset(l2b[:, 0:1], 0.0).then_inc(k_rows0, 1)

            def style():
                dve.wait_ge(sty_done, 1)
                link(V.scalar_tensor_tensor(gam_s[:], gam_raw[:], 0.0, gam_log[:], ALU.max, ALU.add))
                V.tensor_scalar(gam_s[:], gam_s[:], 1e-8, None, ALU.add).then_inc(sty_done, 1)
                dve.wait_ge(sty_done, 2)

            def l2_index():
                link(V.tensor_scalar(l2i_f[:], ids_j[:], -1.0, 16.0, ALU.max, ALU.min))
                link(V.tensor_scalar(l2i_f[:], l2i_f[:], 1.0, float(A2), ALU.add, ALU.mult))
                V.tensor_scalar(l2i[:], l2i_f[:], col(C_P32), None, ALU.add).then_inc(k_const, 1)

            def cond_masks():
                for k in range(NCOND):
                    V.tensor_scalar(cmask[:, k, :], ids_f[:, 3, :], float(k), None, ALU.is_equal).then_inc(k_oh, 1)

            def l2_tables():
                dve.wait_ge(ld_l2, 16 * NG)
                dve.wait_ge(k_bd0, 2)
                for j in range(GRP):
                    rows = slice(A2 * j, A2 * j + A2)
                    V.tensor_copy(bd_w[rows, :, A2 * j:A2 * j + A2], l2g[rows, :, 0:A2])
                V.tensor_tensor(l2b[:], l2g[:, :, A2], l2g[:, :, A2 + 1], ALU.add).then_inc(k_bd, 1)

            def pick_wi(g):
                if g == 0:
                    dve.wait_ge(ld_idrow, 16)
                    dve.wait_ge(ld_wi, 16)
                if g >= GH:
                    dve.wait_ge(up0_done, g)
                elif g >= 2:
                    dve.wait_ge(up0_done, g - 1)
                for j in range(GRP):
                    b = GRP * g + j
                    dve.reg_load(reg, ids_row[0:1, b:b + 1])
                    e = dve.snap(reg, min_val=0, max_val=E0 - 1)
                    ins = V.tensor_copy(wi_sel(g)[:, j:j + 1, :], wi_all[:, bass.ds(e, 1), :])
                ins.then_inc(wi_picked, 1)

            def hidden_t(g):
                dve.wait_ge(tr0_done, g + 1)
                if g >= 2:
                    dve.wait_ge(dn0_done, g - 1)
                V.tensor_copy(h0t[:, g % 2, :], bank_tr(g)).then_inc(h0t_done, 1)

            def l0_sum(g):
                dve.wait_ge(dn0_done, g + 1)
                if g == 0:
                    dve.wait_ge(ld_xn, 16)
                i = g % 2
                link(V.tensor_tensor(res0[:, i, :], bank_sm(g)[:, 0:D], x_nat[:, g, :], ALU.add))
                link(V.bn_stats(stat0[:, i, :], res0[:, i, :]))
                if g >= 2:
                    dve.wait_ge(rs0_ready, g - 1)
                V.bn_aggr(mv0[:, i, :], stat0[:, i, :]).then_inc(var0_ready, 1)

            def l0_norm(g):
                i = g % 2
                dve.wait_ge(rs0_ready, g + 1)
                link(V.tensor_scalar(y0[:, i, :], res0[:, i, :], mv0[:, i, 0:1], rs0[:, i, 1:2], ALU.subtract, ALU.mult))
                link(V.tensor_tensor(y0[:, i, :], y0[:, i, :], bank_sm(g)[:, D:2 * D], ALU.mult))
                V.tensor_tensor(x1[:, g, :], y0[:, i, :], bank_sm(g)[:, 2 * D:3 * D], ALU.add).then_inc(x1_ready, 1)
                dve.wait_ge(x1_ready, g + 1)
                link(V.bn_stats(stat1[:, i, :], x1[:, g, :]))
                if g >= 2:
                    dve.wait_ge(rs1_ready, g - 1)
                V.bn_aggr(mv1[:, i, :], stat1[:, i, :]).then_inc(var1_ready, 1)

            def l1_ln(g):
                i = g % 2
                dve.wait_ge(rs1_ready, g + 1)
                if g == GH:
                    dve.wait_ge(tvar_ready, 1)
                V.tensor_scalar(z1[:, g % GH, :], x1[:, g, :], mv1[:, i, 0:1], rs1[:, i, 1:2], ALU.subtract,
                                ALU.mult).then_inc(z1_ready, 1)

            def time_norm_a(c):
                hv = hn[:].rearrange("p (b s) -> p b s", s=S)
                dve.wait_ge(hn_ready, c + 1)
                link(V.tensor_reduce(tsum[:], hv, AX.X, ALU.add))
                link(V.tensor_scalar(tmean[:], tsum[:], 1.0 / S, None, ALU.mult))
                V.tensor_tensor(cen[:].rearrange("p (b s) -> p b s", s=S), hv, by_seq(tmean[:], BH),
                                ALU.subtract).then_inc(cen_ready, 1)

            def time_norm_b(c):
                dve.wait_ge(sq_ready, c + 1)
                V.tensor_reduce(tvar[:], sq.rearrange("p (b s) -> p b s", s=S), AX.X,
                                ALU.add).then_inc(tvar_ready, 1)
                dve.wait_ge(trs_ready, c + 1)
                seqs = slice(BH * c, BH * c + BH)
                h2v = h2[:].rearrange("p (b s) -> p b s", s=S)
                link(V.tensor_tensor(tscale[:], trs[:, 1, :], gam_s[:, seqs], ALU.mult))
                link(V.tensor_tensor(h2v, cen[:].rearrange("p (b s) -> p b s", s=S), by_seq(tscale[:], BH), ALU.mult))
                V.tensor_tensor(h2v, h2v, by_seq(bet_s[:, seqs], BH), ALU.add).then_inc(h2_ready, 1)
                dve.wait_ge(h2_ready, c + 1)
                link(V.tensor_copy(h2_hi[:, c, :], h2[:]))
                V.tensor_tensor(h2_lo[:, c, :], h2[:], h2_hi[:, c, :].bitcast(F32), ALU.subtract).then_inc(h2s_ready, 1)

            def top2(c):
                dve.wait_ge(route_mm, c + 1)
                link(V.tensor_copy(logit[:], B2[:, 0:GH * E1].rearrange("p (g e) -> p g e", e=E1)))
                for i in range(GH):
                    link(V.max(top[:, i, :], logit[:, i, :]))
                    link(V.max_index(topi[:, i, :], top[:, i, :], logit[:, i, :]))
                link(V.tensor_copy(topf[:], topi[:]))
                V.tensor_tensor(dif[:], top[:, :, 1], top[:, :, 0], ALU.subtract).then_inc(dif_ready, 1)
                dve.wait_ge(ratio_ready, c + 1)
                link(V.tensor_scalar(wtop[:, 0, :], ratio[:], 1.0, None, ALU.add))
                link(V.reciprocal(wtop[:, 1, :], wtop[:, 0, :]))
                link(V.tensor_tensor(wtop[:, 2, :], wtop[:, 1, :], ratio[:], ALU.mult))
                ids = iota8[:].unsqueeze(1).broadcast_to([P, GH, E1])

                def wide(ap):
                    return ap.unsqueeze(2).broadcast_to([P, GH, E1])

                link(V.tensor_tensor(eq1[:], ids, wide(topf[:, :, 0]), ALU.is_equal))
                link(V.tensor_tensor(eq2[:], ids, wide(topf[:, :, 1]), ALU.is_equal))
                link(V.tensor_tensor(eq1[:], eq1[:], wide(wtop[:, 1, :]), ALU.mult))
                link(V.tensor_tensor(eq2[:], eq2[:], wide(wtop[:, 2, :]), ALU.mult))
                V.tensor_tensor(comb[:, c, :, :], eq1[:], eq2[:], ALU.add).then_inc(comb_ready, 1)

            def comb_copy(c):
                dve.wait_ge(combt_mm, c + 1)
                if c:
                    dve.wait_ge(b2_mm, c)
                V.tensor_copy(comb_t[:], B1[0:E1, :]).then_inc(combt_ready, 1)

            def acc_init(c):
                dve.wait_ge(b2_mm, c + 1)
                gs = slice(GH * c, GH * c + GH)
                V.tensor_tensor(acc[:, gs, :], B2.rearrange("p (g d) -> p g d", d=D), x1[:, gs, :],
                                ALU.add).then_inc(acc_ready, 1)
                dve.wait_ge(acc_ready, c + 1)

            def hid_split(n):
                for f in range(NF):
                    u = NF * n + f
                    dve.wait_ge(relu_done, u + 1)
                    if n >= 2 and f == 0:
                        dve.wait_ge(dn1_done, n - 1)
                    V.tensor_copy(hid_hi[n % 2][:, f, :], r1[:, u % NR, :]).then_inc(hi_done, 1)
                    if f % 2 == 0:
                        dve.wait_ge(hi_done, u + 1)
                        V.tensor_tensor(hid_lo[n % 2][:, f, :], r1[:, u % NR, :],
                                        hid_hi[n % 2][:, f, :].bitcast(F32), ALU.subtract).then_inc(lo_dve, 1)

            def gate(n):
                c, e = n // E1, n % E1
                dve.wait_ge(dn1_done, n + 1)
                if n:
                    dve.wait_ge(gate_done, n)
                for i in range(GH):
                    g = GH * c + i
                    ins = V.scalar_tensor_tensor(acc[:, g, :], bank_d(n)[:, P * i:P * i + P],
                                                 comb[:, c, i, e:e + 1], acc[:, g, :], ALU.mult, ALU.add)
                ins.then_inc(gate_done, 1)

            def l2_block(c):
                dve.wait_ge(exp_mm, c + 1)
                if c == 0:
                    dve.wait_ge(k_bd0, 2)
                gs = slice(GH * c, GH * c + GH)
                for j in range(GRP):
                    rows = slice(A2 * j, A2 * j + A2)
                    ins = V.tensor_tensor(bd_h[rows, gs, S * j:S * j + S],
                                          B1[rows, 0:P].rearrange("p (g s) -> p g s", s=S),
                                          by_seq(l2b[rows, gs], GH), ALU.add)
                ins.then_inc(bdh_ready, 1)

            def norm_stats(ready):
                for i in range(GH):
                    ins = V.bn_stats(stat2[:, i, :], pre[:, i, :])
                link(ins)
                for i in range(GH):
                    ins = V.bn_aggr(mv2[:, i, :], stat2[:, i, :])
                ins.then_inc(ready, 1)

            def norm_apply(dst, gamma, beta, ready):
                for i in range(GH):
                    ins = V.tensor_scalar(zz[:, i, :], pre[:, i, :], mv2[:, i, 0:1], rs2[:, 1, i:i + 1],
                                          ALU.subtract, ALU.mult)
                link(ins)
                link(V.tensor_tensor(zz, zz, gamma.unsqueeze(1).broadcast_to([P, GH, D]), ALU.mult))
                V.tensor_tensor(dst, zz, beta.unsqueeze(1).broadcast_to([P, GH, D]), ALU.add).then_inc(ready, 1)

            def l2_sum(c):
                dve.wait_ge(up2_mm, c + 1)
                dve.wait_ge(accb_ready, c + 1)
                link(V.tensor_tensor(pre, B2.rearrange("p (g d) -> p g d", d=D), accb, ALU.add))
                norm_stats(var2_ready)

            def l2_norm(c):
                dve.wait_ge(rs2_ready, c + 1)
                dve.wait_ge(ld_late, 32)
                norm_apply(x3[:, GH * c:GH * c + GH, :], bcast[:, 1, :], bcast[:, 2, :], x3_ready)

            def mask(c, k, act_sem, need, buf, ready):
                dve.wait_ge(act_sem, need)
                v = buf.rearrange("p (b s) -> p b s", s=S)
                V.tensor_tensor(v, v, by_seq(cmask[:, k, BH * c:BH * c + BH], BH), ALU.mult).then_inc(ready, 1)

            def l3_sum(c):
                dve.wait_ge(l3o_mm, c + 1)
                dve.wait_ge(x3_ready, c + 1)
                link(V.tensor_tensor(pre, B0.rearrange("p (g d) -> p g d", d=D), x3[:, GH * c:GH * c + GH, :],
                                     ALU.add))
                norm_stats(var3_ready)

            def l3_norm(c):
                dve.wait_ge(rs3_ready, c + 1)
                norm_apply(yout[:, GH * c:GH * c + GH, :], bcast[:, 3, :], bcast[:, 4, :], y_ready)

            def side(k):
                if k == 0:
                    pick_wi(GH)
                if k in (1, 3, 5):
                    pick_wi(GH + k // 2 + 1)
                if k in (1, 3, 5, 7):
                    hidden_t(GH + k // 2)
                if k in (2, 4, 6, 8):
                    l0_sum(GH + k // 2 - 1)
                if k in (3, 5, 7, 9):
                    l0_norm(GH + k // 2 - 1)
                if k in (4, 6, 8, 10):
                    l1_ln(GH + k // 2 - 2)
                if k == 10:
                    time_norm_a(1)
                if k == 11:
                    time_norm_b(1)
                if k == 13:
                    l2_tables()
                if k == 12:
                    top2(1)
                if k == 14:
                    comb_copy(1)
                if k == 15:
                    acc_init(1)
                if k == 20:
                    l2_block(0)
                if k == 21:
                    l2_sum(0)
                if k == 22:
                    l2_norm(0)
                if k == 25:
                    mask(0, 0, l3a_act, 1, a_l3[:, 0, :], l3a_mask)
                    mask(0, 1, l3a_act, 2, a_l3[:, 1, :], l3a_mask)
                if k == 27:
                    mask(0, 2, l3b_act, 1, a_sr2, l3b_mask)
                if k == 29:
                    l3_sum(0)
                if k == 30:
                    l3_norm(0)

            with dve.register("dve_expert") as reg:
                tables()
                l2_index()
                cond_masks()
                style()
                pick_wi(0)
                pick_wi(1)
                for g in range(GH):
                    hidden_t(g)
                    if g + 2 < GH:
                        pick_wi(g + 2)
                    l0_sum(g)
                    if g >= 1:
                        l0_norm(g - 1)
                    if g >= 2:
                        l1_ln(g - 2)
                l0_norm(GH - 1)
                l1_ln(GH - 2)
                l1_ln(GH - 1)
                time_norm_a(0)
                time_norm_b(0)
                top2(0)
                comb_copy(0)
                acc_init(0)
                for n in range(NE):
                    hid_split(n)
                    side(2 * n)
                    if n:
                        gate(n - 1)
                    side(2 * n + 1)
                gate(NE - 1)
                l2_block(1)
                l2_sum(1)
                l2_norm(1)
                mask(1, 0, l3a_act, 5, a_l3[:, 0, :], l3a_mask)
                mask(1, 1, l3a_act, 6, a_l3[:, 1, :], l3a_mask)
                mask(1, 2, l3b_act, 2, a_sr2, l3b_mask)
                l3_sum(1)
                l3_norm(1)

        @block.gpsimd
        def _(pool):
            G = nc.gpsimd
            seq = [0]

            def link(ins):
                seq[0] += 1
                ins.then_inc(pool_seq, 1)
                pool.wait_ge(pool_seq, seq[0])

            def inv_sqrt(src, tmp, dst, scale, eps, ready):
                link(G.tensor_scalar(tmp, src, scale, eps, ALU.mult, ALU.add))
                G.tensor_tensor(dst, tmp, half_exp[:, 0:tmp.shape[-1]], ALU.pow).then_inc(ready, 1)

            def rs_l0(g):
                i = g % 2
                pool.wait_ge(var0_ready, g + 1)
                inv_sqrt(mv0[:, i, 1:2], rs0[:, i, 0:1], rs0[:, i, 1:2], 1.0, 1e-12, rs0_ready)

            def rs_l1(g):
                i = g % 2
                pool.wait_ge(var1_ready, g + 1)
                inv_sqrt(mv1[:, i, 1:2], rs1[:, i, 0:1], rs1[:, i, 1:2], 1.0, 1e-5, rs1_ready)

            def rs_time(c):
                pool.wait_ge(tvar_ready, c + 1)
                inv_sqrt(tvar[:], trs[:, 0, :], trs[:, 1, :], 1.0 / S, 1e-8, trs_ready)

            def exp_dif(c):
                pool.wait_ge(dif_ready, c + 1)
                G.tensor_tensor(ratio[:], euler[:], dif[:], ALU.pow).then_inc(ratio_ready, 1)

            def split_lo(e):
                pool.wait_ge(w_hi, 2 * (e + 1))
                G.tensor_tensor(w1_lo[:, e, :], w1_raw[:, e % RAW, :], w1_hi[:, e, :].bitcast(F32),
                                ALU.subtract).then_inc(w_lo, 1)
                G.tensor_tensor(w2_lo[:, e, :], w2_raw[:, e % RAW, :], w2_hi[:, e, :].bitcast(F32),
                                ALU.subtract).then_inc(w_lo, 1)

            def hid_lo_half(n):
                for f in range(1, NF, 2):
                    u = NF * n + f
                    pool.wait_ge(hi_done, u + 1)
                    G.tensor_tensor(hid_lo[n % 2][:, f, :], r1[:, u % NR, :],
                                    hid_hi[n % 2][:, f, :].bitcast(F32), ALU.subtract).then_inc(lo_pool, 1)

            def up_bias(c):
                pool.wait_ge(gate_done, E1 * (c + 1))
                pool.wait_ge(ld_late, 32)
                if c:
                    pool.wait_ge(var2_ready, c)
                G.tensor_tensor(accb, acc[:, GH * c:GH * c + GH, :],
                                bcast[:, 0, :].unsqueeze(1).broadcast_to([P, GH, D]), ALU.add).then_inc(accb_ready, 1)

            def rs_l2(c):
                pool.wait_ge(var2_ready, c + 1)
                inv_sqrt(mv2[:, :, 1], rs2[:, 0, :], rs2[:, 1, :], 1.0, 1e-5, rs2_ready)

            def rs_l3(c):
                pool.wait_ge(var3_ready, c + 1)
                inv_sqrt(mv2[:, :, 1], rs2[:, 0, :], rs2[:, 1, :], 1.0, 1e-5, rs3_ready)

            def side(k):
                if k in (2, 4, 6, 8):
                    rs_l0(GH + k // 2 - 1)
                if k in (3, 5, 7, 9):
                    rs_l1(GH + k // 2 - 1)
                if k == 9:
                    pool.wait_ge(up0_done, NG)
                    pool.wait_ge(wo_picked, NG)
                    G.memset(bd_h, 0.0).then_inc(k_bd0, 1)
                    G.memset(bd_w, 0.0).then_inc(k_bd0, 1)
                if k == 11:
                    rs_time(1)
                if k == 12:
                    exp_dif(1)
                if k == 18:
                    up_bias(0)
                if k == 21:
                    rs_l2(0)
                if k == 29:
                    rs_l3(0)

            G.iota(iota8[:], pattern=[[1, E1]], base=0, channel_multiplier=0).then_inc(k_const, 1)
            pool.wait_ge(k_const, 2)
            for g in range(NG):
                G.indirect_dma_start(l2g[:, g, :], None, in_l2tab,
                                     bass.IndirectOffsetOnAxis(ap=l2i[:, g:g + 1], axis=0)).then_inc(ld_l2, 16)
            pool.wait_ge(k_rows0, 1)
            for g in range(GH):
                rs_l0(g)
                if g < GH:
                    split_lo(g) if g < 3 else None
                rs_l1(g)
            split_lo(3)
            rs_time(0)
            exp_dif(0)
            for e in range(4, E1):
                split_lo(e)
            for n in range(NE):
                hid_lo_half(n)
                side(2 * n)
                side(2 * n + 1)
            up_bias(1)
            rs_l2(1)
            rs_l3(1)


def lay_out(i, np):
    f4 = np.float32
    x = np.asarray(i["x"])
    ids = [np.asarray(i[k]).astype(np.int32, copy=False) for k in ("itok_B_0_7", "itok_B_6_14", "itok_B_0_15", "itok_B_0_2")]
    cols = np.zeros((P, NCOL), f4)

    def put(c, v):
        cols[:v.shape[0], c] = v

    put(C_LNG, i["L1_cond_ln_g"])
    put(C_LNB, i["L1_cond_ln_b"])
    put(C_HB1, i["L1_cond_hyp_b1"])
    put(C_HB2, i["L1_cond_hyp_b2"])
    put(C_SB1, i["L1_cond_sty_b1"])
    put(C_SB2G, i["L1_cond_sty_b2"][:D])
    put(C_SB2B, i["L1_cond_sty_b2"][D:])
    put(C_B1NR, i["L3_cond_b1_nr"])
    put(C_B1TSR, i["L3_cond_b1_tsr"])
    put(C_B1SR0, i["L3_cond_b1_sr"][:P])
    put(C_B1SR1, i["L3_cond_b1_sr"][P:])
    put(C_B2SR, i["L3_cond_b2_sr"])
    put(C_DB, np.tile(i["L2_cond_down_b"], GRP))
    put(C_P32, np.tile(np.arange(32, dtype=f4), 4))
    cols[:, C_EB1:] = i["L1_cond_exp_b1"].reshape(E1 * NF, P).T
    mats = np.zeros((P, NMAT), f4)
    parts = dict(hyp_w1=i["L1_cond_hyp_w1"], hyp_w2=i["L1_cond_hyp_w2"], sty_w1=i["L1_cond_sty_w1"],
                 sty_w2=i["L1_cond_sty_w2"], subj=i["L1_cond_subj_emb"], router=i["L1_cond_router_w"],
                 ident=np.eye(P, dtype=f4), downT=np.tile(i["L2_cond_down_W"].T, (1, GRP)),
                 upT=np.tile(i["L2_cond_up_W"].T, (GRP, 1)), exp_b2=i["L1_cond_exp_b2"],
                 w1_nr=i["L3_cond_w1_nr"], w1_tsr=i["L3_cond_w1_tsr"], w1_sr=i["L3_cond_w1_sr"],
                 w2_sr0=i["L3_cond_w2_sr"][:P], w2_sr1=i["L3_cond_w2_sr"][P:], w2_nr=i["L3_cond_w2_nr"],
                 w2_tsr=i["L3_cond_w2_tsr"], w3_sr=i["L3_cond_w3_sr"])
    for name, m in parts.items():
        a, b = MATS[name]
        mats[:m.shape[0], a:b] = m
    rows = np.zeros((8, NROW), f4)
    rows[:, R_BI:R_BI + FF] = i["L0_cond_bi"]
    rows[:, R_BO:R_BO + D] = i["L0_cond_bo"]
    rows[:, R_GAM:R_GAM + D] = i["L0_cond_gamma"]
    rows[:, R_BET:R_BET + D] = i["L0_cond_beta"]
    rows[0, R_B3:] = i["L3_cond_b2_nr"]
    rows[1, R_B3:] = i["L3_cond_b2_tsr"]
    rows[2, R_B3:] = i["L3_cond_b3_sr"]
    bc = np.stack([i["L2_cond_up_b"], i["L2_cond_ln_gamma"], i["L2_cond_ln_beta"], i["L3_cond_gamma"], i["L3_cond_beta"]])
    tab = np.zeros((NBLK, A2, A2 + 2), f4)
    tab[1:17, :, :A2] = i["L2_cond_expert_W"].transpose(0, 2, 1)
    tab[1:17, :, A2] = i["L2_cond_expert_b"]
    tab[1:17, :, A2 + 1] = i["L2_cond_domain_emb"]
    for blk, e in ((0, 0), (17, 15)):
        tab[blk, :, :A2] = np.eye(A2, dtype=f4)
        tab[blk, :, A2 + 1] = i["L2_cond_domain_emb"][e]

    def w_in(w):
        return w.transpose(1, 0, 2)

    def w_out(w):
        return w.reshape(w.shape[0], NF, P, D).transpose(2, 0, 1, 3).reshape(P, w.shape[0], NF * D)

    return {
        "x_nat": x.reshape(NG, P, D).transpose(1, 0, 2),
        "x_t": x.reshape(NTOK, D).T,
        "ids_row": ids[0].reshape(1, B),
        "ids_all": np.broadcast_to(np.stack(ids)[None], (P, 4, B)),
        "ids_j": np.repeat(ids[2].reshape(NG, GRP).T, A2, axis=0),
        "cols": cols,
        "mats": mats,
        "rows": rows,
        "bcast": np.broadcast_to(bc[None], (P, 5, D)),
        "l2tab": tab.reshape(NBLK * A2, A2 + 2),
        "wi": w_in(i["L0_cond_Wi"]),
        "wo": w_out(i["L0_cond_Wo"]),
        "w1": w_in(i["L1_cond_exp_w1"]),
        "w2": w_out(i["L1_cond_exp_w2"]),
    }


def kernel(**inputs):
    import numpy as np
    import concourse.bacc as bacc
    from concourse.bass_utils import run_bass_kernel_spmd

    laid = lay_out({k: np.asarray(v) for k, v in inputs.items()}, np)
    nc = bacc.Bacc("TRN2", target_bir_lowering=False, num_devices=1)
    arrays, aps = {}, {}
    for name, a in laid.items():
        a = np.ascontiguousarray(a)
        arrays[f"in_{name}_dram"] = a
        aps[f"in_{name}"] = nc.dram_tensor(f"in_{name}_dram", a.shape, mybir.dt.from_np(a.dtype),
                                           kind="ExternalInput").ap()
    out = nc.dram_tensor("out_dram", (P, NG, D), F32, kind="ExternalOutput").ap()
    build_program(nc, out=out, **aps)
    r = run_bass_kernel_spmd(nc, [arrays], core_ids=[0])
    got = r.results[0]["out_dram"]
    return got.transpose(1, 0, 2).reshape(B, S, D)
```

```python
import concourse.bass as bass
from concourse import mybir
from contextlib import ExitStack

F32 = mybir.dt.float32
F32R = mybir.dt.float32r
BF16 = mybir.dt.bfloat16
I32 = mybir.dt.int32
U32 = mybir.dt.uint32
ALU = mybir.AluOpType
ACT = mybir.ActivationFunctionType
AX = mybir.AxisListType

P = 128
D = 128
B, S = 32, 32
NTOK = B * S
GRP = P // S
NG = NTOK // P
NH = 2
GH = NG // NH
BH = B // NH
T = NTOK // NH
FF = 512
NF = FF // P
E0, E1, NSUBJ = 8, 8, 32
A2 = 32
NCOND = 3
NBLK = 18
RAW = 4
PG = 2
PS = PG * GRP
PT = PG * P
NE = NH * E1
NU = 3
NR = 3
HALF_EXP = -0.5
EULER = 2.718281828459045

C_LNG, C_LNB, C_HB1, C_HB2, C_SB1, C_SB2G, C_SB2B = range(7)
C_B1NR, C_B1TSR, C_B1SR0, C_B1SR1, C_B2SR, C_DB, C_P32 = range(7, 14)
C_EB1 = 14
NCOL = C_EB1 + E1 * NF

MATS = {}
NMAT = 0
for _name, _w in (("hyp_w1", 128), ("hyp_w2", 128), ("sty_w1", 64), ("sty_w2", 256), ("subj", 64),
                  ("router", 8), ("ident", 128), ("downT", 32), ("upT", 128), ("exp_b2", 128),
                  ("w1_nr", 128), ("w1_tsr", 128), ("w1_sr", 256), ("w2_sr0", 128), ("w2_sr1", 128),
                  ("w2_nr", 128), ("w2_tsr", 128), ("w3_sr", 128)):
    MATS[_name] = (NMAT, NMAT + _w)
    NMAT += _w
MAT_EARLY = MATS["w1_nr"][0]

R_BI, R_BO, R_GAM, R_BET, R_B3, R_UB = 0, 512, 640, 768, 896, 1024
NROW = 1152
RW = 8 * NROW // P


def build_program(nc, in_x_nat, in_x_t, in_ids_row, in_ids_all, in_ids_j, in_cols, in_mats, in_rows,
                  in_bcast, in_l2tab, in_wi, in_wo, in_w1, out):
    ctx = ExitStack()
    with ctx:
        def sb(name, shape, dt=F32):
            return ctx.enter_context(nc.sbuf_tensor(name, shape, dt))

        def sem(name):
            return ctx.enter_context(nc.semaphore(name))

        x_nat = sb("x_nat", [P, NG, D])
        x_t = sb("x_t", [P, NTOK])
        ids_row = sb("ids_row", [1, B], I32)
        ids_all = sb("ids_all", [P, 4, B], I32)
        ids_f = sb("ids_f", [P, 4, B])
        ids_j = sb("ids_j", [P, NG], I32)
        cols = sb("cols", [P, NCOL])
        mats = sb("mats", [P, MAT_EARLY])
        bcast = sb("bcast", [P, 4, D])
        rows_p = sb("rows_p", [P, RW])
        rows_q = sb("rows_q", [P, 3, RW], BF16)
        rows3 = sb("rows3", [96, NROW], BF16)
        w1_hi = sb("w1_hi", [P, E1, FF], F32R)
        w1_lo = sb("w1_lo", [P, E1, FF], F32R)
        w2_hi = sb("w2_hi", [P, E1, FF], F32R)
        w2_lo = sb("w2_lo", [P, E1, FF], F32R)
        wi_all = sb("wi_all", [P, E0, FF])
        wi_sel0 = sb("wi_sel0", [P, GRP, FF])
        wo_sel0 = sb("wo_sel0", [P, GRP, FF])
        oh0 = sb("oh0", [96, NTOK], BF16)
        ohc = x_t[0:96, 0:NTOK // 2].bitcast(BF16)
        ohs = sb("ohs", [NSUBJ, B])
        cmask = sb("cmask", [P, NCOND, B])
        half_exp = sb("half_exp", [P, 16])
        euler = sb("euler", [P, GH])
        iota8 = sb("iota8", [P, E1], I32)
        se_t = sb("se_t", [64, B])
        hy1 = sb("hy1", [P, B])
        hy2 = sb("hy2", [P, B])
        st1 = sb("st1", [64, B])
        gam_raw = sb("gam_raw", [P, B])
        gam_abs = sb("gam_abs", [P, B])
        gam_exp = sb("gam_exp", [P, B])
        gam_log = sb("gam_log", [P, B])
        gam_s = sb("gam_s", [P, B])
        bet_s = sb("bet_s", [P, B])
        with nc.sbuf_tensor("w_raw", [P, RAW, 2 * FF], F32) as w_raw_ring:
            pass
        hid_hi0 = sb("hid_hi0", [P, NF, T], F32R)
        hid_lo0 = sb("hid_lo0", [P, NF, T], F32R)
        with nc.sbuf_tensor("wi_sel1", [P, GRP, FF], F32) as wi_sel1, \
                nc.sbuf_tensor("wo_sel1", [P, GRP, FF], F32) as wo_sel1:
            pass
        hid_hi = [hid_hi0, sb("hid_hi1", [P, NF, T], F32R)]
        hid_lo = [hid_lo0, sb("hid_lo1", [P, NF, T], F32R)]

        def wi_sel(g):
            return wi_sel1 if g < GH and g % 2 else wi_sel0

        def wo_sel(g):
            return wo_sel1 if g < GH and g % 2 else wo_sel0

        def w_raw(e, k):
            return w_raw_ring[:, e % RAW, k * FF:k * FF + FF]

        h0 = sb("h0", [P, 2, FF])
        h0t = sb("h0t", [P, 2, FF])
        res0 = sb("res0", [P, 2, D])
        y0 = sb("y0", [P, 2, D])
        stat0 = sb("stat0", [P, 2, 6])
        mv0 = sb("mv0", [P, 2, 2])
        rs0 = sb("rs0", [P, 2, 2])
        x1 = x_nat
        stat1 = sb("stat1", [P, 2, 6])
        mv1 = sb("mv1", [P, 2, 2])
        rs1 = sb("rs1", [P, 2, 2])
        z1 = sb("z1", [P, GH, D])
        hn = sb("hn", [P, T])
        cen = h2 = hn
        tsum = sb("tsum", [P, 2, PS])
        tmean = sb("tmean", [P, 2, PS])
        sq = z1[:, :, :].rearrange("p g d -> p (g d)")
        tvar = sb("tvar", [P, 2, PS])
        trs = sb("trs", [P, 2, 2, PS])
        tscale = sb("tscale", [P, 2, PS])
        h2_hi = sb("h2_hi", [P, NH, T], F32R)
        h2_lo = sb("h2_lo", [P, NH, T], F32R)
        logit = sb("logit", [P, GH, E1])
        top = sb("top", [P, GH, 8])
        topi = sb("topi", [P, GH, 8], U32)
        topf = sb("topf", [P, GH, 8])
        dif = sb("dif", [P, GH])
        ratio = sb("ratio", [P, GH])
        wtop = sb("wtop", [P, 3, GH])
        eq1 = sb("eq1", [P, GH, E1])
        eq2 = sb("eq2", [P, GH, E1])
        combf = sb("combf", [P, GH, E1])
        comb4 = sb("comb4", [P, GH, P])
        part = sb("part", [P, GH, E1], BF16)
        comb3_t = sb("comb3_t", [96, NH, T], BF16)
        comb_t = sq
        sel8 = sb("sel8", [96, E1], BF16)
        gb = sb("gb", [P, 2, T])
        gated = sb("gated", [P, 2, T])
        acc = sb("acc", [P, NH, T])
        r1 = sb("r1", [P, NR, T])
        l2g = sb("l2g", [P, NG, A2 + 2])
        l2i_f = sb("l2i_f", [P, NG])
        l2i = sb("l2i", [P, NG], I32)
        l2b = sb("l2b", [P, NG])
        old = wi_all[:, :, :].rearrange("p e n -> p (e n)")
        old_wi = wi_sel0[:, :, :].rearrange("p j n -> p (j n)")
        old_wo = wo_sel0[:, :, :].rearrange("p j n -> p (j n)")

        def groups(ap):
            return ap.rearrange("p (g d) -> p g d", d=D)

        bd_h = groups(old[:, 0:2 * T])
        bd_w = groups(old[:, 2 * T:4 * T])
        x3 = groups(old[:, 4 * T:6 * T])
        tt = old[:, 6 * T:7 * T]
        zz = groups(old[:, 7 * T:8 * T])
        a_l3 = old_wi.rearrange("p (k t) -> p k t", k=4)
        a_sr2 = old_wo[:, 0:T]
        mats_l3 = old_wo[:, T:T + NMAT - MAT_EARLY]
        hb = sb("hb", [P, P])
        stat2 = sb("stat2", [P, GH, 6])
        mv2 = sb("mv2", [P, GH, 2])
        rs2 = sb("rs2", [P, 2, GH])
        ps = ctx.enter_context(nc.psum_tensor("ps", [P, 8, 512], F32))

        def bank_up(g):
            return ps[:, 3 * (g % 2) if g < GH else 0, :]

        def bank_tr(g):
            return ps[:, 1 + 3 * (g % 2) if g < GH else 1, :]

        def bank_sm(g):
            return ps[:, 2 + 3 * (g % 2) if g < GH else 2, :]

        def bank_z(q):
            return ps[:, 6 if q < 2 else 1, :]

        B0, B1, B2 = ps[:, 0, :], ps[:, 1, :], ps[:, 2, :]

        def bank_u(n):
            return ps[:, 3 + n % NU, :]

        D_BANK, GB_BANK = ps[:, 6, :], ps[:, 7, :]

        def mat(name, rows=P, first=0):
            a, b = MATS[name]
            if a >= MAT_EARLY:
                return mats_l3[:, a - MAT_EARLY:b - MAT_EARLY]
            return mats[first:first + rows, a:b]

        def col(c, rows=P):
            return cols[0:rows, c:c + 1]

        ld_idrow = sem("ld_idrow")
        ld_ids = sem("ld_ids")
        ld_mats = sem("ld_mats")
        ld_mats_l3 = sem("ld_mats_l3")
        ld_rows = sem("ld_rows")
        rows_spread = sem("rows_spread")
        ld_xt = sem("ld_xt")
        ld_xn = sem("ld_xn")
        ld_bcast = sem("ld_bcast")
        ld_wi = sem("ld_wi")
        ld_wip = sem("ld_wip")
        ld_wop = [sem("ld_wop_even"), sem("ld_wop_odd")]
        ld_raw = [sem(f"ld_raw{e}") for e in range(RAW)]
        ld_l2 = sem("ld_l2")
        st_out = sem("st_out")
        const_dve = sem("const_dve")
        const_pool = sem("const_pool")
        rows_split = sem("rows_split")
        oh_ready = sem("oh_ready")
        ohc_ready = sem("ohc_ready")
        cmask_ready = sem("cmask_ready")
        l2i_ready = sem("l2i_ready")
        bd_zero = sem("bd_zero")
        bd_ready = sem("bd_ready")
        sty_mm = sem("sty_mm")
        sty_ev = sem("sty_ev")
        sty_act = sem("sty_act")
        pick_dve = sem("pick_dve")
        pick_act = sem("pick_act")
        up0_done = sem("up0_done")
        gelu0_done = sem("gelu0_done")
        tr0_done = sem("tr0_done")
        h0t_done = sem("h0t_done")
        dn0_done = sem("dn0_done")
        var0_ready = sem("var0_ready")
        rs0_ready = sem("rs0_ready")
        x1_ready = sem("x1_ready")
        var1_ready = sem("var1_ready")
        rs1_ready = sem("rs1_ready")
        z1_ready = sem("z1_ready")
        zt_done = sem("zt_done")
        hn_ready = sem("hn_ready")
        cen_ready = sem("cen_ready")
        sq_ready = sem("sq_ready")
        tvar_ready = sem("tvar_ready")
        trs_ready = sem("trs_ready")
        h2_ready = sem("h2_ready")
        h2s_ready = sem("h2s_ready")
        route_mm = sem("route_mm")
        dif_ready = sem("dif_ready")
        ratio_ready = sem("ratio_ready")
        comb_ready = sem("comb_ready")
        combt_mm = sem("combt_mm")
        combt_ready = sem("combt_ready")
        acc_mm = sem("acc_mm")
        acc_ready = sem("acc_ready")
        w_hi = sem("w_hi")
        w_lo_pool = sem("w_lo_pool")
        w_lo_dve = sem("w_lo_dve")
        up1_done = sem("up1_done")
        relu_done = sem("relu_done")
        hi_dve = sem("hi_dve")
        hi_act = sem("hi_act")
        lo_dve = sem("lo_dve")
        lo_pool = sem("lo_pool")
        dn1_done = sem("dn1_done")
        gb_mm = sem("gb_mm")
        gb_ready = sem("gb_ready")
        gated_ready = sem("gated_ready")
        acc_done = sem("acc_done")
        dproj_mm = sem("dproj_mm")
        hb_ready = sem("hb_ready")
        exp_mm = sem("exp_mm")
        bdh_ready = sem("bdh_ready")
        up2_mm = sem("up2_mm")
        var2_ready = sem("var2_ready")
        rs2_ready = sem("rs2_ready")
        x3_ready = sem("x3_ready")
        x3t_mm = sem("x3t_mm")
        x3t_ready = sem("x3t_ready")
        l3a_mm = sem("l3a_mm")
        l3a_act = sem("l3a_act")
        l3a_mask = sem("l3a_mask")
        l3b_mm = sem("l3b_mm")
        l3b_act = sem("l3b_act")
        l3b_mask = sem("l3b_mask")
        l3o_mm = sem("l3o_mm")
        var3_ready = sem("var3_ready")
        rs3_ready = sem("rs3_ready")
        y_ready = sem("y_ready")
        dve_seq = sem("dve_seq")
        pool_seq = sem("pool_seq")
        act_seq = sem("act_seq")

        def wait_r1_used(eng, u):
            n, f = u // NF, u % NF
            if f == NF - 1:
                eng.wait_ge(lo_pool, 2 * n + 2)
            elif f % 2 == 0:
                eng.wait_ge(lo_dve, 2 * n + f // 2 + 1)
            else:
                eng.wait_ge(lo_pool, 2 * n + 1)

        def wait_hidden_free(eng, n):
            if n == 0:
                eng.wait_ge(w_hi, 2 * E1)
                eng.wait_ge(w_lo_pool, 3 * E1 // 2)
                eng.wait_ge(w_lo_dve, E1 // 2)
            if n == 1:
                eng.wait_ge(up0_done, GH)
                eng.wait_ge(dn0_done, GH)
            if n >= 2:
                eng.wait_ge(dn1_done, n - 1)

        def split_by_pool(e):
            return e + e // 2

        def load_raw(eng, e):
            eng.dma_start(w_raw_ring[:, e % RAW, :], in_w1[:, e, :]).then_inc(ld_raw[e % RAW], 16)

        block = ctx.enter_context(nc.Block())

        @block.sync
        def _(sp):
            sp.dma_start(ids_row[:], in_ids_row).then_inc(ld_idrow, 16)
            sp.dma_start(x_t[:, 0:T], in_x_t[:, 0:T]).then_inc(ld_xt, 16)
            sp.dma_start(wi_all[:], in_wi).then_inc(ld_wi, 16)
            sp.wait_ge(ld_idrow, 16)

            with sp.register("sp_expert") as reg:
                def fetch(g, src, dst, done):
                    for j in range(GRP):
                        b = GRP * g + j
                        sp.reg_load(reg, ids_row[0:1, b:b + 1])
                        e = sp.snap(reg, min_val=0, max_val=E0 - 1)
                        sp.dma_start(dst[:, j:j + 1, :], src[:, bass.ds(e, 1), :]).then_inc(done, 16)

                fetch(0, in_wo, wo_sel(0), ld_wop[0])
                sp.dma_start(x_nat[:], in_x_nat).then_inc(ld_xn, 16)
                fetch(1, in_wo, wo_sel(1), ld_wop[1])
                load_raw(sp, 0)
                load_raw(sp, 1)
                sp.wait_ge(dn0_done, 1)
                fetch(2, in_wo, wo_sel(2), ld_wop[0])
                load_raw(sp, 2)
                load_raw(sp, 3)
                sp.wait_ge(dn0_done, 2)
                fetch(3, in_wo, wo_sel(3), ld_wop[1])
                for e in range(RAW, E1):
                    sp.wait_ge(w_hi, 2 * (e - RAW + 1))
                    sp.wait_ge(w_lo_pool, split_by_pool(e - RAW + 1))
                    sp.wait_ge(w_lo_dve, (e - RAW) // 2 + 1)
                    load_raw(sp, e)
                sp.dma_start(x_t[:, T:2 * T], in_x_t[:, T:2 * T]).then_inc(ld_xt, 16)
                for g in range(GH, NG):
                    sp.wait_ge(up0_done, g)
                    fetch(g, in_wi, wi_sel(g), ld_wip)
                    sp.wait_ge(dn0_done, g)
                    fetch(g, in_wo, wo_sel(g), ld_wop[0])
            sp.wait_ge(dn0_done, NG)
            sp.dma_start(mats_l3, in_mats[:, MAT_EARLY:NMAT]).then_inc(ld_mats_l3, 16)
            sp.dma_start(bcast[:], in_bcast).then_inc(ld_bcast, 16)
            for c in range(NH):
                sp.wait_ge(y_ready, c + 1)
                sp.dma_start(out[:, c * GH:(c + 1) * GH, :], zz).then_inc(st_out, 16)
            sp.wait_ge(st_out, 16 * NH)

        @block.tensor
        def _(pe):
            ident = mat("ident")

            def style():
                pe.wait_ge(ld_mats, 16)
                pe.wait_ge(oh_ready, 1)
                pe.matmul(B0[0:64, 0:B], mat("subj", NSUBJ), ohs[:], start=True, stop=True).then_inc(sty_mm, 1)
                pe.wait_ge(sty_ev, 1)
                pe.matmul(B1[:, 0:B], mat("hyp_w1", 64), se_t[:], start=True, stop=True).then_inc(sty_mm, 1)
                pe.wait_ge(sty_ev, 2)
                pe.matmul(B0[:, 0:B], mat("hyp_w2"), hy1[:], start=True, stop=True).then_inc(sty_mm, 1)
                pe.wait_ge(sty_ev, 3)
                pe.matmul(B1[0:64, 0:B], mat("sty_w1"), hy2[:], start=True, stop=True).then_inc(sty_mm, 1)
                pe.wait_ge(sty_ev, 4)
                w = mat("sty_w2", 64)
                pe.matmul(B0[:, 0:B], w[:, 0:D], st1[:], start=True, stop=True).then_inc(sty_mm, 1)
                pe.matmul(B1[:, 0:B], w[:, D:2 * D], st1[:], start=True, stop=True).then_inc(sty_mm, 1)

            def l0_up(g):
                if g == 0:
                    pe.wait_ge(rows_spread, 48)
                    pe.wait_ge(oh_ready, 2)
                    pe.wait_ge(ld_xt, 16)
                    pe.wait_ge(sty_act, 2)
                if g == GH:
                    pe.wait_ge(ld_xt, 32)
                if g < GH:
                    pe.wait_ge(pick_dve, g + 1)
                    pe.wait_ge(pick_act, g + 1)
                else:
                    pe.wait_ge(ld_wip, 16 * GRP * (g - GH + 1))
                if g >= GH:
                    pe.wait_ge(gelu0_done, g)
                elif g >= 2:
                    pe.wait_ge(gelu0_done, g - 1)
                bank = bank_up(g)
                pe.matmul(bank, oh0[:, P * g:P * g + P], rows3[:, R_BI:R_BI + FF], start=True, stop=False,
                          skip_group_check=True)
                for j in range(GRP):
                    mm = pe.matmul(bank[S * j:S * j + S, :], x_t[:, P * g + S * j:P * g + S * j + S],
                                   wi_sel(g)[:, j, :], start=False, stop=True, skip_group_check=True)
                mm.then_inc(up0_done, 1)

            def l0_turn(g):
                pe.wait_ge(gelu0_done, g + 1)
                if g >= GH:
                    pe.wait_ge(h0t_done, g)
                    pe.wait_ge(combt_ready, 1)
                elif g >= 2:
                    pe.wait_ge(h0t_done, g - 1)
                for f in range(NF):
                    mm = pe.transpose(bank_tr(g)[:, P * f:P * f + P], h0[:, g % 2, P * f:P * f + P], ident)
                mm.then_inc(tr0_done, 1)

            def l0_down(g):
                pe.wait_ge(h0t_done, g + 1)
                if g >= GH:
                    pe.wait_ge(x1_ready, g)
                    pe.wait_ge(acc_ready, 1)
                elif g >= 2:
                    pe.wait_ge(x1_ready, g - 1)
                pe.wait_ge(ld_wop[g % 2 if g < GH else 0], 16 * GRP * (g // 2 + 1 if g < GH else g - GH + 3))
                bank = bank_sm(g)
                pe.matmul(bank[:, 0:3 * D], oh0[:, P * g:P * g + P], rows3[:, R_BO:R_BO + 3 * D], start=True,
                          stop=False, skip_group_check=True)
                for f in range(NF):
                    for j in range(GRP):
                        mm = pe.matmul(bank[S * j:S * j + S, 0:D],
                                       h0t[:, g % 2, P * f + S * j:P * f + S * j + S],
                                       wo_sel(g)[:, j, P * f:P * f + P], start=False,
                                       stop=f == NF - 1, skip_group_check=True)
                mm.then_inc(dn0_done, 1)

            def z_turn(q):
                pe.wait_ge(z1_ready, PG * (q + 1))
                for i in range(PG * (q % 2), PG * (q % 2) + PG):
                    mm = pe.transpose(bank_z(q)[:, P * i:P * i + P], z1[:, i, :], ident)
                mm.then_inc(zt_done, 1)

            def route(c):
                pe.wait_ge(h2_ready, 2 * c + 2)
                for i in range(GH):
                    mm = pe.matmul(B2[:, E1 * i:E1 * i + E1], h2[:, P * i:P * i + P], mat("router"),
                                   start=True, stop=True)
                mm.then_inc(route_mm, 1)

            def comb_turn(c):
                pe.wait_ge(comb_ready, c + 1)
                for i in range(GH):
                    mm = pe.transpose(B1[:, P * i:P * i + P], comb4[:, i, :], ident)
                mm.then_inc(combt_mm, 1)

            def acc_start(c):
                pe.wait_ge(combt_ready, c + 1)
                pe.matmul(B2, mat("exp_b2", E1, 96), comb_t[96:96 + E1, :], start=True, stop=False,
                          skip_group_check=True)
                for i in range(GH):
                    mm = pe.matmul(B2[:, P * i:P * i + P], x1[:, GH * c + i, :], ident, start=False, stop=True,
                                   skip_group_check=True)
                mm.then_inc(acc_mm, 1)

            def l1_up(n):
                c, e = n // E1, n % E1
                if c == 0:
                    pe.wait_ge(w_hi, 2 * (e + 1))
                    pe.wait_ge(w_lo_pool, split_by_pool(e) + 1)
                if e == 0:
                    pe.wait_ge(h2s_ready, 2 * c + 2)
                hi, lo = h2_hi[:, c, :], h2_lo[:, c, :]
                for f in range(NF):
                    u = NF * n + f
                    if u >= NU:
                        pe.wait_ge(relu_done, u - NU + 1)
                        if (u - NU) % NF == NF - 1:
                            pe.wait_ge(hi_act, (u - NU) // NF + 1)
                    whi, wlo = w1_hi[:, e, P * f:P * f + P], w1_lo[:, e, P * f:P * f + P]
                    pe.matmul(bank_u(u), whi, hi, start=True, stop=False)
                    pe.matmul(bank_u(u), whi, lo, start=False, stop=False)
                    pe.matmul(bank_u(u), wlo, hi, start=False, stop=True).then_inc(up1_done, 1)

            def l1_weight(n):
                c, e = n // E1, n % E1
                if n == 0:
                    pe.wait_ge(oh_ready, 2)
                if n:
                    pe.wait_ge(gb_ready, n)
                pe.matmul(GB_BANK, sel8[:, e:e + 1].broadcast_to([96, P]), comb3_t[:, c, :], start=True,
                          stop=True).then_inc(gb_mm, 1)

            def l1_down(n):
                e = n % E1
                if n < E1:
                    pe.wait_ge(w_lo_dve, e // 2 + 1)
                    pe.wait_ge(w_lo_pool, split_by_pool(e + 1))
                pe.wait_ge(hi_dve, 3 * (n + 1))
                pe.wait_ge(hi_act, n + 1)
                pe.wait_ge(lo_dve, 2 * (n + 1))
                pe.wait_ge(lo_pool, 2 * (n + 1))
                if n >= 1:
                    pe.wait_ge(gated_ready, n)
                for f in range(NF):
                    hi, lo = hid_hi[n % 2][:, f, :], hid_lo[n % 2][:, f, :]
                    whi, wlo = w2_hi[:, e, P * f:P * f + P], w2_lo[:, e, P * f:P * f + P]
                    pe.matmul(D_BANK, whi, hi, start=f == 0, stop=False)
                    pe.matmul(D_BANK, whi, lo, start=False, stop=False)
                    mm = pe.matmul(D_BANK, wlo, hi, start=False, stop=f == NF - 1)
                mm.then_inc(dn1_done, 1)

            def l2_down(c):
                pe.wait_ge(acc_done, E1 * (c + 1))
                xv = acc[:, c, :].rearrange("p (g j s) -> p g j s", g=GH, j=GRP)
                for j in range(GRP):
                    mm = pe.matmul(B2[A2 * j:A2 * j + A2, 0:P], mat("downT"), xv[:, :, j, :],
                                   start=True, stop=True, skip_group_check=True)
                mm.then_inc(dproj_mm, 1)

            def l2_expert(c):
                pe.wait_ge(hb_ready, c + 1)
                if c == 0:
                    pe.wait_ge(bd_ready, 1)
                for i in range(GH):
                    mm = pe.matmul(B1[:, S * i:S * i + S], bd_w[:, GH * c + i, :], hb[:, S * i:S * i + S],
                                   start=True, stop=True)
                mm.then_inc(exp_mm, 1)

            def l2_residual(c):
                for i in range(GH):
                    t = slice(P * i, P * i + P)
                    pe.matmul(B2[:, t], oh0[:, t], rows3[:, R_UB:R_UB + D], start=i == 0, stop=False,
                              skip_group_check=True)
                    pe.matmul(B2[:, t], acc[:, c, t], ident, start=False, stop=False, skip_group_check=True)

            def l2_up(c):
                pe.wait_ge(bdh_ready, c + 1)
                for i in range(GH):
                    mm = pe.matmul(B2[:, P * i:P * i + P], bd_h[:, GH * c + i, :], mat("upT"), start=False,
                                   stop=True, skip_group_check=True)
                mm.then_inc(up2_mm, 1)

            def x3_turn(c):
                pe.wait_ge(x3_ready, c + 1)
                for i in range(GH):
                    mm = pe.transpose(B1[:, P * i:P * i + P], x3[:, GH * c + i, :], ident)
                mm.then_inc(x3t_mm, 1)

            def l3_a(c, k):
                w = (mat("w1_nr"), mat("w1_tsr"), mat("w1_sr")[:, 0:P], mat("w1_sr")[:, P:2 * P])[3 - k]
                if k == 0:
                    pe.wait_ge(x3t_ready, c + 1)
                    pe.wait_ge(ld_mats_l3, 16)
                if k == 3:
                    pe.wait_ge(l3a_act, 4 * c + 1)
                pe.matmul((B0, B2, B1, B0)[k], w, tt, start=True, stop=True).then_inc(l3a_mm, 1)

            def l3_b(c):
                pe.wait_ge(l3a_act, 4 * c + 2)
                pe.matmul(B2, mat("w2_sr1"), a_l3[:, 0, :], start=True, stop=False)
                pe.matmul(B2, mat("w2_sr0"), a_l3[:, 1, :], start=False, stop=True).then_inc(l3b_mm, 1)

            def l3_out(c):
                pe.wait_ge(l3a_act, 4 * c + 4)
                if c == 0:
                    pe.wait_ge(ohc_ready, 1)
                for part_, buf, w, need in ((0, None, None, 0), (1, a_l3[:, 2, :], "w2_tsr", 1),
                                            (2, a_l3[:, 3, :], "w2_nr", 2), (3, a_sr2, "w3_sr", 0)):
                    if part_ in (1, 2):
                        pe.wait_ge(l3a_mask, 2 * c + need)
                    if part_ == 3:
                        pe.wait_ge(l3b_mask, c + 1)
                    for i in range(GH):
                        o = B0[:, P * i:P * i + P]
                        g = GH * c + i
                        if part_ == 0:
                            pe.matmul(o, ohc[:, P * g:P * g + P], rows3[:, R_B3:R_B3 + D], start=i == 0,
                                      stop=False, skip_group_check=True)
                        else:
                            mm = pe.matmul(o, buf[:, P * i:P * i + P], mat(w), start=False, stop=part_ == 3,
                                           skip_group_check=True)
                mm.then_inc(l3o_mm, 1)

            def side(k):
                if k in (0, 2, 4, 6):
                    l0_up(GH + k // 2)
                if k in (2, 4, 6, 8):
                    l0_down(GH + k // 2 - 1)
                if k in (1, 3, 5, 7):
                    l0_turn(GH + k // 2)
                if k == 8:
                    z_turn(2)
                if k == 10:
                    z_turn(3)
                if k == 12:
                    route(1)
                if k == 14:
                    comb_turn(1)
                if k == 15:
                    acc_start(1)
                if k == 18:
                    l2_down(0)
                if k == 19:
                    l2_expert(0)
                    l2_residual(0)
                if k == 20:
                    l2_up(0)
                if k == 23:
                    x3_turn(0)
                if k == 24:
                    l3_a(0, 0)
                    l3_a(0, 1)
                if k == 25:
                    l3_a(0, 2)
                    l3_a(0, 3)
                if k == 26:
                    l3_b(0)
                if k == 28:
                    l3_out(0)

            style()
            l0_up(0)
            l0_up(1)
            for g in range(GH):
                l0_turn(g)
                l0_down(g)
                if g + 2 < GH:
                    l0_up(g + 2)
                if g == GH - 1:
                    z_turn(0)
            z_turn(1)
            route(0)
            l1_up(0)
            comb_turn(0)
            acc_start(0)
            side(0)
            side(1)
            for n in range(1, NE):
                l1_up(n)
                l1_weight(n - 1)
                side(2 * n)
                l1_down(n - 1)
                side(2 * n + 1)
            l1_weight(NE - 1)
            l1_down(NE - 1)
            l2_down(1)
            l2_expert(1)
            l2_residual(1)
            l2_up(1)
            x3_turn(1)
            for k in range(4):
                l3_a(1, k)
            l3_b(1)
            l3_out(1)

        @block.scalar
        def _(act):
            seq = [0]

            def link(ins):
                seq[0] += 1
                ins.then_inc(act_seq, 1)
                act.wait_ge(act_seq, seq[0])

            def style():
                act.wait_ge(ld_ids, 48)
                act.wait_ge(sty_mm, 1)
                nc.scalar.copy(se_t[:], B0[0:64, 0:B]).then_inc(sty_ev, 1)
                act.wait_ge(sty_mm, 2)
                nc.scalar.activation(hy1[:], B1[:, 0:B], ACT.Relu, bias=col(C_HB1)).then_inc(sty_ev, 1)
                act.wait_ge(sty_mm, 3)
                nc.scalar.activation(hy2[:], B0[:, 0:B], ACT.Identity, bias=col(C_HB2)).then_inc(sty_ev, 1)
                act.wait_ge(sty_mm, 4)
                nc.scalar.activation(st1[:], B1[0:64, 0:B], ACT.Relu, bias=col(C_SB1, 64)).then_inc(sty_ev, 1)
                act.wait_ge(sty_mm, 6)
                link(nc.scalar.activation(gam_raw[:], B0[:, 0:B], ACT.Identity, bias=col(C_SB2G)))
                nc.scalar.activation(bet_s[:], B1[:, 0:B], ACT.Identity, bias=col(C_SB2B)).then_inc(sty_act, 1)
                link(nc.scalar.activation(gam_abs[:], gam_raw[:], ACT.Abs))
                link(nc.scalar.activation(gam_exp[:], gam_abs[:], ACT.Exp, scale=-1.0))
                nc.scalar.activation(gam_log[:], gam_exp[:], ACT.Ln, bias=1.0).then_inc(sty_act, 1)

            def gelu0(g):
                act.wait_ge(up0_done, g + 1)
                if g >= 2:
                    act.wait_ge(tr0_done, g - 1)
                nc.scalar.activation(h0[:, g % 2, :], bank_up(g), ACT.Gelu).then_inc(gelu0_done, 1)

            def hidden_t(g):
                act.wait_ge(tr0_done, g + 1)
                if g >= 2:
                    act.wait_ge(dn0_done, g - 1)
                nc.scalar.copy(h0t[:, g % 2, :], bank_tr(g)).then_inc(h0t_done, 1)

            def pick_wi(g):
                if g >= 2:
                    act.wait_ge(up0_done, g - 1)
                if g == 0:
                    act.wait_ge(ld_idrow, 16)
                    act.wait_ge(ld_wi, 16)
                for j in (2, 3):
                    b = GRP * g + j
                    act.reg_load(reg, ids_row[0:1, b:b + 1])
                    e = act.snap(reg, min_val=0, max_val=E0 - 1)
                    ins = nc.scalar.copy(wi_sel(g)[:, j:j + 1, :], wi_all[:, bass.ds(e, 1), :])
                ins.then_inc(pick_act, 1)

            def split_hi(e):
                act.wait_ge(ld_raw[e % RAW], 16 * (e // RAW + 1))
                nc.scalar.copy(w1_hi[:, e, :], w_raw(e, 0)).then_inc(w_hi, 1)
                nc.scalar.copy(w2_hi[:, e, :], w_raw(e, 1)).then_inc(w_hi, 1)

            def ln_affine(q):
                act.wait_ge(zt_done, q + 1)
                if q >= 2:
                    act.wait_ge(route_mm, 1)
                    act.wait_ge(h2s_ready, 2)
                t = slice(PT * (q % 2), PT * (q % 2) + PT)
                nc.scalar.activation(hn[:, t], bank_z(q)[:, t], ACT.Identity, bias=col(C_LNB),
                                     scale=col(C_LNG)).then_inc(hn_ready, 1)

            def square(q):
                act.wait_ge(cen_ready, q + 1)
                if q >= 2:
                    act.wait_ge(acc_mm, 1)
                t = slice(PT * (q % 2), PT * (q % 2) + PT)
                nc.scalar.activation(sq[:, t], cen[:, t], ACT.Square).then_inc(sq_ready, 1)

            def acc_copy(c):
                act.wait_ge(acc_mm, c + 1)
                nc.scalar.copy(acc[:, c, :], B2).then_inc(acc_ready, 1)

            def relu(n):
                e = n % E1
                for f in range(NF):
                    u = NF * n + f
                    act.wait_ge(up1_done, u + 1)
                    if u >= NR:
                        wait_r1_used(act, u - NR)
                    c = C_EB1 + NF * e + f
                    nc.scalar.activation(r1[:, u % NR, :], bank_u(u), ACT.Relu, bias=col(c)).then_inc(relu_done, 1)
                wait_hidden_free(act, n)
                nc.scalar.activation(hid_hi[n % 2][:, NF - 1, :], bank_u(u), ACT.Relu, bias=col(c)).then_inc(hi_act, 1)

            def weight_copy(n):
                act.wait_ge(gb_mm, n + 1)
                if n >= 2:
                    act.wait_ge(gated_ready, n - 1)
                nc.scalar.copy(gb[:, n % 2, :], GB_BANK).then_inc(gb_ready, 1)

            def l2_gelu(c):
                act.wait_ge(dproj_mm, c + 1)
                if c:
                    act.wait_ge(exp_mm, c)
                nc.scalar.activation(hb[:], B2[:, 0:P], ACT.Gelu, bias=col(C_DB)).then_inc(hb_ready, 1)

            def x3t_copy(c):
                act.wait_ge(x3t_mm, c + 1)
                if c:
                    act.wait_ge(l3a_mm, 4 * c)
                nc.scalar.copy(tt, B1).then_inc(x3t_ready, 1)

            def l3_gelu(c, k):
                act.wait_ge(l3a_mm, 4 * c + k + 1)
                if c and k == 0:
                    act.wait_ge(l3o_mm, c)
                    act.wait_ge(l3b_mm, c)
                nc.scalar.activation(a_l3[:, k, :], (B0, B2, B1, B0)[k], ACT.Gelu,
                                     bias=col((C_B1NR, C_B1TSR, C_B1SR0, C_B1SR1)[3 - k])).then_inc(l3a_act, 1)

            def l3_gelu2(c):
                act.wait_ge(l3b_mm, c + 1)
                nc.scalar.activation(a_sr2, B2, ACT.Gelu, bias=col(C_B2SR)).then_inc(l3b_act, 1)

            def side(k):
                if k in (0, 2, 4, 6):
                    gelu0(GH + k // 2)
                if k in (1, 3, 5, 7):
                    hidden_t(GH + k // 2)
                if k in (8, 10):
                    ln_affine(k // 2 - 2)
                    square(k // 2 - 2)
                if k == 15:
                    acc_copy(1)
                if k == 18:
                    l2_gelu(0)
                if k == 23:
                    x3t_copy(0)
                if k == 24:
                    l3_gelu(0, 0)
                    l3_gelu(0, 1)
                if k == 25:
                    l3_gelu(0, 2)
                    l3_gelu(0, 3)
                if k == 26:
                    l3_gelu2(0)

            act.dma_start(rows_p[:], in_rows).then_inc(ld_rows, 16)
            act.dma_start(mats[:, 0:MAT_EARLY], in_mats[:, 0:MAT_EARLY]).then_inc(ld_mats, 16)
            act.wait_ge(rows_split, 1)
            act.wait_ge(const_dve, 1)
            for q in range(3):
                act.dma_start(rows3[32 * q:32 * q + 8, :], rows_q[:, q, :]).then_inc(rows_spread, 16)
            with act.register("act_expert") as reg:
                pick_wi(0)
                style()
                pick_wi(1)
                gelu0(0)
                hidden_t(0)
                for g in range(1, GH):
                    if g + 1 < GH:
                        pick_wi(g + 1)
                    gelu0(g)
                    hidden_t(g)
                    split_hi(g - 1)
            ln_affine(0)
            square(0)
            split_hi(3)
            ln_affine(1)
            square(1)
            for e in range(RAW, E1):
                split_hi(e)
            relu(0)
            acc_copy(0)
            side(0)
            side(1)
            for n in range(1, NE):
                relu(n)
                weight_copy(n - 1)
                side(2 * n)
                side(2 * n + 1)
            weight_copy(NE - 1)
            l2_gelu(1)
            x3t_copy(1)
            for k in range(4):
                l3_gelu(1, k)
            l3_gelu2(1)

        @block.vector
        def _(dve):
            V = nc.vector
            seq = [0]

            def link(ins):
                seq[0] += 1
                ins.then_inc(dve_seq, 1)
                dve.wait_ge(dve_seq, seq[0])

            def by_seq(ap, n):
                return ap.unsqueeze(2).broadcast_to([ap.shape[0], n, S])

            def tables():
                V.memset(euler[:], EULER)
                V.memset(half_exp[:], HALF_EXP)
                V.memset(rows3[:], 0.0).then_inc(const_dve, 1)
                dve.wait_ge(ld_rows, 16)
                link(V.tensor_copy(rows_q[:, 0, :], rows_p[:]))
                link(V.tensor_tensor(rows_p[:], rows_p[:], rows_q[:, 0, :], ALU.subtract))
                link(V.tensor_copy(rows_q[:, 1, :], rows_p[:]))
                V.tensor_tensor(rows_q[:, 2, :], rows_p[:], rows_q[:, 1, :], ALU.subtract).then_inc(rows_split, 1)
                dve.wait_ge(ld_ids, 48)
                link(V.tensor_copy(ids_f[:], ids_all[:]))
                V.tensor_scalar(ohs[:], ids_f[0:NSUBJ, 1, :], col(C_P32, NSUBJ), None, ALU.is_equal).then_inc(oh_ready, 1)
                link(V.tensor_scalar(l2i_f[:], ids_j[:], -1.0, 16.0, ALU.max, ALU.min))
                link(V.tensor_scalar(l2i_f[:], l2i_f[:], 1.0, float(A2), ALU.add, ALU.mult))
                V.tensor_scalar(l2i[:], l2i_f[:], col(C_P32), None, ALU.add).then_inc(l2i_ready, 1)
                V.tensor_scalar(oh0[:].rearrange("p (b s) -> p b s", s=S), by_seq(ids_f[0:96, 0, :], B),
                                col(C_P32, 96), None, ALU.is_equal)
                dve.wait_ge(const_pool, 1)
                V.tensor_scalar(sel8[:], iota8[0:96, :], col(C_P32, 96), None, ALU.is_equal).then_inc(oh_ready, 1)
                for k in range(NCOND):
                    V.tensor_scalar(cmask[:, k, :], ids_f[:, 3, :], float(k), None, ALU.is_equal).then_inc(cmask_ready, 1)

            def style():
                dve.wait_ge(sty_act, 2)
                link(V.scalar_tensor_tensor(gam_s[:], gam_raw[:], 0.0, gam_log[:], ALU.max, ALU.add))
                link(V.tensor_scalar(gam_s[:], gam_s[:], 1e-8, None, ALU.add))

            def cond_rows():
                dve.wait_ge(up0_done, NG)
                V.tensor_scalar(ohc.rearrange("p (b s) -> p b s", s=S), by_seq(ids_f[0:96, 3, :], B),
                                col(C_P32, 96), None, ALU.is_equal).then_inc(ohc_ready, 1)

            def l2_tables():
                dve.wait_ge(ld_l2, 16 * NG)
                dve.wait_ge(bd_zero, 2)
                for j in range(GRP):
                    rows = slice(A2 * j, A2 * j + A2)
                    V.tensor_copy(bd_w[rows, :, A2 * j:A2 * j + A2], l2g[rows, :, 0:A2])
                V.tensor_tensor(l2b[:], l2g[:, :, A2], l2g[:, :, A2 + 1], ALU.add).then_inc(bd_ready, 1)

            def pick_wi(g):
                if g >= 2:
                    dve.wait_ge(up0_done, g - 1)
                if g == 0:
                    dve.wait_ge(ld_idrow, 16)
                    dve.wait_ge(ld_wi, 16)
                for j in (0, 1):
                    b = GRP * g + j
                    dve.reg_load(reg, ids_row[0:1, b:b + 1])
                    e = dve.snap(reg, min_val=0, max_val=E0 - 1)
                    ins = V.tensor_copy(wi_sel(g)[:, j:j + 1, :], wi_all[:, bass.ds(e, 1), :])
                ins.then_inc(pick_dve, 1)

            def l0_sum(g):
                dve.wait_ge(dn0_done, g + 1)
                if g == 0:
                    dve.wait_ge(ld_xn, 16)
                i = g % 2
                link(V.tensor_tensor(res0[:, i, :], bank_sm(g)[:, 0:D], x_nat[:, g, :], ALU.add))
                link(V.bn_stats(stat0[:, i, :], res0[:, i, :]))
                if g >= 2:
                    dve.wait_ge(rs0_ready, g - 1)
                V.bn_aggr(mv0[:, i, :], stat0[:, i, :]).then_inc(var0_ready, 1)

            def l0_norm(g):
                i = g % 2
                dve.wait_ge(rs0_ready, g + 1)
                link(V.tensor_scalar(y0[:, i, :], res0[:, i, :], mv0[:, i, 0:1], rs0[:, i, 1:2], ALU.subtract, ALU.mult))
                link(V.tensor_tensor(y0[:, i, :], y0[:, i, :], bank_sm(g)[:, D:2 * D], ALU.mult))
                V.tensor_tensor(x1[:, g, :], y0[:, i, :], bank_sm(g)[:, 2 * D:3 * D], ALU.add).then_inc(x1_ready, 1)
                dve.wait_ge(x1_ready, g + 1)
                link(V.bn_stats(stat1[:, i, :], x1[:, g, :]))
                if g >= 2:
                    dve.wait_ge(rs1_ready, g - 1)
                V.bn_aggr(mv1[:, i, :], stat1[:, i, :]).then_inc(var1_ready, 1)

            def l1_ln(g):
                i = g % 2
                dve.wait_ge(rs1_ready, g + 1)
                if g == GH:
                    dve.wait_ge(acc_mm, 1)
                V.tensor_scalar(z1[:, g % GH, :], x1[:, g, :], mv1[:, i, 0:1], rs1[:, i, 1:2], ALU.subtract,
                                ALU.mult).then_inc(z1_ready, 1)

            def split_lo(e):
                dve.wait_ge(w_hi, 2 * e + 2)
                V.tensor_tensor(w2_lo[:, e, :], w_raw(e, 1), w2_hi[:, e, :].bitcast(F32),
                                ALU.subtract).then_inc(w_lo_dve, 1)

            def time_norm_a(q):
                i = q % 2
                hv = hn[:, PT * i:PT * i + PT].rearrange("p (b s) -> p b s", s=S)
                dve.wait_ge(hn_ready, q + 1)
                link(V.tensor_reduce(tsum[:, i, :], hv, AX.X, ALU.add))
                link(V.tensor_scalar(tmean[:, i, :], tsum[:, i, :], 1.0 / S, None, ALU.mult))
                V.tensor_tensor(hv, hv, by_seq(tmean[:, i, :], PS), ALU.subtract).then_inc(cen_ready, 1)

            def time_norm_b(q):
                i = q % 2
                dve.wait_ge(sq_ready, q + 1)
                V.tensor_reduce(tvar[:, i, :], sq[:, PT * i:PT * i + PT].rearrange("p (b s) -> p b s", s=S), AX.X,
                                ALU.add).then_inc(tvar_ready, 1)

            def time_norm_c(q):
                i, c = q % 2, q // 2
                t = slice(PT * i, PT * i + PT)
                dve.wait_ge(trs_ready, q + 1)
                seqs = slice(PS * q, PS * q + PS)
                h2v = h2[:, t].rearrange("p (b s) -> p b s", s=S)
                link(V.tensor_tensor(tscale[:, i, :], trs[:, i, 1, :], gam_s[:, seqs], ALU.mult))
                link(V.tensor_tensor(h2v, h2v, by_seq(tscale[:, i, :], PS), ALU.mult))
                V.tensor_tensor(h2v, h2v, by_seq(bet_s[:, seqs], PS), ALU.add).then_inc(h2_ready, 1)
                dve.wait_ge(h2_ready, q + 1)
                link(V.tensor_copy(h2_hi[:, c, t], h2[:, t]))
                V.tensor_tensor(h2_lo[:, c, t], h2[:, t], h2_hi[:, c, t].bitcast(F32), ALU.subtract).then_inc(h2s_ready, 1)

            def top2(c):
                dve.wait_ge(route_mm, c + 1)
                link(V.tensor_copy(logit[:], B2[:, 0:GH * E1].rearrange("p (g e) -> p g e", e=E1)))
                for i in range(GH):
                    ins = V.max(top[:, i, :], logit[:, i, :])
                link(ins)
                V.tensor_tensor(dif[:], top[:, :, 1], top[:, :, 0], ALU.subtract).then_inc(dif_ready, 1)
                for i in range(GH):
                    ins = V.max_index(topi[:, i, :], top[:, i, :], logit[:, i, :])
                link(ins)
                link(V.tensor_copy(topf[:], topi[:]))
                ids = iota8[:].unsqueeze(1).broadcast_to([P, GH, E1])
                V.tensor_tensor(eq1[:], ids, topf[:, :, 0:1].broadcast_to([P, GH, E1]), ALU.is_equal)
                link(V.tensor_tensor(eq2[:], ids, topf[:, :, 1:2].broadcast_to([P, GH, E1]), ALU.is_equal))

            def combine(c):
                dve.wait_ge(ratio_ready, c + 1)

                def wide(ap):
                    return ap.unsqueeze(2).broadcast_to([P, GH, E1])

                link(V.tensor_scalar(wtop[:, 0, :], ratio[:], 1.0, None, ALU.add))
                link(V.reciprocal(wtop[:, 1, :], wtop[:, 0, :]))
                link(V.tensor_tensor(wtop[:, 2, :], wtop[:, 1, :], ratio[:], ALU.mult))
                V.tensor_tensor(eq1[:], eq1[:], wide(wtop[:, 1, :]), ALU.mult)
                link(V.tensor_tensor(eq2[:], eq2[:], wide(wtop[:, 2, :]), ALU.mult))
                link(V.tensor_tensor(combf[:], eq1[:], eq2[:], ALU.add))
                if c:
                    dve.wait_ge(combt_mm, c)
                else:
                    dve.wait_ge(const_pool, 2)
                V.tensor_copy(comb4[:, :, 96:96 + E1], combf[:])
                link(V.tensor_copy(part[:], combf[:]))
                V.tensor_copy(comb4[:, :, 0:E1], part[:])
                link(V.tensor_tensor(combf[:], combf[:], part[:], ALU.subtract))
                link(V.tensor_copy(part[:], combf[:]))
                V.tensor_copy(comb4[:, :, 32:32 + E1], part[:])
                V.tensor_tensor(comb4[:, :, 64:64 + E1], combf[:], part[:], ALU.subtract).then_inc(comb_ready, 1)

            def comb_copy(c):
                dve.wait_ge(combt_mm, c + 1)
                if c:
                    dve.wait_ge(acc_mm, c)
                V.tensor_copy(comb3_t[:, c, :], B1[0:96, :])
                V.tensor_copy(comb_t[96:P, :], B1[96:P, :]).then_inc(combt_ready, 1)

            def hid_split(n):
                wait_hidden_free(dve, n)
                for f in range(NF - 1):
                    u = NF * n + f
                    dve.wait_ge(relu_done, u + 1)
                    V.tensor_copy(hid_hi[n % 2][:, f, :], r1[:, u % NR, :]).then_inc(hi_dve, 1)
                    if f % 2 == 0:
                        dve.wait_ge(hi_dve, 3 * n + f + 1)
                        V.tensor_tensor(hid_lo[n % 2][:, f, :], r1[:, u % NR, :],
                                        hid_hi[n % 2][:, f, :].bitcast(F32), ALU.subtract).then_inc(lo_dve, 1)

            def gate(n):
                dve.wait_ge(dn1_done, n + 1)
                dve.wait_ge(gb_ready, n + 1)
                if n >= 2:
                    dve.wait_ge(acc_done, n - 1)
                V.tensor_tensor(gated[:, n % 2, :], D_BANK, gb[:, n % 2, :], ALU.mult).then_inc(gated_ready, 1)

            def l2_block(c):
                dve.wait_ge(exp_mm, c + 1)
                gs = slice(GH * c, GH * c + GH)
                for j in range(GRP):
                    rows = slice(A2 * j, A2 * j + A2)
                    ins = V.tensor_tensor(bd_h[rows, gs, S * j:S * j + S],
                                          B1[rows, 0:P].rearrange("p (g s) -> p g s", s=S),
                                          by_seq(l2b[rows, gs], GH), ALU.add)
                ins.then_inc(bdh_ready, 1)

            def norm_stats(src, ready):
                for i in range(GH):
                    ins = V.bn_stats(stat2[:, i, :], src[:, i, :])
                link(ins)
                for i in range(GH):
                    ins = V.bn_aggr(mv2[:, i, :], stat2[:, i, :])
                ins.then_inc(ready, 1)

            def norm_apply(src, dst, gamma, beta, ready):
                for i in range(GH):
                    ins = V.tensor_scalar(zz[:, i, :], src[:, i, :], mv2[:, i, 0:1], rs2[:, 1, i:i + 1],
                                          ALU.subtract, ALU.mult)
                link(ins)
                link(V.tensor_tensor(zz, zz, gamma.unsqueeze(1).broadcast_to([P, GH, D]), ALU.mult))
                V.tensor_tensor(dst, zz, beta.unsqueeze(1).broadcast_to([P, GH, D]), ALU.add).then_inc(ready, 1)

            def l2_sum(c):
                dve.wait_ge(up2_mm, c + 1)
                norm_stats(groups(B2), var2_ready)

            def l2_norm(c):
                dve.wait_ge(rs2_ready, c + 1)
                dve.wait_ge(ld_bcast, 16)
                if c:
                    dve.wait_ge(st_out, 16 * c)
                norm_apply(groups(B2), x3[:, GH * c:GH * c + GH, :], bcast[:, 0, :], bcast[:, 1, :], x3_ready)

            def mask(c, k, act_sem, need, buf, ready):
                dve.wait_ge(act_sem, need)
                v = buf.rearrange("p (b s) -> p b s", s=S)
                V.tensor_tensor(v, v, by_seq(cmask[:, k, BH * c:BH * c + BH], BH), ALU.mult).then_inc(ready, 1)

            def l3_sum(c):
                dve.wait_ge(l3o_mm, c + 1)
                dve.wait_ge(x3_ready, c + 1)
                y = x3[:, GH * c:GH * c + GH, :]
                link(V.tensor_tensor(y, groups(B0), y, ALU.add))
                norm_stats(y, var3_ready)

            def l3_norm(c):
                dve.wait_ge(rs3_ready, c + 1)
                norm_apply(x3[:, GH * c:GH * c + GH, :], zz, bcast[:, 2, :], bcast[:, 3, :], y_ready)

            def side(k):
                if k in (2, 4, 6, 8):
                    l0_sum(GH + k // 2 - 1)
                if k in (3, 5, 7, 9):
                    l0_norm(GH + k // 2 - 1)
                if k in (4, 6, 8, 10):
                    l1_ln(GH + k // 2 - 2)
                if k == 8:
                    time_norm_a(2)
                    cond_rows()
                if k == 9:
                    time_norm_b(2)
                if k == 10:
                    time_norm_a(3)
                    time_norm_c(2)
                if k == 11:
                    time_norm_b(3)
                    time_norm_c(3)
                if k == 12:
                    top2(1)
                if k == 13:
                    combine(1)
                    l2_tables()
                if k == 14:
                    comb_copy(1)
                if k == 19:
                    l2_block(0)
                if k == 20:
                    l2_sum(0)
                if k == 21:
                    l2_norm(0)
                if k == 25:
                    mask(0, 1, l3a_act, 3, a_l3[:, 2, :], l3a_mask)
                    mask(0, 0, l3a_act, 4, a_l3[:, 3, :], l3a_mask)
                if k == 27:
                    mask(0, 2, l3b_act, 1, a_sr2, l3b_mask)
                if k == 28:
                    l3_sum(0)
                if k == 29:
                    l3_norm(0)

            with dve.register("dve_expert") as reg:
                tables()
                pick_wi(0)
                style()
                pick_wi(1)
                for g in range(GH):
                    if g + 2 < GH:
                        pick_wi(g + 2)
                    l0_sum(g)
                    if g >= 1:
                        l0_norm(g - 1)
                    if g >= 2:
                        l1_ln(g - 2)
            split_lo(0)
            l0_norm(GH - 1)
            time_norm_a(0)
            l1_ln(GH - 2)
            l1_ln(GH - 1)
            time_norm_b(0)
            split_lo(2)
            time_norm_a(1)
            time_norm_b(1)
            time_norm_c(0)
            time_norm_c(1)
            split_lo(4)
            split_lo(6)
            hid_split(0)
            top2(0)
            combine(0)
            comb_copy(0)
            for n in range(1, NE):
                hid_split(n)
                side(2 * n)
                gate(n - 1)
                side(2 * n + 1)
            gate(NE - 1)
            l2_block(1)
            l2_sum(1)
            l2_norm(1)
            mask(1, 1, l3a_act, 7, a_l3[:, 2, :], l3a_mask)
            mask(1, 0, l3a_act, 8, a_l3[:, 3, :], l3a_mask)
            mask(1, 2, l3b_act, 2, a_sr2, l3b_mask)
            l3_sum(1)
            l3_norm(1)

        @block.gpsimd
        def _(pool):
            G = nc.gpsimd
            seq = [0]

            def link(ins):
                seq[0] += 1
                ins.then_inc(pool_seq, 1)
                pool.wait_ge(pool_seq, seq[0])

            def inv_sqrt(src, tmp, dst, scale, eps, ready):
                link(G.tensor_scalar(tmp, src, scale, eps, ALU.mult, ALU.add))
                G.tensor_tensor(dst, tmp, half_exp[:, 0:tmp.shape[-1]], ALU.pow).then_inc(ready, 1)

            def rs_l0(g):
                i = g % 2
                pool.wait_ge(var0_ready, g + 1)
                inv_sqrt(mv0[:, i, 1:2], rs0[:, i, 0:1], rs0[:, i, 1:2], 1.0, 1e-12, rs0_ready)

            def rs_l1(g):
                i = g % 2
                pool.wait_ge(var1_ready, g + 1)
                inv_sqrt(mv1[:, i, 1:2], rs1[:, i, 0:1], rs1[:, i, 1:2], 1.0, 1e-5, rs1_ready)

            def rs_time(q):
                i = q % 2
                pool.wait_ge(tvar_ready, q + 1)
                inv_sqrt(tvar[:, i, :], trs[:, i, 0, :], trs[:, i, 1, :], 1.0 / S, 1e-8, trs_ready)

            def exp_dif(c):
                pool.wait_ge(dif_ready, c + 1)
                G.tensor_tensor(ratio[:], euler[:], dif[:], ALU.pow).then_inc(ratio_ready, 1)

            def split_w1(e):
                pool.wait_ge(w_hi, 2 * e + 1)
                G.tensor_tensor(w1_lo[:, e, :], w_raw(e, 0), w1_hi[:, e, :].bitcast(F32),
                                ALU.subtract).then_inc(w_lo_pool, 1)

            def split_w2(e):
                pool.wait_ge(w_hi, 2 * e + 2)
                G.tensor_tensor(w2_lo[:, e, :], w_raw(e, 1), w2_hi[:, e, :].bitcast(F32),
                                ALU.subtract).then_inc(w_lo_pool, 1)

            def hid_lo_half(n):
                wait_hidden_free(pool, n)
                for f in (1, 3):
                    u = NF * n + f
                    if f == 1:
                        pool.wait_ge(hi_dve, 3 * n + 2)
                    else:
                        pool.wait_ge(hi_act, n + 1)
                    G.tensor_tensor(hid_lo[n % 2][:, f, :], r1[:, u % NR, :],
                                    hid_hi[n % 2][:, f, :].bitcast(F32), ALU.subtract).then_inc(lo_pool, 1)

            def add_gated(n):
                c = n // E1
                pool.wait_ge(gated_ready, n + 1)
                pool.wait_ge(acc_ready, c + 1)
                if n:
                    pool.wait_ge(acc_done, n)
                G.tensor_tensor(acc[:, c, :], acc[:, c, :], gated[:, n % 2, :], ALU.add).then_inc(acc_done, 1)

            def rs_l2(c):
                pool.wait_ge(var2_ready, c + 1)
                if c:
                    pool.wait_ge(y_ready, c)
                inv_sqrt(mv2[:, :, 1], rs2[:, 0, :], rs2[:, 1, :], 1.0, 1e-5, rs2_ready)

            def rs_l3(c):
                pool.wait_ge(var3_ready, c + 1)
                inv_sqrt(mv2[:, :, 1], rs2[:, 0, :], rs2[:, 1, :], 1.0, 1e-5, rs3_ready)

            def side(k):
                if k in (2, 4, 6, 8):
                    rs_l0(GH + k // 2 - 1)
                if k in (3, 5, 7, 9):
                    rs_l1(GH + k // 2 - 1)
                if k == 9:
                    pool.wait_ge(dn0_done, NG)
                    G.memset(bd_h, 0.0).then_inc(bd_zero, 1)
                    G.memset(bd_w, 0.0).then_inc(bd_zero, 1)
                if k in (9, 11):
                    rs_time((k - 5) // 2)
                if k == 12:
                    exp_dif(1)
                if k == 20:
                    rs_l2(0)
                if k == 28:
                    rs_l3(0)

            pool.dma_start(cols[:], in_cols).then_inc(ld_ids, 16)
            pool.dma_start(ids_all[:], in_ids_all).then_inc(ld_ids, 16)
            pool.dma_start(ids_j[:], in_ids_j).then_inc(ld_ids, 16)
            G.iota(iota8[:], pattern=[[1, E1]], base=0, channel_multiplier=0).then_inc(const_pool, 1)
            G.memset(comb4[:], 0.0).then_inc(const_pool, 1)
            pool.wait_ge(l2i_ready, 1)
            for g in range(NG):
                G.indirect_dma_start(l2g[:, g, :], None, in_l2tab,
                                     bass.IndirectOffsetOnAxis(ap=l2i[:, g:g + 1], axis=0)).then_inc(ld_l2, 16)
            pool.wait_ge(const_dve, 1)
            rs_l0(0)
            rs_l0(1)
            rs_l1(0)
            split_w1(0)
            rs_l0(2)
            rs_l1(1)
            split_w1(1)
            rs_l0(3)
            rs_l1(2)
            rs_l1(3)
            split_w2(1)
            rs_time(0)
            split_w1(2)
            rs_time(1)
            split_w1(3)
            split_w2(3)
            for e in range(RAW, E1):
                split_w1(e)
                if e % 2:
                    split_w2(e)
            hid_lo_half(0)
            exp_dif(0)
            for n in range(1, NE):
                hid_lo_half(n)
                side(2 * n)
                add_gated(n - 1)
                side(2 * n + 1)
            add_gated(NE - 1)
            rs_l2(1)
            rs_l3(1)


def lay_out(i, np):
    f4 = np.float32
    x = np.asarray(i["x"])
    ids = [np.asarray(i[k]).astype(np.int32, copy=False) for k in ("itok_B_0_7", "itok_B_6_14", "itok_B_0_15", "itok_B_0_2")]
    cols = np.zeros((P, NCOL), f4)

    def put(c, v):
        cols[:v.shape[0], c] = v

    put(C_LNG, i["L1_cond_ln_g"])
    put(C_LNB, i["L1_cond_ln_b"])
    put(C_HB1, i["L1_cond_hyp_b1"])
    put(C_HB2, i["L1_cond_hyp_b2"])
    put(C_SB1, i["L1_cond_sty_b1"])
    put(C_SB2G, i["L1_cond_sty_b2"][:D])
    put(C_SB2B, i["L1_cond_sty_b2"][D:])
    put(C_B1NR, i["L3_cond_b1_nr"])
    put(C_B1TSR, i["L3_cond_b1_tsr"])
    put(C_B1SR0, i["L3_cond_b1_sr"][:P])
    put(C_B1SR1, i["L3_cond_b1_sr"][P:])
    put(C_B2SR, i["L3_cond_b2_sr"])
    put(C_DB, np.tile(i["L2_cond_down_b"], GRP))
    put(C_P32, np.tile(np.arange(32, dtype=f4), 4))
    cols[:, C_EB1:] = i["L1_cond_exp_b1"].reshape(E1 * NF, P).T
    mats = np.zeros((P, NMAT), f4)
    parts = dict(hyp_w1=i["L1_cond_hyp_w1"], hyp_w2=i["L1_cond_hyp_w2"], sty_w1=i["L1_cond_sty_w1"],
                 sty_w2=i["L1_cond_sty_w2"], subj=i["L1_cond_subj_emb"], router=i["L1_cond_router_w"],
                 ident=np.eye(P, dtype=f4), downT=i["L2_cond_down_W"].T,
                 upT=np.tile(i["L2_cond_up_W"].T, (GRP, 1)), exp_b2=i["L1_cond_exp_b2"],
                 w1_nr=i["L3_cond_w1_nr"], w1_tsr=i["L3_cond_w1_tsr"], w1_sr=i["L3_cond_w1_sr"],
                 w2_sr0=i["L3_cond_w2_sr"][:P], w2_sr1=i["L3_cond_w2_sr"][P:], w2_nr=i["L3_cond_w2_nr"],
                 w2_tsr=i["L3_cond_w2_tsr"], w3_sr=i["L3_cond_w3_sr"])
    for name, m in parts.items():
        a, b = MATS[name]
        r = 96 if name == "exp_b2" else 0
        mats[r:r + m.shape[0], a:b] = m
    rows = np.zeros((8, NROW), f4)
    rows[:, R_UB:R_UB + D] = i["L2_cond_up_b"]
    rows[:, R_BI:R_BI + FF] = i["L0_cond_bi"]
    rows[:, R_BO:R_BO + D] = i["L0_cond_bo"]
    rows[:, R_GAM:R_GAM + D] = i["L0_cond_gamma"]
    rows[:, R_BET:R_BET + D] = i["L0_cond_beta"]
    rows[0, R_B3:R_UB] = i["L3_cond_b2_nr"]
    rows[1, R_B3:R_UB] = i["L3_cond_b2_tsr"]
    rows[2, R_B3:R_UB] = i["L3_cond_b3_sr"]
    bc = np.stack([i["L2_cond_ln_gamma"], i["L2_cond_ln_beta"], i["L3_cond_gamma"], i["L3_cond_beta"]])
    tab = np.zeros((NBLK, A2, A2 + 2), f4)
    tab[1:17, :, :A2] = i["L2_cond_expert_W"].transpose(0, 2, 1)
    tab[1:17, :, A2] = i["L2_cond_expert_b"]
    tab[1:17, :, A2 + 1] = i["L2_cond_domain_emb"]
    for blk, e in ((0, 0), (17, 15)):
        tab[blk, :, :A2] = np.eye(A2, dtype=f4)
        tab[blk, :, A2 + 1] = i["L2_cond_domain_emb"][e]

    def w_in(w):
        return w.transpose(1, 0, 2)

    def w_out(w):
        return w.reshape(w.shape[0], NF, P, D).transpose(2, 0, 1, 3).reshape(P, w.shape[0], NF * D)

    return {
        "x_nat": x.reshape(NG, P, D).transpose(1, 0, 2),
        "x_t": x.reshape(NTOK, D).T,
        "ids_row": ids[0].reshape(1, B),
        "ids_all": np.broadcast_to(np.stack(ids)[None], (P, 4, B)),
        "ids_j": np.repeat(ids[2].reshape(NG, GRP).T, A2, axis=0),
        "cols": cols,
        "mats": mats,
        "rows": rows.reshape(P, RW),
        "bcast": np.broadcast_to(bc[None], (P, 4, D)),
        "l2tab": tab.reshape(NBLK * A2, A2 + 2),
        "wi": w_in(i["L0_cond_Wi"]),
        "wo": w_out(i["L0_cond_Wo"]),
        "w1": np.concatenate([w_in(i["L1_cond_exp_w1"]), w_out(i["L1_cond_exp_w2"])], axis=2),
    }


def kernel(**inputs):
    import numpy as np
    import concourse.bacc as bacc
    from concourse.bass_utils import run_bass_kernel_spmd

    laid = lay_out({k: np.asarray(v) for k, v in inputs.items()}, np)
    nc = bacc.Bacc("TRN2", target_bir_lowering=False, num_devices=1)
    arrays, aps = {}, {}
    for name, a in laid.items():
        a = np.ascontiguousarray(a)
        arrays[f"in_{name}_dram"] = a
        aps[f"in_{name}"] = nc.dram_tensor(f"in_{name}_dram", a.shape, mybir.dt.from_np(a.dtype),
                                           kind="ExternalInput").ap()
    out = nc.dram_tensor("out_dram", (P, NG, D), F32, kind="ExternalOutput").ap()
    build_program(nc, out=out, **aps)
    r = run_bass_kernel_spmd(nc, [arrays], core_ids=[0])
    got = r.results[0]["out_dram"]
    return got.transpose(1, 0, 2).reshape(B, S, D)
```

```python
import concourse.bass as bass
from concourse import mybir
from contextlib import ExitStack

F32 = mybir.dt.float32
F32R = mybir.dt.float32r
BF16 = mybir.dt.bfloat16
I32 = mybir.dt.int32
U32 = mybir.dt.uint32
ALU = mybir.AluOpType
ACT = mybir.ActivationFunctionType
AX = mybir.AxisListType

P = 128
D = 128
B, S = 32, 32
NTOK = B * S
GRP = P // S
NG = NTOK // P
NH = 2
GH = NG // NH
T = NTOK // NH
FF = 512
NF = FF // P
E0, E1, NSUBJ = 8, 8, 32
A2 = 32
NCOND = 3
NBLK = 18
EH = E1 // 2
POOL_E = 2
RAW = 4
PG = 2
PS = PG * GRP
PT = PG * P
NE = NH * E1

UNITS = ((0, GH), (GH, GH // 2), (GH + GH // 2, GH // 2))
NU = 4
NR = 4
HALF_EXP = -0.5
EULER = 2.718281828459045

C_LNG, C_LNB, C_HB1, C_HB2, C_SB1, C_SB2G, C_SB2B = range(7)
C_B1NR, C_B1TSR, C_B1SR0, C_B1SR1, C_B2SR, C_DB, C_P32, C_L2G, C_L2B = range(7, 16)
C_EB1 = 16
NCOL = C_EB1 + E1 * NF

MATS = {}
NMAT = 0
for _name, _w in (("hyp_w1", 128), ("hyp_w2", 128), ("sty_w1", 64), ("sty_w2", 256), ("subj", 64),
                  ("router", 8), ("ident", 128), ("downT", 32), ("upT", 128), ("exp_b2", 128),
                  ("w1_nr", 128), ("w1_tsr", 128), ("w1_sr", 256), ("w2_sr0", 128), ("w2_sr1", 128),
                  ("w2_nr", 128), ("w2_tsr", 128), ("w3_sr", 128)):
    MATS[_name] = (NMAT, NMAT + _w)
    NMAT += _w
MAT_STYLE = MATS["router"][0]
MAT_EARLY = MATS["w1_nr"][0]

R_BI, R_BO, R_GAM, R_BET, R_B3, R_UB = 0, 512, 640, 768, 896, 1024
NROW = 1152
RW = 8 * NROW // P


def build_program(nc, in_x_t, in_ids_row, in_ids_all, in_ids_j, in_cols, in_mats, in_rows,
                  in_bcast, in_l2tab, in_wi, in_wo, in_w1, out):
    ctx = ExitStack()
    with ctx:
        def sb(name, shape, dt=F32):
            return ctx.enter_context(nc.sbuf_tensor(name, shape, dt))

        def sem(name):
            return ctx.enter_context(nc.semaphore(name))

        x_t = sb("x_t", [P, NTOK])
        ids_row = sb("ids_row", [1, B], I32)
        ids_all = sb("ids_all", [P, 4, B], I32)
        ids_f = sb("ids_f", [P, 4, B])
        ids_j = sb("ids_j", [P, NG], I32)
        cols = sb("cols", [P, NCOL])
        mats = sb("mats", [P, MAT_EARLY])
        bcast = sb("bcast", [P, 2, D])
        rows_p = sb("rows_p", [P, RW])
        rows_q = sb("rows_q", [P, 3, RW], BF16)
        rows3 = sb("rows3", [96, NROW], BF16)
        def parts(name, before):
            with nc.sbuf_tensor(name + "_l3", [P, EH, FF], F32) as after:
                pass
            early = sb(name + "_early", [P, EH, FF], F32R)
            with nc.sbuf_tensor(before, [P, GRP, FF], F32) as place:
                pass
            late = sb(name + "_late", [P, E1 - EH, FF], F32R)
            return lambda e: early[:, e, :] if e < EH else late[:, e - EH, :], place, after

        w1_hi, wi_sel7, a_l3_b = parts("w1_hi", "wi_sel7")
        w1_lo, wo_sel7, l3_b_place = parts("w1_lo", "wo_sel7")
        w2_hi, wi_sel6, _unused = parts("w2_hi", "wi_sel6")
        w2_lo, wo_sel6, _unused = parts("w2_lo", "wo_sel6")
        with nc.sbuf_tensor("wi_all", [P, E0, FF], F32) as wi_all:
            pass
        w_raw_ring = sb("w_raw", [P, RAW, 2 * FF])
        wi_sel0 = sb("wi_sel0", [P, GRP, FF])
        wo_sel0 = sb("wo_sel0", [P, GRP, FF])
        oh0 = sb("oh0", [96, NTOK], BF16)
        ohc = x_t[0:96, 0:NTOK // 2].bitcast(BF16)
        ohs = sb("ohs", [NSUBJ, B])
        cmask = sb("cmask", [P, NCOND, B])
        half_exp = sb("half_exp", [P, 16])
        euler = sb("euler", [P, GH])
        iota8 = sb("iota8", [P, E1], I32)
        se_t = sb("se_t", [64, B])
        hy1 = sb("hy1", [P, B])
        hy2 = sb("hy2", [P, B])
        st1 = sb("st1", [64, B])
        gam_raw = sb("gam_raw", [P, B])
        gam_abs = sb("gam_abs", [P, B])
        gam_exp = sb("gam_exp", [P, B])
        gam_log = sb("gam_log", [P, B])
        gam_s = sb("gam_s", [P, B])
        bet_s = sb("bet_s", [P, B])
        with nc.sbuf_tensor("wi_sel2", [P, GRP, FF], F32) as wi_sel2, \
                nc.sbuf_tensor("wo_sel2", [P, GRP, FF], F32) as wo_sel2:
            pass
        hid_hi0 = sb("hid_hi0", [P, NF, T], F32R)
        hid_lo0 = sb("hid_lo0", [P, NF, T], F32R)
        with nc.sbuf_tensor("wi_sel1", [P, GRP, FF], F32) as wi_sel1, \
                nc.sbuf_tensor("wo_sel1", [P, GRP, FF], F32) as wo_sel1:
            pass
        hid_hi = [hid_hi0, sb("hid_hi1", [P, NF, T], F32R)]
        hid_lo = [hid_lo0, sb("hid_lo1", [P, NF, T], F32R)]

        def wi_sel(g):
            return (wi_sel0, wi_sel1, wi_sel2, wi_sel1, wi_sel0, wi_sel1, wi_sel6, wi_sel7)[g]

        def wo_sel(g):
            return (wo_sel0, wo_sel1, wo_sel2, wo_sel3, wo_sel0, wo_sel1, wo_sel6, wo_sel7)[g]

        def w_raw(e, k):
            return w_raw_ring[:, e % RAW, k * FF:k * FF + FF]

        h0 = sb("h0", [P, 2, FF])
        h0t = sb("h0t", [P, 2, FF])
        gb0 = sb("gb0", [P, GH, 2 * D])
        y0 = sb("y0", [P, 2, D])
        stat0 = sb("stat0", [P, 2, 6])
        mv0 = sb("mv0", [P, 2, 2])
        rs0 = sb("rs0", [P, 2, 2])
        x1 = sb("x1", [P, NG, D])
        stat1 = sb("stat1", [P, 2, 6])
        mv1 = sb("mv1", [P, 2, 2])
        rs1 = sb("rs1", [P, 2, 2])
        z1 = sb("z1", [P, GH, D])
        hn = sb("hn", [P, T])
        cen = h2 = hn
        tsum = sb("tsum", [P, 2, PS])
        tmean = sb("tmean", [P, 2, PS])
        sq = z1[:, :, :].rearrange("p g d -> p (g d)")
        tvar = sb("tvar", [P, 2, PS])
        trs = sb("trs", [P, 2, 2, PS])
        tscale = sb("tscale", [P, 2, PS])
        with nc.sbuf_tensor("wo_sel3", [P, GRP, FF], F32) as wo_sel3:
            pass
        h2_hi = sb("h2_hi", [P, NH, T], F32R)
        h2_lo = sb("h2_lo", [P, NH, T], F32R)
        logit = sb("logit", [P, GH, E1])
        top = sb("top", [P, GH, 8])
        topi = sb("topi", [P, GH, 8], U32)
        topf = sb("topf", [P, GH, 8])
        dif = sb("dif", [P, GH])
        ratio = sb("ratio", [P, GH])
        wtop = sb("wtop", [P, 3, GH])
        eq1 = sb("eq1", [P, GH, E1])
        eq2 = sb("eq2", [P, GH, E1])
        combf = sb("combf", [P, GH, E1])
        comb_t = sb("comb_t", [E1, NH, T])
        gb = sb("gb", [P, 2, T])
        gated = sb("gated", [P, 2, T])
        acc = sb("acc", [P, NH, T])
        r1 = sb("r1", [P, NR, T])
        l2g = sb("l2g", [P, NG, A2 + 2])
        l2i_f = sb("l2i_f", [P, NG])
        l2i = sb("l2i", [P, NG], I32)
        l2b = sb("l2b", [P, NG])
        old = w_raw_ring[:, :, :].rearrange("p e n -> p (e n)")
        old_wi = wi_sel0[:, :, :].rearrange("p j n -> p (j n)")
        old_wo = wo_sel0[:, :, :].rearrange("p j n -> p (j n)")

        def groups(ap):
            return ap.rearrange("p (g d) -> p g d", d=D)

        bd_h = groups(old[:, 0:2 * T])
        bd_w = groups(old[:, 2 * T:4 * T])
        z3 = groups(old[:, 4 * T:5 * T])
        tt = (old[:, 5 * T:6 * T], l3_b_place[:, 0, :])
        zz = (groups(old[:, 6 * T:7 * T]), groups(l3_b_place[:, 1, :]))
        a_l3 = (old_wi.rearrange("p (k t) -> p k t", k=4), a_l3_b)
        nr_act, tsr_act = [tuple(a[:, k, :] for a in a_l3) for k in (3, 2)]
        a_sr2 = (old_wo[:, 0:T], l3_b_place[:, 2, :])
        mats_l3 = old_wo[:, T:T + NMAT - MAT_EARLY]
        hb = sb("hb", [P, P])
        stat2 = sb("stat2", [P, NG, 6])
        mv2 = sb("mv2", [P, NG, 2])
        rs2 = sb("rs2", [P, 2, NG])
        ps = ctx.enter_context(nc.psum_tensor("ps", [P, 8, 512], F32))

        def bank_up(g):
            return ps[:, 3 * (g % 2) if g < GH else 0, :]

        def bank_tr(g):
            return ps[:, 1 + 3 * (g % 2) if g < GH else 1, :]

        def bank_sm(g):
            return ps[:, (2, 5, 7, 6)[g] if g < GH else 2, :]

        def bank_z(q):
            return ps[:, 4 if q < 2 else 1, :]

        def bank_route(c):
            return ps[:, (6, 2)[c], :]

        def bank_comb(c):
            return ps[:, (6, 1)[c], :]

        def first(u):
            return UNITS[u][0] % GH

        def width(u):
            return P * UNITS[u][1]

        def tok(u):
            return slice(P * first(u), P * first(u) + width(u))

        def seqs32(u):
            return slice(S * first(u), S * first(u) + width(u) // GRP)

        def seqs_of(u):
            return slice(GRP * UNITS[u][0], GRP * (UNITS[u][0] + UNITS[u][1]))

        def half(u):
            return UNITS[u][0] // GH

        def bank(u, k):
            return ps[:, ((0, 1, 2), (3, 4, 5), (1, 6, 7))[u][k], 0:width(u)]

        def bank_u(n):
            return ps[:, (3, 4, 5, 7)[n % NU], :]

        S0, S1 = ps[:, 6, :], ps[:, 7, :]
        D_BANK, IDLE_BANK = ps[:, 6, :], ps[:, 7, :]

        def mat(name, rows=P, first=0):
            a, b = MATS[name]
            if a >= MAT_EARLY:
                return mats_l3[:, a - MAT_EARLY:b - MAT_EARLY]
            return mats[first:first + rows, a:b]

        def col(c, rows=P):
            return cols[0:rows, c:c + 1]

        ld_idrow = sem("ld_idrow")
        ld_ids = sem("ld_ids")
        ld_idj = sem("ld_idj")
        ld_mats = sem("ld_mats")
        ld_mats_l1 = sem("ld_mats_l1")
        ld_mats_l3 = sem("ld_mats_l3")
        ld_rows = sem("ld_rows")
        rows_spread = sem("rows_spread")
        ld_xt = [sem("ld_xt_low"), sem("ld_xt_high")]
        ld_bcast = sem("ld_bcast")
        ld_wi = sem("ld_wi")
        ld_wip = {g: sem(f"ld_wip{g}") for g in range(GH, NG)}
        ld_wop = [sem(f"ld_wop{g}") for g in range(NG)]
        ld_raw = [sem(f"ld_raw{e}") for e in range(RAW)]
        ld_l2 = sem("ld_l2")
        st_out = sem("st_out")
        const_dve = sem("const_dve")
        const_pool = sem("const_pool")
        rows_split = sem("rows_split")
        oh_ready = sem("oh_ready")
        ohc_ready = sem("ohc_ready")
        cmask_ready = sem("cmask_ready")
        l2i_ready = sem("l2i_ready")
        bd_zero = sem("bd_zero")
        bd_ready = sem("bd_ready")
        sty_mm = sem("sty_mm")
        sty_ev = sem("sty_ev")
        sty_act = sem("sty_act")
        pick_dve = sem("pick_dve")
        up0_done = sem("up0_done")
        gelu0_done = sem("gelu0_done")
        tr0_done = sem("tr0_done")
        h0t_done = sem("h0t_done")
        rows0_done = sem("rows0_done")
        gb0_ready = sem("gb0_ready")
        dn0_done = sem("dn0_done")
        var0_ready = sem("var0_ready")
        rs0_ready = sem("rs0_ready")
        x1_ready = sem("x1_ready")
        var1_ready = sem("var1_ready")
        rs1_ready = sem("rs1_ready")
        z1_ready = sem("z1_ready")
        zt_done = sem("zt_done")
        hn_ready = sem("hn_ready")
        cen_ready = sem("cen_ready")
        sq_ready = sem("sq_ready")
        tvar_ready = sem("tvar_ready")
        trs_ready = sem("trs_ready")
        h2_ready = sem("h2_ready")
        h2s_ready = sem("h2s_ready")
        route_mm = sem("route_mm")
        dif_ready = sem("dif_ready")
        ratio_ready = sem("ratio_ready")
        comb_ready = sem("comb_ready")
        combt_mm = sem("combt_mm")
        combt_ready = sem("combt_ready")
        acc_mm = sem("acc_mm")
        acc_ready = sem("acc_ready")
        w_hi = sem("w_hi")
        w_lo_pool = sem("w_lo_pool")
        w_lo_dve = sem("w_lo_dve")
        up1_done = sem("up1_done")
        relu_done = sem("relu_done")
        hi_dve = sem("hi_dve")
        hi_act = sem("hi_act")
        lo_dve = sem("lo_dve")
        lo_pool = sem("lo_pool")
        dn1_done = sem("dn1_done")
        ld_gb = [sem("ld_gb_even"), sem("ld_gb_odd")]
        gated_ready = sem("gated_ready")
        acc_done = sem("acc_done")
        acc_last = sem("acc_last")
        dproj_mm = sem("dproj_mm")
        hb_ready = sem("hb_ready")
        exp_mm = sem("exp_mm")
        bdh_ready = sem("bdh_ready")
        up2_mm = sem("up2_mm")
        var2_ready = sem("var2_ready")
        rs2_ready = sem("rs2_ready")
        z3_ready = sem("z3_ready")
        z3t_mm = sem("z3t_mm")
        x3t_ready = sem("x3t_ready")
        l3a_mm = sem("l3a_mm")
        l3a_act = sem("l3a_act")
        l3a_mask = sem("l3a_mask")
        l3a_mask_pool = sem("l3a_mask_pool")
        l3b_mm = sem("l3b_mm")
        l3b_act = sem("l3b_act")
        l3b_mask = sem("l3b_mask")
        l3o_mm = sem("l3o_mm")
        var3_ready = sem("var3_ready")
        rs3_ready = sem("rs3_ready")
        y_ready = sem("y_ready")
        dve_seq = sem("dve_seq")
        pool_seq = sem("pool_seq")
        act_seq = sem("act_seq")

        def wait_r1_used(eng, u):
            n, f = u // NF, u % NF
            if f == NF - 1:
                eng.wait_ge(lo_pool, 2 * n + 2)
            elif f % 2 == 0:
                eng.wait_ge(lo_dve, 2 * n + f // 2 + 1)
            else:
                eng.wait_ge(lo_pool, 2 * n + 1)

        def wait_hidden_free(eng, n):
            if n == 0:
                eng.wait_ge(up0_done, 3)
                eng.wait_ge(dn0_done, 3)
            if n == 1:
                eng.wait_ge(up0_done, 6)
                eng.wait_ge(dn0_done, 6)
            if n >= 2:
                eng.wait_ge(dn1_done, n - 1)

        def later_splits(n):
            return {1: (3,), 2: (4,), 3: (5,), 4: (6,), 5: (7,)}.get(n, ())

        def low_by_dve(e):
            return e + 1 + max(0, e + 1 - POOL_E)

        def load_weights(eng, n):
            c, e = n // E1, n % E1
            if e == 0:
                eng.wait_ge(combt_ready, c + 1)
            if n >= 2:
                eng.wait_ge(gated_ready, n - 1)
            eng.dma_start(gb[:, n % 2, :], comb_t[e:e + 1, c, :].unsqueeze(1).broadcast_to([1, P, T])).then_inc(ld_gb[n % 2], 16)

        def load_raw(eng, e):
            eng.dma_start(w_raw_ring[:, e % RAW, :], in_w1[:, e, :]).then_inc(ld_raw[e % RAW], 16)

        block = ctx.enter_context(nc.Block())

        @block.sync
        def _(sp):
            sp.dma_start(ids_row[:], in_ids_row).then_inc(ld_idrow, 16)
            sp.dma_start(cols[:], in_cols).then_inc(ld_ids, 16)
            sp.dma_start(ids_all[:], in_ids_all).then_inc(ld_ids, 16)
            sp.dma_start(wi_all[:], in_wi).then_inc(ld_wi, 16)
            sp.dma_start(x_t[:, 0:T], in_x_t[:, 0:T]).then_inc(ld_xt[0], 16)
            sp.dma_start(mats[:, MAT_STYLE:MAT_EARLY], in_mats[:, MAT_STYLE:MAT_EARLY]).then_inc(ld_mats_l1, 16)
            sp.wait_ge(ld_idrow, 16)

            with sp.register("sp_expert") as reg:
                def fetch(g, src, dst, done):
                    for j in range(GRP):
                        b = GRP * g + j
                        sp.reg_load(reg, ids_row[0:1, b:b + 1])
                        e = sp.snap(reg, min_val=0, max_val=E0 - 1)
                        sp.dma_start(dst[:, j:j + 1, :], src[:, bass.ds(e, 1), :]).then_inc(done, 16)

                def fetch_both(g):
                    fetch(g, in_wi, wi_sel(g), ld_wip[g])
                    fetch(g, in_wo, wo_sel(g), ld_wop[g])

                sp.wait_ge(rows_split, 1)
                sp.wait_ge(const_dve, 1)
                for q in range(3):
                    sp.dma_start(rows3[32 * q:32 * q + 8, :], rows_q[:, q, :]).then_inc(rows_spread, 16)
                fetch(0, in_wo, wo_sel(0), ld_wop[0])
                for g in range(1, GH):
                    fetch(g, in_wo, wo_sel(g), ld_wop[g])
                sp.wait_ge(pick_dve, GH)
                sp.dma_start(x_t[:, T:2 * T], in_x_t[:, T:2 * T]).then_inc(ld_xt[1], 16)
                sp.wait_ge(up0_done, 1)
                fetch(4, in_wi, wi_sel(4), ld_wip[4])
                sp.wait_ge(dn0_done, 1)
                fetch(4, in_wo, wo_sel(4), ld_wop[4])
                load_raw(sp, 0)
                sp.wait_ge(dn0_done, 2)
                sp.wait_ge(up0_done, 4)
                fetch_both(5)
                load_raw(sp, 1)
                fetch_both(6)
                load_raw(sp, 2)
                load_raw(sp, 3)
                fetch_both(7)
                for e in range(RAW, E1):
                    sp.wait_ge(w_hi, 2 * (e - RAW + 1))
                    sp.wait_ge(w_lo_pool, min(POOL_E, e - RAW + 1))
                    sp.wait_ge(w_lo_dve, low_by_dve(e - RAW))
                    load_raw(sp, e)
                    if e < RAW + 2:
                        load_weights(sp, e - RAW)
                load_weights(sp, 2)
                load_weights(sp, 3)
            sp.wait_ge(dn0_done, NG)
            sp.dma_start(mats_l3, in_mats[:, MAT_EARLY:NMAT]).then_inc(ld_mats_l3, 16)
            sp.dma_start(bcast[:], in_bcast).then_inc(ld_bcast, 16)
            for n in range(4, NE):
                load_weights(sp, n)
            for u, (g0, n) in enumerate(UNITS):
                sp.wait_ge(y_ready, u + 1)
                sp.dma_start(out[:, g0:g0 + n, :], zz[half(u)][:, first(u):first(u) + n, :]).then_inc(st_out, 16)
            sp.wait_ge(st_out, 16 * len(UNITS))

        @block.tensor
        def _(pe):
            ident = mat("ident")
            def style():
                pe.wait_ge(ld_mats, 16)
                pe.wait_ge(oh_ready, 1)
                pe.matmul(S0[0:64, 0:B], mat("subj", NSUBJ), ohs[:], start=True, stop=True).then_inc(sty_mm, 1)
                pe.wait_ge(sty_ev, 1)
                pe.matmul(S1[:, 0:B], mat("hyp_w1", 64), se_t[:], start=True, stop=True).then_inc(sty_mm, 1)
                pe.wait_ge(sty_ev, 2)
                pe.matmul(S0[:, 0:B], mat("hyp_w2"), hy1[:], start=True, stop=True).then_inc(sty_mm, 1)
                pe.wait_ge(sty_ev, 3)
                pe.matmul(S1[0:64, 0:B], mat("sty_w1"), hy2[:], start=True, stop=True).then_inc(sty_mm, 1)
                pe.wait_ge(sty_ev, 4)
                w = mat("sty_w2", 64)
                pe.matmul(S0[:, 0:B], w[:, 0:D], st1[:], start=True, stop=True).then_inc(sty_mm, 1)
                pe.matmul(S1[:, 0:B], w[:, D:2 * D], st1[:], start=True, stop=True).then_inc(sty_mm, 1)

            def keep_warm(n):
                for _ in range(n):
                    pe.matmul(IDLE_BANK, oh0[:, 0:P], oh0[:, 0:T], start=True, stop=True)

            def l0_up(g):
                if g == 0:
                    pe.wait_ge(rows_spread, 48)
                    pe.wait_ge(oh_ready, 2)
                    pe.wait_ge(ld_xt[0], 16)
                    pe.wait_ge(ld_mats_l1, 16)
                if g == GH:
                    pe.wait_ge(ld_xt[1], 16)
                if g >= GH:
                    pe.wait_ge(gelu0_done, g)
                elif g >= 2:
                    pe.wait_ge(gelu0_done, g - 1)
                out0 = bank_up(g)
                pe.matmul(out0, oh0[:, P * g:P * g + P], rows3[:, R_BI:R_BI + FF], start=True, stop=False,
                          skip_group_check=True)
                if g < GH:
                    pe.wait_ge(pick_dve, g + 1)
                else:
                    pe.wait_ge(ld_wip[g], 16 * GRP)
                for j in range(GRP):
                    mm = pe.matmul(out0[S * j:S * j + S, :], x_t[:, P * g + S * j:P * g + S * j + S],
                                   wi_sel(g)[:, j, :], start=False, stop=True, skip_group_check=True)
                mm.then_inc(up0_done, 1)

            def l0_turn(g):
                pe.wait_ge(gelu0_done, g + 1)
                if g >= GH:
                    pe.wait_ge(h0t_done, g)
                elif g >= 2:
                    pe.wait_ge(h0t_done, g - 1)
                for f in range(NF):
                    mm = pe.transpose(bank_tr(g)[:, P * f:P * f + P], h0[:, g % 2, P * f:P * f + P], ident)
                mm.then_inc(tr0_done, 1)

            def l0_rows(g):
                if g >= GH:
                    pe.wait_ge(x1_ready, g)
                if g == 2:
                    pe.wait_ge(sty_act, 2)
                out0, t = bank_sm(g), slice(P * g, P * g + P)
                pe.matmul(out0[:, 0:3 * D], oh0[:, t], rows3[:, R_BO:R_BO + 3 * D], start=True, stop=False,
                          skip_group_check=True)
                pe.matmul(out0[:, 0:D], x_t[:, t], ident, start=False, stop=False,
                          skip_group_check=True).then_inc(rows0_done, 1)

            def l0_down(g):
                pe.wait_ge(gb0_ready, g + 1)
                pe.wait_ge(h0t_done, g + 1)
                pe.wait_ge(ld_wop[g], 16 * GRP)
                out0 = bank_sm(g)
                for f in range(NF):
                    for j in range(GRP):
                        mm = pe.matmul(out0[S * j:S * j + S, 0:D],
                                       h0t[:, g % 2, P * f + S * j:P * f + S * j + S],
                                       wo_sel(g)[:, j, P * f:P * f + P], start=False,
                                       stop=f == NF - 1, skip_group_check=True)
                mm.then_inc(dn0_done, 1)

            def z_turn(q):
                pe.wait_ge(z1_ready, PG * (q + 1))
                if q >= 2:
                    pe.wait_ge(h0t_done, NG)
                for i in range(PG * (q % 2), PG * (q % 2) + PG):
                    mm = pe.transpose(bank_z(q)[:, P * i:P * i + P], z1[:, i, :], ident)
                mm.then_inc(zt_done, 1)

            def route(c):
                pe.wait_ge(h2_ready, 2 * c + 2)
                for i in range(GH):
                    mm = pe.matmul(bank_route(c)[:, E1 * i:E1 * i + E1], h2[:, P * i:P * i + P], mat("router"),
                                   start=True, stop=True)
                mm.then_inc(route_mm, 1)

            def comb_turn(c):
                pe.wait_ge(comb_ready, c + 1)
                for i in range(GH):
                    mm = pe.matmul(bank_comb(c)[0:E1, P * i:P * i + P], combf[:, i, :], ident, start=True, stop=True)
                mm.then_inc(combt_mm, 1)

            def acc_start(c):
                pe.wait_ge(combt_ready, c + 1)
                pe.matmul(bank_route(c), mat("exp_b2", E1), comb_t[:, c, :], start=True, stop=False,
                          skip_group_check=True)
                for i in range(GH):
                    mm = pe.matmul(bank_route(c)[:, P * i:P * i + P], x1[:, GH * c + i, :], ident, start=False, stop=True,
                                   skip_group_check=True)
                mm.then_inc(acc_mm, 1)

            def l1_up(n):
                c, e = n // E1, n % E1
                if c == 0:
                    pe.wait_ge(w_hi, 2 * (e + 1))
                    if e < POOL_E:
                        pe.wait_ge(w_lo_pool, e + 1)
                    else:
                        pe.wait_ge(w_lo_dve, low_by_dve(e) - 1)
                if e == 0:
                    pe.wait_ge(h2s_ready, 2 * c + 2)
                hi, lo = h2_hi[:, c, :], h2_lo[:, c, :]
                for f in range(NF):
                    if n < 2 and f == 2:
                        l0_rows(GH + 1 + n)
                    u = NF * n + f
                    if u >= NU:
                        pe.wait_ge(relu_done, u - NU + 1)
                        if (u - NU) % 2:
                            pe.wait_ge(hi_act, (u - NU) // 2 + 1)
                    whi, wlo = w1_hi(e)[:, P * f:P * f + P], w1_lo(e)[:, P * f:P * f + P]
                    pe.matmul(bank_u(u), whi, hi, start=True, stop=False)
                    pe.matmul(bank_u(u), whi, lo, start=False, stop=False)
                    pe.matmul(bank_u(u), wlo, hi, start=False, stop=True).then_inc(up1_done, 1)

            def l1_down(n):
                e = n % E1
                if n < E1:
                    pe.wait_ge(w_lo_dve, low_by_dve(e))
                pe.wait_ge(hi_dve, 2 * (n + 1))
                pe.wait_ge(hi_act, 2 * (n + 1))
                pe.wait_ge(lo_dve, 2 * (n + 1))
                pe.wait_ge(lo_pool, 2 * (n + 1))
                if n >= 1:
                    pe.wait_ge(gated_ready, n)
                for f in range(NF):
                    hi, lo = hid_hi[n % 2][:, f, :], hid_lo[n % 2][:, f, :]
                    whi, wlo = w2_hi(e)[:, P * f:P * f + P], w2_lo(e)[:, P * f:P * f + P]
                    pe.matmul(D_BANK, whi, hi, start=f == 0, stop=False)
                    pe.matmul(D_BANK, whi, lo, start=False, stop=False)
                    mm = pe.matmul(D_BANK, wlo, hi, start=False, stop=f == NF - 1)
                mm.then_inc(dn1_done, 1)

            def l2_down(u):
                g0, n = UNITS[u]
                c = g0 // GH
                if c:
                    pe.wait_ge(acc_last, u)
                else:
                    pe.wait_ge(acc_done, E1)
                    pe.wait_ge(acc_ready, NH)
                if u == 1:
                    pe.wait_ge(hi_act, 2 * NE)
                xv = acc[:, c, tok(u)].rearrange("p (g j s) -> p g j s", g=n, j=GRP)
                for j in range(GRP):
                    mm = pe.matmul(bank(u, 2)[A2 * j:A2 * j + A2, 0:S * n], mat("downT"), xv[:, :, j, :],
                                   start=True, stop=True, skip_group_check=True)
                mm.then_inc(dproj_mm, 1)

            def l2_expert(u):
                g0, n = UNITS[u]
                pe.wait_ge(hb_ready, u + 1)
                if u == 0:
                    pe.wait_ge(bd_ready, 1)
                h = hb[:, seqs32(u)]
                for i in range(n):
                    mm = pe.matmul(bank(u, 1)[:, S * i:S * i + S], bd_w[:, g0 + i, :], h[:, S * i:S * i + S],
                                   start=True, stop=True)
                mm.then_inc(exp_mm, 1)

            def l2_residual(u):
                g0, n = UNITS[u]
                for i in range(n):
                    t = slice(P * i, P * i + P)
                    pe.matmul(bank(u, 2)[:, t], oh0[:, t], rows3[:, R_UB:R_UB + D], start=i == 0, stop=False,
                              skip_group_check=True)
                    pe.matmul(bank(u, 2)[:, t], acc[:, g0 // GH, tok(u)][:, t], ident, start=False, stop=False,
                              skip_group_check=True)

            def l2_up(u):
                g0, n = UNITS[u]
                pe.wait_ge(bdh_ready, u + 1)
                for i in range(n):
                    mm = pe.matmul(bank(u, 2)[:, P * i:P * i + P], bd_h[:, g0 + i, :], mat("upT"), start=False,
                                   stop=True, skip_group_check=True)
                mm.then_inc(up2_mm, 1)

            def z3_turn(u):
                pe.wait_ge(z3_ready, u + 1)
                for i in range(UNITS[u][1]):
                    mm = pe.transpose(bank(u, 1)[:, P * i:P * i + P], z3[:, first(u) + i, :], ident)
                mm.then_inc(z3t_mm, 1)

            def l3_a(u, k):
                w = (mat("w1_nr"), mat("w1_tsr"), mat("w1_sr")[:, 0:P], mat("w1_sr")[:, P:2 * P])[3 - k]
                if k == 0:
                    if u == 2:
                        pe.wait_ge(l3a_act, 4)
                    pe.wait_ge(x3t_ready, u + 1)
                    pe.wait_ge(ld_mats_l3, 16)
                if k == 3:
                    pe.wait_ge(l3a_act, 4 * u + 1)
                pe.matmul(bank(u, (0, 2, 1, 0)[k]), w, tt[half(u)][:, tok(u)], start=True, stop=True).then_inc(l3a_mm, 1)

            def l3_b(u):
                pe.wait_ge(l3a_act, 4 * u + 2)
                pe.matmul(bank(u, 2), mat("w2_sr1"), a_l3[half(u)][:, 0, tok(u)], start=True, stop=False)
                pe.matmul(bank(u, 2), mat("w2_sr0"), a_l3[half(u)][:, 1, tok(u)], start=False, stop=True).then_inc(l3b_mm, 1)

            def l3_out(u, k):
                g0, n = UNITS[u]
                if k == 0:
                    pe.wait_ge(l3a_act, 4 * u + 4)
                    if u == 0:
                        pe.wait_ge(ohc_ready, 1)
                if k == 1:
                    pe.wait_ge(l3a_mask_pool, u + 1)
                if k == 2:
                    pe.wait_ge(l3a_mask, u + 1)
                if k == 3:
                    pe.wait_ge(l3b_mask, u + 1)
                h = half(u)
                buf = (tt[h], a_l3[h][:, 2, :], a_l3[h][:, 3, :], a_sr2[h])[k][:, tok(u)]
                w = mat(("ident", "w2_tsr", "w2_nr", "w3_sr")[k])
                for i in range(n):
                    o = bank(u, 0)[:, P * i:P * i + P]
                    if k == 0:
                        g = g0 + i
                        pe.matmul(o, ohc[:, P * g:P * g + P], rows3[:, R_B3:R_B3 + D], start=i == 0,
                                  stop=False, skip_group_check=True)
                    mm = pe.matmul(o, buf[:, P * i:P * i + P], w, start=False, stop=k == 3, skip_group_check=True)
                if k == 3:
                    mm.then_inc(l3o_mm, 1)

            def side(k):
                if k == 2:
                    l0_down(GH + 2)
                    l0_up(GH + 3)
                if k == 3:
                    l0_turn(GH + 3)
                if k == 4:
                    l0_rows(GH + 3)
                if k == 5:
                    l0_down(GH + 3)
                    z_turn(2)
                if k == 8:
                    z_turn(3)
                if k == 14:
                    route(1)
                if k == 17:
                    comb_turn(1)
                if k == 18:
                    acc_start(1)
                if k == 20:
                    l2_down(0)
                if k == 21:
                    l2_expert(0)
                    l2_residual(0)
                if k == 22:
                    l2_up(0)
                if k == 25:
                    z3_turn(0)

            style()
            l0_up(0)
            l0_up(1)
            l0_rows(0)
            l0_turn(0)
            for g in range(GH):
                if g + 2 < GH:
                    l0_up(g + 2)
                if g + 1 < GH:
                    l0_rows(g + 1)
                    l0_turn(g + 1)
                l0_down(g)
            l0_up(GH)
            z_turn(0)
            keep_warm(5)
            l0_rows(GH)
            z_turn(1)
            keep_warm(3)
            l0_turn(GH)
            l0_down(GH)
            l0_up(GH + 1)
            keep_warm(3)
            l0_turn(GH + 1)
            keep_warm(1)
            route(0)
            l1_up(0)
            l0_down(GH + 1)
            comb_turn(0)
            l0_up(GH + 2)
            acc_start(0)
            l0_turn(GH + 2)
            for n in range(1, NE):
                l1_up(n)
                side(2 * n)
                l1_down(n - 1)
                side(2 * n + 1)
            l3_a(0, 0)
            l3_a(0, 1)
            l1_down(NE - 1)
            l3_a(0, 2)
            l2_down(1)
            l2_down(2)
            l3_a(0, 3)
            l2_expert(1)
            l2_residual(1)
            l2_up(1)
            l2_expert(2)
            l2_residual(2)
            l2_up(2)
            l3_b(0)
            l3_out(0, 0)
            z3_turn(1)
            l3_out(0, 1)
            l3_a(1, 0)
            l3_a(1, 1)
            z3_turn(2)
            l3_out(0, 2)
            l3_a(1, 2)
            l3_a(1, 3)
            l3_out(0, 3)
            l3_b(1)
            l3_a(2, 0)
            l3_a(2, 1)
            l3_out(1, 0)
            l3_out(1, 1)
            l3_out(1, 2)
            l3_out(1, 3)
            l3_a(2, 2)
            l3_a(2, 3)
            l3_b(2)
            for k in range(4):
                l3_out(2, k)

        @block.scalar
        def _(act):
            seq = [0]

            def link(ins):
                seq[0] += 1
                ins.then_inc(act_seq, 1)
                act.wait_ge(act_seq, seq[0])

            def style():
                act.wait_ge(sty_mm, 1)
                nc.scalar.copy(se_t[:], S0[0:64, 0:B]).then_inc(sty_ev, 1)
                act.wait_ge(ld_ids, 32)
                act.wait_ge(sty_mm, 2)
                nc.scalar.activation(hy1[:], S1[:, 0:B], ACT.Relu, bias=col(C_HB1)).then_inc(sty_ev, 1)
                act.wait_ge(sty_mm, 3)
                nc.scalar.activation(hy2[:], S0[:, 0:B], ACT.Identity, bias=col(C_HB2)).then_inc(sty_ev, 1)
                act.wait_ge(sty_mm, 4)
                nc.scalar.activation(st1[:], S1[0:64, 0:B], ACT.Relu, bias=col(C_SB1, 64)).then_inc(sty_ev, 1)
                act.wait_ge(sty_mm, 6)
                nc.scalar.activation(gam_raw[:], S0[:, 0:B], ACT.Identity, bias=col(C_SB2G)).then_inc(sty_act, 1)
                nc.scalar.activation(bet_s[:], S1[:, 0:B], ACT.Identity, bias=col(C_SB2B)).then_inc(sty_act, 1)

            def softplus():
                act.wait_ge(sty_act, 2)
                link(nc.scalar.activation(gam_abs[:], gam_raw[:], ACT.Abs))
                link(nc.scalar.activation(gam_exp[:], gam_abs[:], ACT.Exp, scale=-1.0))
                nc.scalar.activation(gam_log[:], gam_exp[:], ACT.Ln, bias=1.0).then_inc(sty_act, 1)

            def gelu0(g):
                act.wait_ge(up0_done, g + 1)
                if g >= 2:
                    act.wait_ge(tr0_done, g - 1)
                nc.scalar.activation(h0[:, g % 2, :], bank_up(g), ACT.Gelu).then_inc(gelu0_done, 1)

            def hidden_t(g):
                act.wait_ge(tr0_done, g + 1)
                if g >= 2:
                    act.wait_ge(dn0_done, g - 1)
                nc.scalar.copy(h0t[:, g % 2, :], bank_tr(g)).then_inc(h0t_done, 1)

            def gam_bet(g):
                act.wait_ge(rows0_done, g + 1)
                nc.scalar.copy(gb0[:, g % GH, :], bank_sm(g)[:, D:3 * D]).then_inc(gb0_ready, 1)

            def split_hi(e):
                if e == EH:
                    act.wait_ge(up0_done, NG)
                    act.wait_ge(dn0_done, NG)
                act.wait_ge(ld_raw[e % RAW], 16 * (e // RAW + 1))
                nc.scalar.copy(w1_hi(e), w_raw(e, 0)).then_inc(w_hi, 1)
                nc.scalar.copy(w2_hi(e), w_raw(e, 1)).then_inc(w_hi, 1)

            def ln_affine(q):
                act.wait_ge(zt_done, q + 1)
                if q >= 2:
                    act.wait_ge(route_mm, 1)
                    act.wait_ge(h2s_ready, 2)
                t = slice(PT * (q % 2), PT * (q % 2) + PT)
                nc.scalar.activation(hn[:, t], bank_z(q)[:, t], ACT.Identity, bias=col(C_LNB),
                                     scale=col(C_LNG)).then_inc(hn_ready, 1)

            def square(q):
                act.wait_ge(cen_ready, q + 1)
                if q >= 2:
                    act.wait_ge(acc_mm, 1)
                t = slice(PT * (q % 2), PT * (q % 2) + PT)
                nc.scalar.activation(sq[:, t], cen[:, t], ACT.Square).then_inc(sq_ready, 1)

            def acc_copy(c):
                act.wait_ge(acc_mm, c + 1)
                nc.scalar.copy(acc[:, c, :], bank_route(c)).then_inc(acc_ready, 1)

            def relu(n):
                e = n % E1
                for f in range(NF):
                    if n == 0 and f == 2:
                        gam_bet(GH + 1)
                    u = NF * n + f
                    act.wait_ge(up1_done, u + 1)
                    if u >= NR:
                        wait_r1_used(act, u - NR)
                    c = C_EB1 + NF * e + f
                    nc.scalar.activation(r1[:, u % NR, :], bank_u(u), ACT.Relu, bias=col(c)).then_inc(relu_done, 1)
                    if f % 2:
                        if f == 1:
                            wait_hidden_free(act, n)
                        nc.scalar.activation(hid_hi[n % 2][:, f, :], bank_u(u), ACT.Relu, bias=col(c)).then_inc(hi_act, 1)

            def l2_gelu(u):
                act.wait_ge(dproj_mm, u + 1)
                if u == 1:
                    act.wait_ge(exp_mm, 1)
                nc.scalar.activation(hb[:, seqs32(u)], bank(u, 2)[:, 0:width(u) // GRP], ACT.Gelu,
                                     bias=col(C_DB)).then_inc(hb_ready, 1)

            def x3t_affine(u):
                act.wait_ge(z3t_mm, u + 1)
                nc.scalar.activation(tt[half(u)][:, tok(u)], bank(u, 1), ACT.Identity, bias=col(C_L2B),
                                     scale=col(C_L2G)).then_inc(x3t_ready, 1)

            def l3_gelu(u, k):
                act.wait_ge(l3a_mm, 4 * u + k + 1)
                nc.scalar.activation(a_l3[half(u)][:, k, tok(u)], bank(u, (0, 2, 1, 0)[k]), ACT.Gelu,
                                     bias=col((C_B1NR, C_B1TSR, C_B1SR0, C_B1SR1)[3 - k])).then_inc(l3a_act, 1)

            def l3_gelu2(u):
                act.wait_ge(l3b_mm, u + 1)
                nc.scalar.activation(a_sr2[half(u)][:, tok(u)], bank(u, 2), ACT.Gelu, bias=col(C_B2SR)).then_inc(l3b_act, 1)

            def side(k):
                if k == 2:
                    gelu0(GH + 3)
                if k == 3:
                    hidden_t(GH + 3)
                if k == 4:
                    gam_bet(GH + 3)
                if k in (5, 9):
                    ln_affine(2 + k // 9)
                if k in (7, 11):
                    square(2 + k // 11)
                if k == 18:
                    acc_copy(1)
                if k == 20:
                    l2_gelu(0)
                if k == 25:
                    x3t_affine(0)

            act.dma_start(mats[:, 0:MAT_STYLE], in_mats[:, 0:MAT_STYLE]).then_inc(ld_mats, 16)
            act.dma_start(rows_p[:], in_rows).then_inc(ld_rows, 16)
            style()
            softplus()
            gelu0(0)
            gelu0(1)
            gam_bet(0)
            for g in range(GH - 2):
                hidden_t(g)
                gelu0(g + 2)
                gam_bet(g + 1)
            hidden_t(GH - 2)
            gam_bet(GH - 1)
            hidden_t(GH - 1)
            ln_affine(0)
            gelu0(GH)
            square(0)
            ln_affine(1)
            gam_bet(GH)
            hidden_t(GH)
            square(1)
            split_hi(0)
            gelu0(GH + 1)
            split_hi(1)
            hidden_t(GH + 1)
            relu(0)
            gelu0(GH + 2)
            acc_copy(0)
            hidden_t(GH + 2)
            gam_bet(GH + 2)
            split_hi(2)
            for n in range(1, NE):
                relu(n)
                side(2 * n)
                for e in later_splits(n):
                    split_hi(e)
                side(2 * n + 1)
            l3_gelu(0, 0)
            l3_gelu(0, 1)
            l3_gelu(0, 2)
            l2_gelu(1)
            l2_gelu(2)
            l3_gelu(0, 3)
            l3_gelu2(0)
            x3t_affine(1)
            l3_gelu(1, 0)
            l3_gelu(1, 1)
            x3t_affine(2)
            l3_gelu(1, 2)
            l3_gelu(1, 3)
            l3_gelu2(1)
            for k in range(4):
                l3_gelu(2, k)
            l3_gelu2(2)

        @block.vector
        def _(dve):
            V = nc.vector
            seq = [0]

            def link(ins):
                seq[0] += 1
                ins.then_inc(dve_seq, 1)
                dve.wait_ge(dve_seq, seq[0])

            def by_seq(ap, n):
                return ap.unsqueeze(2).broadcast_to([ap.shape[0], n, S])

            def tables():
                V.memset(euler[:], EULER)
                V.memset(half_exp[:], HALF_EXP)
                V.memset(rows3[:], 0.0).then_inc(const_dve, 1)
                dve.wait_ge(ld_rows, 16)
                link(V.tensor_copy(rows_q[:, 0, :], rows_p[:]))
                link(V.tensor_tensor(rows_p[:], rows_p[:], rows_q[:, 0, :], ALU.subtract))
                link(V.tensor_copy(rows_q[:, 1, :], rows_p[:]))
                V.tensor_tensor(rows_q[:, 2, :], rows_p[:], rows_q[:, 1, :], ALU.subtract).then_inc(rows_split, 1)
                dve.wait_ge(ld_ids, 32)
                link(V.tensor_copy(ids_f[:], ids_all[:]))
                V.tensor_scalar(ohs[:], ids_f[0:NSUBJ, 1, :], col(C_P32, NSUBJ), None, ALU.is_equal).then_inc(oh_ready, 1)
                dve.wait_ge(ld_idj, 16)
                link(V.tensor_scalar(l2i_f[:], ids_j[:], -1.0, 16.0, ALU.max, ALU.min))
                link(V.tensor_scalar(l2i_f[:], l2i_f[:], 1.0, float(A2), ALU.add, ALU.mult))
                V.tensor_scalar(l2i[:], l2i_f[:], col(C_P32), None, ALU.add).then_inc(l2i_ready, 1)
                V.tensor_scalar(oh0[:].rearrange("p (b s) -> p b s", s=S), by_seq(ids_f[0:96, 0, :], B),
                                col(C_P32, 96), None, ALU.is_equal).then_inc(oh_ready, 1)
                for k in range(NCOND):
                    V.tensor_scalar(cmask[:, k, :], ids_f[:, 3, :], float(k), None, ALU.is_equal).then_inc(cmask_ready, 1)

            def style():
                dve.wait_ge(sty_act, 3)
                link(V.scalar_tensor_tensor(gam_s[:], gam_raw[:], 0.0, gam_log[:], ALU.max, ALU.add))
                link(V.tensor_scalar(gam_s[:], gam_s[:], 1e-8, None, ALU.add))

            def cond_rows():
                dve.wait_ge(dn0_done, NG)
                V.tensor_scalar(ohc.rearrange("p (b s) -> p b s", s=S), by_seq(ids_f[0:96, 3, :], B),
                                col(C_P32, 96), None, ALU.is_equal).then_inc(ohc_ready, 1)

            def l2_tables():
                dve.wait_ge(ld_l2, 16 * NG)
                dve.wait_ge(bd_zero, 2)
                for j in range(GRP):
                    rows = slice(A2 * j, A2 * j + A2)
                    V.tensor_copy(bd_w[rows, :, A2 * j:A2 * j + A2], l2g[rows, :, 0:A2])
                V.tensor_tensor(l2b[:], l2g[:, :, A2], l2g[:, :, A2 + 1], ALU.add).then_inc(bd_ready, 1)

            def pick_wi(g):
                if g == 3:
                    dve.wait_ge(up0_done, 2)
                if g == 0:
                    dve.wait_ge(ld_idrow, 16)
                    dve.wait_ge(ld_wi, 16)
                for j in range(GRP):
                    b = GRP * g + j
                    dve.reg_load(reg, ids_row[0:1, b:b + 1])
                    e = dve.snap(reg, min_val=0, max_val=E0 - 1)
                    ins = V.tensor_copy(wi_sel(g)[:, j:j + 1, :], wi_all[:, bass.ds(e, 1), :])
                ins.then_inc(pick_dve, 1)

            def l0_sum(g):
                dve.wait_ge(dn0_done, g + 1)
                i = g % 2
                link(V.bn_stats(stat0[:, i, :], bank_sm(g)[:, 0:D]))
                if g >= 2:
                    dve.wait_ge(rs0_ready, g - 1)
                V.bn_aggr(mv0[:, i, :], stat0[:, i, :]).then_inc(var0_ready, 1)

            def l0_norm(g):
                i = g % 2
                dve.wait_ge(rs0_ready, g + 1)
                dve.wait_ge(gb0_ready, g + 1)
                link(V.scalar_tensor_tensor(y0[:, i, :], bank_sm(g)[:, 0:D], mv0[:, i, 0:1], gb0[:, g % GH, 0:D],
                                            ALU.subtract, ALU.mult))
                V.scalar_tensor_tensor(x1[:, g, :], y0[:, i, :], rs0[:, i, 1:2], gb0[:, g % GH, D:2 * D],
                                       ALU.mult, ALU.add).then_inc(x1_ready, 1)
                dve.wait_ge(x1_ready, g + 1)
                link(V.bn_stats(stat1[:, i, :], x1[:, g, :]))
                if g >= 2:
                    dve.wait_ge(rs1_ready, g - 1)
                V.bn_aggr(mv1[:, i, :], stat1[:, i, :]).then_inc(var1_ready, 1)

            def l1_ln(g):
                i = g % 2
                dve.wait_ge(rs1_ready, g + 1)
                if g == GH:
                    dve.wait_ge(zt_done, 2)
                V.tensor_scalar(z1[:, g % GH, :], x1[:, g, :], mv1[:, i, 0:1], rs1[:, i, 1:2], ALU.subtract,
                                ALU.mult).then_inc(z1_ready, 1)

            def split_lo(e):
                if e == EH:
                    dve.wait_ge(dn0_done, NG)
                for k in (1,) if e < POOL_E else (0, 1):
                    dve.wait_ge(w_hi, 2 * e + k + 1)
                    V.tensor_tensor((w1_lo, w2_lo)[k](e), w_raw(e, k),
                                    (w1_hi, w2_hi)[k](e).bitcast(F32), ALU.subtract).then_inc(w_lo_dve, 1)

            def time_norm_a(q):
                i = q % 2
                hv = hn[:, PT * i:PT * i + PT].rearrange("p (b s) -> p b s", s=S)
                dve.wait_ge(hn_ready, q + 1)
                link(V.tensor_reduce(tsum[:, i, :], hv, AX.X, ALU.add))
                link(V.tensor_scalar(tmean[:, i, :], tsum[:, i, :], 1.0 / S, None, ALU.mult))
                V.tensor_tensor(hv, hv, by_seq(tmean[:, i, :], PS), ALU.subtract).then_inc(cen_ready, 1)

            def time_norm_b(q):
                i = q % 2
                dve.wait_ge(sq_ready, q + 1)
                V.tensor_reduce(tvar[:, i, :], sq[:, PT * i:PT * i + PT].rearrange("p (b s) -> p b s", s=S), AX.X,
                                ALU.add).then_inc(tvar_ready, 1)

            def time_norm_c(q):
                if q == 0:
                    dve.wait_ge(dn0_done, GH)
                i, c = q % 2, q // 2
                t = slice(PT * i, PT * i + PT)
                dve.wait_ge(trs_ready, q + 1)
                seqs = slice(PS * q, PS * q + PS)
                h2v = h2[:, t].rearrange("p (b s) -> p b s", s=S)
                link(V.tensor_tensor(tscale[:, i, :], trs[:, i, 1, :], gam_s[:, seqs], ALU.mult))
                link(V.tensor_tensor(h2v, h2v, by_seq(tscale[:, i, :], PS), ALU.mult))
                V.tensor_tensor(h2v, h2v, by_seq(bet_s[:, seqs], PS), ALU.add).then_inc(h2_ready, 1)
                dve.wait_ge(h2_ready, q + 1)
                link(V.tensor_copy(h2_hi[:, c, t], h2[:, t]))
                V.tensor_tensor(h2_lo[:, c, t], h2[:, t], h2_hi[:, c, t].bitcast(F32), ALU.subtract).then_inc(h2s_ready, 1)

            def top2(c):
                dve.wait_ge(route_mm, c + 1)
                link(V.tensor_copy(logit[:], bank_route(c)[:, 0:GH * E1].rearrange("p (g e) -> p g e", e=E1)))
                for i in range(GH):
                    ins = V.max(top[:, i, :], logit[:, i, :])
                link(ins)
                V.tensor_tensor(dif[:], top[:, :, 1], top[:, :, 0], ALU.subtract).then_inc(dif_ready, 1)
                for i in range(GH):
                    ins = V.max_index(topi[:, i, :], top[:, i, :], logit[:, i, :])
                link(ins)
                link(V.tensor_copy(topf[:], topi[:]))
                if c == 0:
                    dve.wait_ge(const_pool, 1)
                ids = iota8[:].unsqueeze(1).broadcast_to([P, GH, E1])
                V.tensor_tensor(eq1[:], ids, topf[:, :, 0:1].broadcast_to([P, GH, E1]), ALU.is_equal)
                link(V.tensor_tensor(eq2[:], ids, topf[:, :, 1:2].broadcast_to([P, GH, E1]), ALU.is_equal))

            def combine(c):
                dve.wait_ge(ratio_ready, c + 1)

                def wide(ap):
                    return ap.unsqueeze(2).broadcast_to([P, GH, E1])

                link(V.tensor_scalar(wtop[:, 0, :], ratio[:], 1.0, None, ALU.add))
                link(V.reciprocal(wtop[:, 1, :], wtop[:, 0, :]))
                link(V.tensor_tensor(wtop[:, 2, :], wtop[:, 1, :], ratio[:], ALU.mult))
                V.tensor_tensor(eq1[:], eq1[:], wide(wtop[:, 1, :]), ALU.mult)
                link(V.tensor_tensor(eq2[:], eq2[:], wide(wtop[:, 2, :]), ALU.mult))
                if c:
                    dve.wait_ge(combt_mm, c)
                V.tensor_tensor(combf[:], eq1[:], eq2[:], ALU.add).then_inc(comb_ready, 1)

            def comb_copy(c):
                dve.wait_ge(combt_mm, c + 1)
                V.tensor_copy(comb_t[:, c, :], bank_comb(c)[0:E1, :]).then_inc(combt_ready, 1)

            def hid_split(n):
                wait_hidden_free(dve, n)
                for f in (0, 2):
                    u = NF * n + f
                    dve.wait_ge(relu_done, u + 1)
                    V.tensor_copy(hid_hi[n % 2][:, f, :], r1[:, u % NR, :]).then_inc(hi_dve, 1)
                    dve.wait_ge(hi_dve, 2 * n + f // 2 + 1)
                    V.tensor_tensor(hid_lo[n % 2][:, f, :], r1[:, u % NR, :],
                                    hid_hi[n % 2][:, f, :].bitcast(F32), ALU.subtract).then_inc(lo_dve, 1)

            def gate(n):
                dve.wait_ge(dn1_done, n + 1)
                dve.wait_ge(ld_gb[n % 2], 16 * (n // 2 + 1))
                if n >= 2:
                    dve.wait_ge(acc_done, n - 1)
                V.tensor_tensor(gated[:, n % 2, :], D_BANK, gb[:, n % 2, :], ALU.mult).then_inc(gated_ready, 1)

            def gate_last(u):
                if u == 1:
                    dve.wait_ge(dn1_done, NE)
                    dve.wait_ge(ld_gb[(NE - 1) % 2], 16 * NE // 2)
                    dve.wait_ge(acc_done, NE - 1)
                i, t = (NE - 1) % 2, tok(u)
                link(V.tensor_tensor(gated[:, i, t], D_BANK[:, t], gb[:, i, t], ALU.mult))
                V.tensor_tensor(acc[:, NH - 1, t], acc[:, NH - 1, t], gated[:, i, t], ALU.add).then_inc(acc_last, 1)

            def l2_block(u):
                g0, n = UNITS[u]
                dve.wait_ge(exp_mm, u + 1)
                gs = slice(g0, g0 + n)
                for j in range(GRP):
                    rows = slice(A2 * j, A2 * j + A2)
                    ins = V.tensor_tensor(bd_h[rows, gs, S * j:S * j + S],
                                          bank(u, 1)[rows, 0:S * n].rearrange("p (g s) -> p g s", s=S),
                                          by_seq(l2b[rows, gs], n), ALU.add)
                ins.then_inc(bdh_ready, 1)

            def norm_stats(src, u, ready):
                n = UNITS[u][1]
                for i in range(n):
                    ins = V.bn_stats(stat2[:, UNITS[u][0] + i, :], src[:, i, :])
                link(ins)
                for i in range(n):
                    ins = V.bn_aggr(mv2[:, UNITS[u][0] + i, :], stat2[:, UNITS[u][0] + i, :])
                ins.then_inc(ready, 1)

            def l2_sum(u):
                dve.wait_ge(up2_mm, u + 1)
                norm_stats(groups(bank(u, 2)), u, var2_ready)

            def l2_norm(u):
                dve.wait_ge(rs2_ready, u + 1)
                for i in range(UNITS[u][1]):
                    g = UNITS[u][0] + i
                    ins = V.tensor_scalar(z3[:, g % GH, :], groups(bank(u, 2))[:, i, :], mv2[:, g, 0:1],
                                          rs2[:, 1, g:g + 1], ALU.subtract, ALU.mult)
                ins.then_inc(z3_ready, 1)

            def mask(u, k, act_sem, need, buf, ready):
                dve.wait_ge(act_sem, need)
                v = buf[half(u)][:, tok(u)].rearrange("p (b s) -> p b s", s=S)
                V.tensor_tensor(v, v, by_seq(cmask[:, k, seqs_of(u)], width(u) // S), ALU.mult).then_inc(ready, 1)

            def l3_sum(u):
                dve.wait_ge(l3o_mm, u + 1)
                norm_stats(groups(bank(u, 0)), u, var3_ready)

            def l3_norm(u):
                dve.wait_ge(rs3_ready, u + 1)
                if u == 0:
                    dve.wait_ge(ld_bcast, 16)
                g0, n = UNITS[u]
                y, z = groups(bank(u, 0)), zz[half(u)][:, first(u):first(u) + n, :]
                for i in range(n):
                    ins = V.scalar_tensor_tensor(z[:, i, :], y[:, i, :], mv2[:, g0 + i, 0:1], bcast[:, 0, :],
                                                 ALU.subtract, ALU.mult)
                link(ins)
                for i in range(n):
                    ins = V.scalar_tensor_tensor(z[:, i, :], z[:, i, :], rs2[:, 1, g0 + i:g0 + i + 1],
                                                 bcast[:, 1, :], ALU.mult, ALU.add)
                ins.then_inc(y_ready, 1)

            def side(k):
                if k == 2:
                    l1_ln(GH)
                    l1_ln(GH + 1)
                if k in (3, 5):
                    l0_sum(GH + 2 + k // 5)
                if k in (4, 6):
                    l0_norm(GH + k // 2)
                if k in (5, 7):
                    l1_ln(GH + k // 2)
                if k in (6, 10):
                    time_norm_a(2 + k // 10)
                if k in (8, 12):
                    time_norm_b(2 + k // 12)
                if k in (9, 13):
                    time_norm_c(2 + k // 13)
                if k == 20:
                    cond_rows()
                if k == 15:
                    top2(1)
                if k == 16:
                    combine(1)
                if k == 18:
                    comb_copy(1)
                if k == 19:
                    l2_tables()
                if k == 21:
                    l2_block(0)
                if k == 23:
                    l2_sum(0)
                if k == 24:
                    l2_norm(0)

            tables()
            with dve.register("dve_expert") as reg:
                for g in range(GH):
                    pick_wi(g)
            style()
            for g in range(GH):
                l0_sum(g)
                if g >= 1:
                    l0_norm(g - 1)
                if g >= 2:
                    l1_ln(g - 2)
            l0_norm(GH - 1)
            l1_ln(GH - 2)
            time_norm_a(0)
            l1_ln(GH - 1)
            time_norm_b(0)
            time_norm_a(1)
            time_norm_b(1)
            time_norm_c(0)
            l0_sum(GH)
            time_norm_c(1)
            split_lo(0)
            l0_norm(GH)
            top2(0)
            combine(0)
            comb_copy(0)
            l0_sum(GH + 1)
            hid_split(0)
            l0_norm(GH + 1)
            split_lo(1)
            split_lo(2)
            for n in range(1, NE):
                side(2 * n)
                hid_split(n)
                gate(n - 1)
                side(2 * n + 1)
                for e in later_splits(n):
                    split_lo(e)
            gate_last(1)
            gate_last(2)
            l2_block(1)
            l2_block(2)
            l2_sum(1)
            l2_norm(1)
            mask(0, 0, l3a_act, 4, nr_act, l3a_mask)
            l2_sum(2)
            mask(0, 2, l3b_act, 1, a_sr2, l3b_mask)
            l2_norm(2)
            l3_sum(0)
            mask(1, 0, l3a_act, 8, nr_act, l3a_mask)
            mask(1, 2, l3b_act, 2, a_sr2, l3b_mask)
            l3_norm(0)
            l3_sum(1)
            mask(2, 0, l3a_act, 12, nr_act, l3a_mask)
            mask(2, 2, l3b_act, 3, a_sr2, l3b_mask)
            l3_norm(1)
            l3_sum(2)
            l3_norm(2)

        @block.gpsimd
        def _(pool):
            G = nc.gpsimd
            seq = [0]

            def link(ins):
                seq[0] += 1
                ins.then_inc(pool_seq, 1)
                pool.wait_ge(pool_seq, seq[0])

            def inv_sqrt(src, tmp, dst, scale, eps, ready):
                link(G.tensor_scalar(tmp, src, scale, eps, ALU.mult, ALU.add))
                G.tensor_tensor(dst, tmp, half_exp[:, 0:tmp.shape[-1]], ALU.pow).then_inc(ready, 1)

            def rs_l0(g):
                i = g % 2
                pool.wait_ge(var0_ready, g + 1)
                inv_sqrt(mv0[:, i, 1:2], rs0[:, i, 0:1], rs0[:, i, 1:2], 1.0, 1e-12, rs0_ready)

            def rs_l1(g):
                i = g % 2
                pool.wait_ge(var1_ready, g + 1)
                inv_sqrt(mv1[:, i, 1:2], rs1[:, i, 0:1], rs1[:, i, 1:2], 1.0, 1e-5, rs1_ready)

            def rs_time(q):
                i = q % 2
                pool.wait_ge(tvar_ready, q + 1)
                inv_sqrt(tvar[:, i, :], trs[:, i, 0, :], trs[:, i, 1, :], 1.0 / S, 1e-8, trs_ready)

            def exp_dif(c):
                pool.wait_ge(dif_ready, c + 1)
                G.tensor_tensor(ratio[:], euler[:], dif[:], ALU.pow).then_inc(ratio_ready, 1)

            def split_w1(e):
                pool.wait_ge(w_hi, 2 * e + 1)
                G.tensor_tensor(w1_lo(e), w_raw(e, 0), w1_hi(e).bitcast(F32),
                                ALU.subtract).then_inc(w_lo_pool, 1)

            def hid_lo_half(n):
                wait_hidden_free(pool, n)
                for f in (1, 3):
                    u = NF * n + f
                    pool.wait_ge(hi_act, 2 * n + (f + 1) // 2)
                    G.tensor_tensor(hid_lo[n % 2][:, f, :], r1[:, u % NR, :],
                                    hid_hi[n % 2][:, f, :].bitcast(F32), ALU.subtract).then_inc(lo_pool, 1)

            def add_gated(n):
                c = n // E1
                pool.wait_ge(gated_ready, n + 1)
                pool.wait_ge(acc_ready, c + 1)
                if n:
                    pool.wait_ge(acc_done, n)
                G.tensor_tensor(acc[:, c, :], acc[:, c, :], gated[:, n % 2, :], ALU.add).then_inc(acc_done, 1)

            def rs_l2(u):
                pool.wait_ge(var2_ready, u + 1)
                gs = slice(UNITS[u][0], UNITS[u][0] + UNITS[u][1])
                inv_sqrt(mv2[:, gs, 1], rs2[:, 0, gs], rs2[:, 1, gs], 1.0, 1e-5, rs2_ready)

            def rs_l3(u):
                pool.wait_ge(var3_ready, u + 1)
                gs = slice(UNITS[u][0], UNITS[u][0] + UNITS[u][1])
                inv_sqrt(mv2[:, gs, 1], rs2[:, 0, gs], rs2[:, 1, gs], 1.0, 1e-5, rs3_ready)

            def mask_tsr(u):
                pool.wait_ge(l3a_act, 4 * u + 3)
                pool.wait_ge(cmask_ready, 2)
                v = tsr_act[half(u)][:, tok(u)].rearrange("p (b s) -> p b s", s=S)
                m = cmask[:, 1, seqs_of(u)].unsqueeze(2).broadcast_to([P, width(u) // S, S])
                G.tensor_tensor(v, v, m, ALU.mult).then_inc(l3a_mask_pool, 1)

            def side(k):
                if k == 5:
                    rs_l0(GH + 3)
                if k in (4, 6):
                    rs_l1(GH + k // 2)
                if k in (8, 12):
                    rs_time(2 + k // 12)
                if k == 15:
                    exp_dif(1)
                if k == 17:
                    pool.wait_ge(w_hi, 2 * E1)
                    pool.wait_ge(w_lo_dve, low_by_dve(E1 - 1))
                    G.memset(bd_h, 0.0).then_inc(bd_zero, 1)
                    G.memset(bd_w, 0.0).then_inc(bd_zero, 1)
                if k == 23:
                    rs_l2(0)

            pool.dma_start(ids_j[:], in_ids_j).then_inc(ld_idj, 16)
            G.iota(iota8[:], pattern=[[1, E1]], base=0, channel_multiplier=0).then_inc(const_pool, 1)
            pool.wait_ge(l2i_ready, 1)
            for g in range(NG):
                G.indirect_dma_start(l2g[:, g, :], None, in_l2tab,
                                     bass.IndirectOffsetOnAxis(ap=l2i[:, g:g + 1], axis=0)).then_inc(ld_l2, 16)
            pool.wait_ge(const_dve, 1)
            rs_l0(0)
            for g in range(1, GH):
                rs_l0(g)
                rs_l1(g - 1)
            rs_l1(GH - 1)
            rs_time(0)
            rs_time(1)
            split_w1(0)
            rs_l0(GH)
            rs_l1(GH)
            exp_dif(0)
            hid_lo_half(0)
            split_w1(1)
            rs_l0(GH + 1)
            rs_l1(GH + 1)
            for n in range(1, NE):
                side(2 * n)
                hid_lo_half(n)
                if n == 1:
                    rs_l0(GH + 2)
                add_gated(n - 1)
                side(2 * n + 1)
            mask_tsr(0)
            rs_l2(1)
            rs_l2(2)
            mask_tsr(1)
            rs_l3(0)
            mask_tsr(2)
            rs_l3(1)
            rs_l3(2)


def lay_out(i, np):
    f4 = np.float32
    x = np.asarray(i["x"])
    ids = [np.asarray(i[k]).astype(np.int32, copy=False) for k in ("itok_B_0_7", "itok_B_6_14", "itok_B_0_15", "itok_B_0_2")]
    cols = np.zeros((P, NCOL), f4)

    def put(c, v):
        cols[:v.shape[0], c] = v

    put(C_LNG, i["L1_cond_ln_g"])
    put(C_LNB, i["L1_cond_ln_b"])
    put(C_HB1, i["L1_cond_hyp_b1"])
    put(C_HB2, i["L1_cond_hyp_b2"])
    put(C_SB1, i["L1_cond_sty_b1"])
    put(C_SB2G, i["L1_cond_sty_b2"][:D])
    put(C_SB2B, i["L1_cond_sty_b2"][D:])
    put(C_B1NR, i["L3_cond_b1_nr"])
    put(C_B1TSR, i["L3_cond_b1_tsr"])
    put(C_B1SR0, i["L3_cond_b1_sr"][:P])
    put(C_B1SR1, i["L3_cond_b1_sr"][P:])
    put(C_B2SR, i["L3_cond_b2_sr"])
    put(C_DB, np.tile(i["L2_cond_down_b"], GRP))
    put(C_L2G, i["L2_cond_ln_gamma"])
    put(C_L2B, i["L2_cond_ln_beta"])
    put(C_P32, np.tile(np.arange(32, dtype=f4), 4))
    cols[:, C_EB1:] = i["L1_cond_exp_b1"].reshape(E1 * NF, P).T
    mats = np.zeros((P, NMAT), f4)
    parts = dict(hyp_w1=i["L1_cond_hyp_w1"], hyp_w2=i["L1_cond_hyp_w2"], sty_w1=i["L1_cond_sty_w1"],
                 sty_w2=i["L1_cond_sty_w2"], subj=i["L1_cond_subj_emb"], router=i["L1_cond_router_w"],
                 ident=np.eye(P, dtype=f4), downT=i["L2_cond_down_W"].T,
                 upT=np.tile(i["L2_cond_up_W"].T, (GRP, 1)), exp_b2=i["L1_cond_exp_b2"],
                 w1_nr=i["L3_cond_w1_nr"], w1_tsr=i["L3_cond_w1_tsr"], w1_sr=i["L3_cond_w1_sr"],
                 w2_sr0=i["L3_cond_w2_sr"][:P], w2_sr1=i["L3_cond_w2_sr"][P:], w2_nr=i["L3_cond_w2_nr"],
                 w2_tsr=i["L3_cond_w2_tsr"], w3_sr=i["L3_cond_w3_sr"])
    for name, m in parts.items():
        a, b = MATS[name]
        mats[:m.shape[0], a:b] = m
    rows = np.zeros((8, NROW), f4)
    rows[:, R_UB:R_UB + D] = i["L2_cond_up_b"]
    rows[:, R_BI:R_BI + FF] = i["L0_cond_bi"]
    rows[:, R_BO:R_BO + D] = i["L0_cond_bo"]
    rows[:, R_GAM:R_GAM + D] = i["L0_cond_gamma"]
    rows[:, R_BET:R_BET + D] = i["L0_cond_beta"]
    rows[0, R_B3:R_UB] = i["L3_cond_b2_nr"]
    rows[1, R_B3:R_UB] = i["L3_cond_b2_tsr"]
    rows[2, R_B3:R_UB] = i["L3_cond_b3_sr"]
    bc = np.stack([i["L3_cond_gamma"], i["L3_cond_beta"]])
    tab = np.zeros((NBLK, A2, A2 + 2), f4)
    tab[1:17, :, :A2] = i["L2_cond_expert_W"].transpose(0, 2, 1)
    tab[1:17, :, A2] = i["L2_cond_expert_b"]
    tab[1:17, :, A2 + 1] = i["L2_cond_domain_emb"]
    for blk, e in ((0, 0), (17, 15)):
        tab[blk, :, :A2] = np.eye(A2, dtype=f4)
        tab[blk, :, A2 + 1] = i["L2_cond_domain_emb"][e]

    def w_in(w):
        return w.transpose(1, 0, 2)

    def w_out(w):
        return w.reshape(w.shape[0], NF, P, D).transpose(2, 0, 1, 3).reshape(P, w.shape[0], NF * D)

    return {
        "x_t": x.reshape(NTOK, D).T,
        "ids_row": ids[0].reshape(1, B),
        "ids_all": np.broadcast_to(np.stack(ids)[None], (P, 4, B)),
        "ids_j": np.repeat(ids[2].reshape(NG, GRP).T, A2, axis=0),
        "cols": cols,
        "mats": mats,
        "rows": rows.reshape(P, RW),
        "bcast": np.broadcast_to(bc[None], (P, 2, D)),
        "l2tab": tab.reshape(NBLK * A2, A2 + 2),
        "wi": w_in(i["L0_cond_Wi"]),
        "wo": w_out(i["L0_cond_Wo"]),
        "w1": np.concatenate([w_in(i["L1_cond_exp_w1"]), w_out(i["L1_cond_exp_w2"])], axis=2),
    }


def kernel(**inputs):
    import numpy as np
    import concourse.bacc as bacc
    from concourse.bass_utils import run_bass_kernel_spmd

    laid = lay_out({k: np.asarray(v) for k, v in inputs.items()}, np)
    nc = bacc.Bacc("TRN2", target_bir_lowering=False, num_devices=1)
    arrays, aps = {}, {}
    for name, a in laid.items():
        a = np.ascontiguousarray(a)
        arrays[f"in_{name}_dram"] = a
        aps[f"in_{name}"] = nc.dram_tensor(f"in_{name}_dram", a.shape, mybir.dt.from_np(a.dtype),
                                           kind="ExternalInput").ap()
    out = nc.dram_tensor("out_dram", (P, NG, D), F32, kind="ExternalOutput").ap()
    build_program(nc, out=out, **aps)
    r = run_bass_kernel_spmd(nc, [arrays], core_ids=[0])
    got = r.results[0]["out_dram"]
    return got.transpose(1, 0, 2).reshape(B, S, D)
```
